# Optimizing a Trainium2 kernel written in Bass

```python
import numpy as np
import jax
import jax.numpy as jnp

def _softmax(x, axis=-1):
    return jax.nn.softmax(x, axis=axis)

def _gelu(x):
    return jax.nn.gelu(x, approximate=True)

def _silu(x):
    return jax.nn.silu(x)

def _sigmoid(x):
    return jax.nn.sigmoid(x)

def _layernorm(x, axis=-1, eps=1e-05):
    m = jnp.mean(x, axis=axis, keepdims=True)
    v = jnp.var(x, axis=axis, keepdims=True)
    return (x - m) / jnp.sqrt(v + eps)

def _scatter_add(tgt, idx, src, axis=0):
    return tgt.at[idx].add(src)

def _segment_sum(src, seg, n):
    return jax.ops.segment_sum(src, seg, n)
kernel_name = 'mk_decoder_preln_d2_seqx_r4_7cd703'

def setup_inputs(seed: int=0):
    np.random.seed(seed)
    _w = jnp.asarray

    def _rec_inputs():
        import jax
        import jax.numpy as jnp
        _rk = jax.random.key(seed)
        x = -0.0002928 + 1 * jax.random.normal(jax.random.fold_in(_rk, 1), (16, 100, 256), jnp.float32)
        _lenS = 100 - jax.random.randint(jax.random.fold_in(_rk, 7), (16,), 0, max(1, 100 // 4) + 1, jnp.int32)
        _lenS2 = 361 - jax.random.randint(jax.random.fold_in(_rk, 8), (16,), 0, max(1, 361 // 4) + 1, jnp.int32)
        _ctx_1024P = jax.random.normal(jax.random.fold_in(_rk, 11), (16, 16, 256), jnp.float32)
        _ctx_1024c = jax.random.dirichlet(jax.random.fold_in(_rk, 511), 0.3 * jnp.ones((16,), jnp.float32), (16, 361))
        _ctx_1024t = jnp.einsum('bsk,bkd->bsd', _ctx_1024c, _ctx_1024P)
        _ctx_1024t = _ctx_1024t * jax.lax.rsqrt(jnp.mean(jnp.square(_ctx_1024t)) + 1e-12) * 0.953939
        ctx_1024 = -1.39393e-06 + 0.999914 * (_ctx_1024t + 0.3 * jax.random.normal(jax.random.fold_in(_rk, 611), (16, 361, 256), jnp.float32))
        _validS = jnp.arange(100)[None, :] < _lenS[:, None]
        _validS2 = jnp.arange(361)[None, :] < _lenS2[:, None]
        _causal = jnp.tril(jnp.ones((100, 100), dtype=bool))
        mask_BxSxS2_bk1 = jnp.broadcast_to(_validS2[:, None, :], (16, 100, 361))
        return (x, ctx_1024, mask_BxSxS2_bk1)
    x, ctx_1024, mask_BxSxS2_bk1 = _rec_inputs()

    def _L0_attn_setup():
        import jax, jax.numpy as jnp
        import numpy as np
        import math
        B, T, D = (4, 1024, 256)
        K, H, KH, C = (64, 4, 16, 64)
        MLP = 1024
        EPS = 1e-05

        def _layernorm(x, g, b):
            m = jnp.mean(x, axis=-1, keepdims=True)
            v = jnp.mean((x - m) ** 2, axis=-1, keepdims=True)
            return (x - m) / jnp.sqrt(v + EPS) * g + b

        def _chunked_eigenstate(log_decay, frequency, beta_r, beta_i):
            Bt, Tt, Kt = beta_r.shape
            T_pad = (Tt + C - 1) // C * C
            if T_pad > Tt:
                beta_r = jnp.pad(beta_r, ((0, 0), (0, T_pad - Tt), (0, 0)))
                beta_i = jnp.pad(beta_i, ((0, 0), (0, T_pad - Tt), (0, 0)))
            n_chunks = T_pad // C
            mag = jax.nn.sigmoid(log_decay)
            powers = jnp.arange(C, dtype=log_decay.dtype)
            mag_pow = mag[:, None] ** powers[None, :]
            phases = frequency[:, None] * powers[None, :]
            kr = mag_pow * jnp.cos(phases)
            ki = mag_pow * jnp.sin(phases)
            ii = jnp.arange(C)
            idx = ii[None, :] - ii[:, None]
            mask = (idx >= 0).astype(kr.dtype)
            idxc = jnp.clip(idx, 0, C - 1)
            L_r = kr[:, idxc] * mask[None]
            L_i = ki[:, idxc] * mask[None]
            br = beta_r.reshape(Bt, n_chunks, C, Kt)
            bi = beta_i.reshape(Bt, n_chunks, C, Kt)
            intra_r = jnp.einsum('kjs,bnsk->bnjk', L_r, br) - jnp.einsum('kjs,bnsk->bnjk', L_i, bi)
            intra_i = jnp.einsum('kjs,bnsk->bnjk', L_r, bi) + jnp.einsum('kjs,bnsk->bnjk', L_i, br)
            first_col_r = L_r[:, :, 0]
            first_col_i = L_i[:, :, 0]

            def step(carry, intra):
                sr, si = carry
                ir, im = intra
                cr = first_col_r[None] * sr[:, :, None] - first_col_i[None] * si[:, :, None]
                ci = first_col_r[None] * si[:, :, None] + first_col_i[None] * sr[:, :, None]
                o_r = ir + jnp.transpose(cr, (0, 2, 1))
                o_i = im + jnp.transpose(ci, (0, 2, 1))
                return ((o_r[:, -1, :], o_i[:, -1, :]), (o_r, o_i))
            xs = (jnp.transpose(intra_r, (1, 0, 2, 3)), jnp.transpose(intra_i, (1, 0, 2, 3)))
            init = (jnp.zeros((Bt, Kt), beta_r.dtype), jnp.zeros((Bt, Kt), beta_r.dtype))
            _, (out_r, out_i) = jax.lax.scan(step, init, xs)
            c_r = jnp.transpose(out_r, (1, 0, 2, 3)).reshape(Bt, T_pad, Kt)[:, :Tt]
            c_i = jnp.transpose(out_i, (1, 0, 2, 3)).reshape(Bt, T_pad, Kt)[:, :Tt]
            return (c_r, c_i)
        key = jax.random.key(seed)
        ks = jax.random.split(key, 8)

        def n(k, shape, scale):
            return jax.random.normal(k, shape, dtype=jnp.float32) * scale
        return {'x': jax.random.normal(ks[0], (B, T, D), dtype=jnp.float32), 'w_in': n(ks[1], (2 * K, D), D ** (-0.5)), 'w_out': n(ks[2], (D, 2 * K), (2 * K) ** (-0.5)), 'w_gate': n(ks[3], (D, D), D ** (-0.5)), 'b_gate': jnp.full((D,), -2.0, dtype=jnp.float32), 'log_decay': jax.random.uniform(ks[4], (K,), minval=-3.0, maxval=-0.1, dtype=jnp.float32), 'frequency': jnp.linspace(0.0, 2.0 * math.pi * (1.0 - 1.0 / K), K, dtype=jnp.float32), 'coupling': jnp.eye(KH, dtype=jnp.float32)[None] + 0.01 * jax.random.normal(ks[5], (H, KH, KH), dtype=jnp.float32) / math.sqrt(KH), 'w_mlp1': n(ks[6], (MLP, D), D ** (-0.5)), 'b_mlp1': jnp.zeros((MLP,), jnp.float32), 'w_mlp2': n(ks[7], (D, MLP), MLP ** (-0.5)), 'b_mlp2': jnp.zeros((D,), jnp.float32), 'ln1_g': jnp.ones((D,), jnp.float32), 'ln1_b': jnp.zeros((D,), jnp.float32), 'ln2_g': jnp.ones((D,), jnp.float32), 'ln2_b': jnp.zeros((D,), jnp.float32)}
    _L0_attn_all = _L0_attn_setup()
    _L0_attn_in = {k: v for k, v in _L0_attn_all.items() if k in ('w_in', 'w_out', 'w_gate', 'b_gate', 'log_decay', 'frequency', 'coupling', 'w_mlp1', 'b_mlp1', 'w_mlp2', 'b_mlp2', 'ln1_g', 'ln1_b', 'ln2_g', 'ln2_b')}
    del _L0_attn_all

    def _L0_xattn_setup():
        import jax, jax.numpy as jnp
        import numpy as np
        NUM_HEADS = 16
        DIM_MODEL = 256
        DIM_HEAD = DIM_MODEL // NUM_HEADS

        def _split_heads(x, B):
            return x.reshape(B, -1, NUM_HEADS, DIM_HEAD).transpose(0, 2, 1, 3)
        key = jax.random.key(seed)
        ks = jax.random.split(key, 13)
        B, S, D = (2, 512, DIM_MODEL)
        scale = 1.0 / np.sqrt(D)
        inp = {'query': jax.random.normal(ks[0], (B, S, D), jnp.float32), 'key': jax.random.normal(ks[1], (B, S, D), jnp.float32), 'value': jax.random.normal(ks[2], (B, S, D), jnp.float32), 'Wq': jax.random.normal(ks[3], (D, D), jnp.float32) * scale, 'bq': jax.random.normal(ks[4], (D,), jnp.float32) * scale, 'Wk': jax.random.normal(ks[5], (D, D), jnp.float32) * scale, 'bk': jax.random.normal(ks[6], (D,), jnp.float32) * scale, 'Wv': jax.random.normal(ks[7], (D, D), jnp.float32) * scale, 'bv': jax.random.normal(ks[8], (D,), jnp.float32) * scale, 'Wo': jax.random.normal(ks[9], (D, D), jnp.float32) * scale, 'bo': jax.random.normal(ks[10], (D,), jnp.float32) * scale}
        return inp
    _L0_xattn_all = _L0_xattn_setup()
    _L0_xattn_in = {k: v for k, v in _L0_xattn_all.items() if k in ('Wq', 'bq', 'Wk', 'bk', 'Wv', 'bv', 'Wo', 'bo')}
    del _L0_xattn_all

    def _L0_ffn_setup():
        import jax, jax.numpy as jnp
        import numpy as np
        B, S, D = (2, 512, 256)
        E, G, K = (32, 8, 4)
        H, SH = (512, 512)
        CAP_FACTOR = 1.25

        def _l2norm(v):
            n = jnp.linalg.norm(v, axis=-1, keepdims=True)
            return v / jnp.maximum(n, 1e-12)
        key = jax.random.key(seed)
        ks = jax.random.split(key, 10)
        x = jax.random.normal(ks[0], (B, S, D), jnp.float32)
        group_centroids = jax.random.normal(ks[1], (G, D), jnp.float32) * 0.02
        expert_centroids = jax.random.normal(ks[2], (E, D), jnp.float32) * 0.02
        bias = jnp.zeros((E,), jnp.float32)
        sd_in = 1.0 / np.sqrt(D).astype(np.float32)
        sd_h = 1.0 / np.sqrt(H).astype(np.float32)
        wg = jax.random.normal(ks[3], (E, D, H), jnp.float32) * sd_in
        wu = jax.random.normal(ks[4], (E, D, H), jnp.float32) * sd_in
        wd = jax.random.normal(ks[5], (E, H, D), jnp.float32) * sd_h
        sg = jax.random.normal(ks[6], (D, SH), jnp.float32) * sd_in
        su = jax.random.normal(ks[7], (D, SH), jnp.float32) * sd_in
        sd_w = jax.random.normal(ks[8], (SH, D), jnp.float32) * sd_h
        return dict(x=x, group_centroids=group_centroids, expert_centroids=expert_centroids, bias=bias, wg=wg, wu=wu, wd=wd, sg=sg, su=su, sd=sd_w)
    _L0_ffn_all = _L0_ffn_setup()
    _L0_ffn_in = {k: v for k, v in _L0_ffn_all.items() if k in ('group_centroids', 'expert_centroids', 'bias', 'wg', 'wu', 'wd', 'sg', 'su', 'sd')}
    del _L0_ffn_all

    def _L1_attn_setup():
        import jax, jax.numpy as jnp
        import numpy as np
        H = 16
        GRID = 16
        TOK_PER_FRAME = GRID * GRID

        def _rope(x, pos, dim):
            half = dim // 2
            omega = jnp.arange(half, dtype=x.dtype) / (dim / 2.0)
            inv = 1.0 / 10000.0 ** omega
            freq = pos.astype(x.dtype)[:, None] * inv
            sin = jnp.concatenate([jnp.sin(freq), jnp.sin(freq)], axis=-1)
            cos = jnp.concatenate([jnp.cos(freq), jnp.cos(freq)], axis=-1)
            y = x.reshape(*x.shape[:-1], half, 2)
            y1, y2 = (y[..., 0], y[..., 1])
            rot = jnp.stack((-y2, y1), axis=-1).reshape(x.shape)
            return x * cos + rot * sin

        def _apply_3d_rope(qk, f_ids, h_ids, w_ids, d_dim):
            s = 0
            parts = []
            for pos in (f_ids, h_ids, w_ids):
                parts.append(_rope(qk[..., s:s + d_dim], pos, d_dim))
                s += d_dim
            if s < qk.shape[-1]:
                parts.append(qk[..., s:])
            return jnp.concatenate(parts, axis=-1)
        key = jax.random.key(seed)
        ks = jax.random.split(key, 5)
        D = 256
        B, N = (4, 512)
        sc = 0.02
        return {'hidden_states': jax.random.normal(ks[0], (B, N, D), jnp.float32), 'Wq': jax.random.normal(ks[1], (D, D), jnp.float32) * sc, 'bq': jnp.zeros((D,), jnp.float32), 'Wk': jax.random.normal(ks[2], (D, D), jnp.float32) * sc, 'bk': jnp.zeros((D,), jnp.float32), 'Wv': jax.random.normal(ks[3], (D, D), jnp.float32) * sc, 'bv': jnp.zeros((D,), jnp.float32), 'Wo': jax.random.normal(ks[4], (D, D), jnp.float32) * sc, 'bo': jnp.zeros((D,), jnp.float32)}
    _L1_attn_all = _L1_attn_setup()
    _L1_attn_in = {k: v for k, v in _L1_attn_all.items() if k in ('Wq', 'bq', 'Wk', 'bk', 'Wv', 'bv', 'Wo', 'bo')}
    del _L1_attn_all

    def _L1_xattn_setup():
        import jax, jax.numpy as jnp
        import numpy as np
        B, TQ, TK, D, H = (2, 512, 512, 256, 16)
        key = jax.random.key(seed)
        ks = jax.random.split(key, 8)
        s = 1.0 / np.sqrt(D)
        x_q = jax.random.normal(ks[0], (B, TQ, D), jnp.float32)
        x_k = jax.random.normal(ks[1], (B, TK, D), jnp.float32)
        x_v = jax.random.normal(ks[2], (B, TK, D), jnp.float32)
        causal = jnp.triu(jnp.ones((TQ, TK), jnp.bool_), k=1)
        attn_mask = jnp.broadcast_to(causal, (B, TQ, TK))
        Wq = jax.random.normal(ks[3], (D, D), jnp.float32) * s
        Wk = jax.random.normal(ks[4], (D, D), jnp.float32) * s
        Wv = jax.random.normal(ks[5], (D, D), jnp.float32) * s
        Wo = jax.random.normal(ks[6], (D, D), jnp.float32) * s
        z = jnp.zeros((D,), jnp.float32)
        return {'x_q': x_q, 'x_k': x_k, 'x_v': x_v, 'attn_mask': attn_mask, 'Wq': Wq, 'bq': z, 'Wk': Wk, 'bk': z, 'Wv': Wv, 'bv': z, 'Wo': Wo, 'bo': z, 'n_heads': H}
    _L1_xattn_all = _L1_xattn_setup()
    _L1_xattn_in = {k: v for k, v in _L1_xattn_all.items() if k in ('Wq', 'bq', 'Wk', 'bk', 'Wv', 'bv', 'Wo', 'bo')}
    del _L1_xattn_all

    def _L1_ffn_setup():
        import jax, jax.numpy as jnp
        import numpy as np
        D_MODEL = 256
        D_FF = 1024
        NUM_EXPERTS = 8
        key = jax.random.key(seed)
        ks = jax.random.split(key, 8)
        scale_in = 1.0 / np.sqrt(D_MODEL)
        scale_ff = 1.0 / np.sqrt(D_FF)
        x = jax.random.normal(ks[0], (4, 512, D_MODEL), dtype=jnp.float32)
        gate_w = jax.random.uniform(ks[1], (NUM_EXPERTS, D_MODEL), jnp.float32, -scale_in, scale_in)
        gate_b = jax.random.uniform(ks[2], (NUM_EXPERTS,), jnp.float32, -scale_in, scale_in)
        expert_bias = jnp.zeros((NUM_EXPERTS,), dtype=jnp.float32)
        w1 = jax.random.uniform(ks[3], (NUM_EXPERTS, D_MODEL, D_FF), jnp.float32, -scale_in, scale_in)
        b1 = jax.random.uniform(ks[4], (NUM_EXPERTS, D_FF), jnp.float32, -scale_in, scale_in)
        w2 = jax.random.uniform(ks[5], (NUM_EXPERTS, D_FF, D_MODEL), jnp.float32, -scale_ff, scale_ff)
        b2 = jax.random.uniform(ks[6], (NUM_EXPERTS, D_MODEL), jnp.float32, -scale_ff, scale_ff)
        return {'x': x, 'gate_w': gate_w, 'gate_b': gate_b, 'expert_bias': expert_bias, 'w1': w1, 'b1': b1, 'w2': w2, 'b2': b2}
    _L1_ffn_all = _L1_ffn_setup()
    _L1_ffn_in = {k: v for k, v in _L1_ffn_all.items() if k in ('gate_w', 'gate_b', 'expert_bias', 'w1', 'b1', 'w2', 'b2')}
    del _L1_ffn_all
    return {'x': x, 'ctx_1024': ctx_1024, 'mask_BxSxS2_bk1': mask_BxSxS2_bk1, 'L0_attn_w_in': _L0_attn_in['w_in'], 'L0_attn_w_out': _L0_attn_in['w_out'], 'L0_attn_w_gate': _L0_attn_in['w_gate'], 'L0_attn_b_gate': _L0_attn_in['b_gate'], 'L0_attn_log_decay': _L0_attn_in['log_decay'], 'L0_attn_frequency': _L0_attn_in['frequency'], 'L0_attn_coupling': _L0_attn_in['coupling'], 'L0_attn_w_mlp1': _L0_attn_in['w_mlp1'], 'L0_attn_b_mlp1': _L0_attn_in['b_mlp1'], 'L0_attn_w_mlp2': _L0_attn_in['w_mlp2'], 'L0_attn_b_mlp2': _L0_attn_in['b_mlp2'], 'L0_attn_ln1_g': _L0_attn_in['ln1_g'], 'L0_attn_ln1_b': _L0_attn_in['ln1_b'], 'L0_attn_ln2_g': _L0_attn_in['ln2_g'], 'L0_attn_ln2_b': _L0_attn_in['ln2_b'], 'L0_xattn_Wq': _L0_xattn_in['Wq'], 'L0_xattn_bq': _L0_xattn_in['bq'], 'L0_xattn_Wk': _L0_xattn_in['Wk'], 'L0_xattn_bk': _L0_xattn_in['bk'], 'L0_xattn_Wv': _L0_xattn_in['Wv'], 'L0_xattn_bv': _L0_xattn_in['bv'], 'L0_xattn_Wo': _L0_xattn_in['Wo'], 'L0_xattn_bo': _L0_xattn_in['bo'], 'L0_ffn_group_centroids': _L0_ffn_in['group_centroids'], 'L0_ffn_expert_centroids': _L0_ffn_in['expert_centroids'], 'L0_ffn_bias': _L0_ffn_in['bias'], 'L0_ffn_wg': _L0_ffn_in['wg'], 'L0_ffn_wu': _L0_ffn_in['wu'], 'L0_ffn_wd': _L0_ffn_in['wd'], 'L0_ffn_sg': _L0_ffn_in['sg'], 'L0_ffn_su': _L0_ffn_in['su'], 'L0_ffn_sd': _L0_ffn_in['sd'], 'L1_attn_Wq': _L1_attn_in['Wq'], 'L1_attn_bq': _L1_attn_in['bq'], 'L1_attn_Wk': _L1_attn_in['Wk'], 'L1_attn_bk': _L1_attn_in['bk'], 'L1_attn_Wv': _L1_attn_in['Wv'], 'L1_attn_bv': _L1_attn_in['bv'], 'L1_attn_Wo': _L1_attn_in['Wo'], 'L1_attn_bo': _L1_attn_in['bo'], 'L1_xattn_Wq': _L1_xattn_in['Wq'], 'L1_xattn_bq': _L1_xattn_in['bq'], 'L1_xattn_Wk': _L1_xattn_in['Wk'], 'L1_xattn_bk': _L1_xattn_in['bk'], 'L1_xattn_Wv': _L1_xattn_in['Wv'], 'L1_xattn_bv': _L1_xattn_in['bv'], 'L1_xattn_Wo': _L1_xattn_in['Wo'], 'L1_xattn_bo': _L1_xattn_in['bo'], 'L1_ffn_gate_w': _L1_ffn_in['gate_w'], 'L1_ffn_gate_b': _L1_ffn_in['gate_b'], 'L1_ffn_expert_bias': _L1_ffn_in['expert_bias'], 'L1_ffn_w1': _L1_ffn_in['w1'], 'L1_ffn_b1': _L1_ffn_in['b1'], 'L1_ffn_w2': _L1_ffn_in['w2'], 'L1_ffn_b2': _L1_ffn_in['b2']}

def reference(x, ctx_1024, mask_BxSxS2_bk1, L0_attn_w_in, L0_attn_w_out, L0_attn_w_gate, L0_attn_b_gate, L0_attn_log_decay, L0_attn_frequency, L0_attn_coupling, L0_attn_w_mlp1, L0_attn_b_mlp1, L0_attn_w_mlp2, L0_attn_b_mlp2, L0_attn_ln1_g, L0_attn_ln1_b, L0_attn_ln2_g, L0_attn_ln2_b, L0_xattn_Wq, L0_xattn_bq, L0_xattn_Wk, L0_xattn_bk, L0_xattn_Wv, L0_xattn_bv, L0_xattn_Wo, L0_xattn_bo, L0_ffn_group_centroids, L0_ffn_expert_centroids, L0_ffn_bias, L0_ffn_wg, L0_ffn_wu, L0_ffn_wd, L0_ffn_sg, L0_ffn_su, L0_ffn_sd, L1_attn_Wq, L1_attn_bq, L1_attn_Wk, L1_attn_bk, L1_attn_Wv, L1_attn_bv, L1_attn_Wo, L1_attn_bo, L1_xattn_Wq, L1_xattn_bq, L1_xattn_Wk, L1_xattn_bk, L1_xattn_Wv, L1_xattn_bv, L1_xattn_Wo, L1_xattn_bo, L1_ffn_gate_w, L1_ffn_gate_b, L1_ffn_expert_bias, L1_ffn_w1, L1_ffn_b1, L1_ffn_w2, L1_ffn_b2):
    import jax
    import jax.numpy as jnp

    def _L0_attn_ref(x, w_in, w_out, w_gate, b_gate, log_decay, frequency, coupling, w_mlp1, b_mlp1, w_mlp2, b_mlp2, ln1_g, ln1_b, ln2_g, ln2_b):
        import jax, jax.numpy as jnp
        import numpy as np
        import math
        B, T, D = (4, 1024, 256)
        K, H, KH, C = (64, 4, 16, 64)
        MLP = 1024
        EPS = 1e-05

        def _layernorm(x, g, b):
            m = jnp.mean(x, axis=-1, keepdims=True)
            v = jnp.mean((x - m) ** 2, axis=-1, keepdims=True)
            return (x - m) / jnp.sqrt(v + EPS) * g + b

        def _chunked_eigenstate(log_decay, frequency, beta_r, beta_i):
            Bt, Tt, Kt = beta_r.shape
            T_pad = (Tt + C - 1) // C * C
            if T_pad > Tt:
                beta_r = jnp.pad(beta_r, ((0, 0), (0, T_pad - Tt), (0, 0)))
                beta_i = jnp.pad(beta_i, ((0, 0), (0, T_pad - Tt), (0, 0)))
            n_chunks = T_pad // C
            mag = jax.nn.sigmoid(log_decay)
            powers = jnp.arange(C, dtype=log_decay.dtype)
            mag_pow = mag[:, None] ** powers[None, :]
            phases = frequency[:, None] * powers[None, :]
            kr = mag_pow * jnp.cos(phases)
            ki = mag_pow * jnp.sin(phases)
            ii = jnp.arange(C)
            idx = ii[None, :] - ii[:, None]
            mask = (idx >= 0).astype(kr.dtype)
            idxc = jnp.clip(idx, 0, C - 1)
            L_r = kr[:, idxc] * mask[None]
            L_i = ki[:, idxc] * mask[None]
            br = beta_r.reshape(Bt, n_chunks, C, Kt)
            bi = beta_i.reshape(Bt, n_chunks, C, Kt)
            intra_r = jnp.einsum('kjs,bnsk->bnjk', L_r, br) - jnp.einsum('kjs,bnsk->bnjk', L_i, bi)
            intra_i = jnp.einsum('kjs,bnsk->bnjk', L_r, bi) + jnp.einsum('kjs,bnsk->bnjk', L_i, br)
            first_col_r = L_r[:, :, 0]
            first_col_i = L_i[:, :, 0]

            def step(carry, intra):
                sr, si = carry
                ir, im = intra
                cr = first_col_r[None] * sr[:, :, None] - first_col_i[None] * si[:, :, None]
                ci = first_col_r[None] * si[:, :, None] + first_col_i[None] * sr[:, :, None]
                o_r = ir + jnp.transpose(cr, (0, 2, 1))
                o_i = im + jnp.transpose(ci, (0, 2, 1))
                return ((o_r[:, -1, :], o_i[:, -1, :]), (o_r, o_i))
            xs = (jnp.transpose(intra_r, (1, 0, 2, 3)), jnp.transpose(intra_i, (1, 0, 2, 3)))
            init = (jnp.zeros((Bt, Kt), beta_r.dtype), jnp.zeros((Bt, Kt), beta_r.dtype))
            _, (out_r, out_i) = jax.lax.scan(step, init, xs)
            c_r = jnp.transpose(out_r, (1, 0, 2, 3)).reshape(Bt, T_pad, Kt)[:, :Tt]
            c_i = jnp.transpose(out_i, (1, 0, 2, 3)).reshape(Bt, T_pad, Kt)[:, :Tt]
            return (c_r, c_i)
        residual = x
        x_norm = _layernorm(x, ln1_g, ln1_b)
        beta = x_norm @ w_in.T
        beta_r, beta_i = jnp.split(beta, 2, axis=-1)
        c_r, c_i = _chunked_eigenstate(log_decay, frequency, beta_r, beta_i)
        c_rh = c_r.reshape(x.shape[0], x.shape[1], H, KH)
        c_ih = c_i.reshape(x.shape[0], x.shape[1], H, KH)
        c_r = jnp.einsum('hjk,bthk->bthj', coupling, c_rh).reshape(x.shape[0], x.shape[1], K)
        c_i = jnp.einsum('hjk,bthk->bthj', coupling, c_ih).reshape(x.shape[0], x.shape[1], K)
        h = jnp.concatenate([c_r, c_i], axis=-1) @ w_out.T
        gate = jax.nn.sigmoid(x_norm @ w_gate.T + b_gate)
        x1 = residual + gate * h
        x2n = _layernorm(x1, ln2_g, ln2_b)
        mlp = jax.nn.silu(x2n @ w_mlp1.T + b_mlp1) @ w_mlp2.T + b_mlp2
        return x1 + mlp

    def _L0_xattn_ref(query, key, value, Wq, bq, Wk, bk, Wv, bv, Wo, bo):
        import jax, jax.numpy as jnp
        import numpy as np
        NUM_HEADS = 16
        DIM_MODEL = 256
        DIM_HEAD = DIM_MODEL // NUM_HEADS

        def _split_heads(x, B):
            return x.reshape(B, -1, NUM_HEADS, DIM_HEAD).transpose(0, 2, 1, 3)
        B = query.shape[0]
        q = _split_heads(query @ Wq.T + bq, B)
        k = _split_heads(key @ Wk.T + bk, B)
        v = _split_heads(value @ Wv.T + bv, B)
        inv_sqrt_d = 1.0 / jnp.sqrt(jnp.asarray(DIM_HEAD, q.dtype))
        scores = jnp.einsum('bhqd,bhkd->bhqk', q, k) * inv_sqrt_d
        weights = jax.nn.softmax(scores, axis=-1)
        out = jnp.einsum('bhqk,bhkd->bhqd', weights, v)
        out = out.transpose(0, 2, 1, 3).reshape(B, -1, NUM_HEADS * DIM_HEAD)
        return out @ Wo.T + bo

    def _L0_ffn_ref(x, group_centroids, expert_centroids, bias, wg, wu, wd, sg, su, sd):
        import jax, jax.numpy as jnp
        import numpy as np
        B, S, D = (2, 512, 256)
        E, G, K = (32, 8, 4)
        H, SH = (512, 512)
        CAP_FACTOR = 1.25

        def _l2norm(v):
            n = jnp.linalg.norm(v, axis=-1, keepdims=True)
            return v / jnp.maximum(n, 1e-12)
        b, s, d = x.shape
        xf = x.reshape(-1, d)
        N = xf.shape[0]
        shared = jax.nn.silu(xf @ sg) * (xf @ su) @ sd
        xn = _l2norm(xf)
        group_scores = xn @ _l2norm(group_centroids).T
        n_top_groups = max(1, G // 2)
        _, top_group_idx = jax.lax.top_k(group_scores, n_top_groups)
        expert_scores = xn @ _l2norm(expert_centroids).T + bias
        expert_to_group = jnp.arange(E) // (E // G)
        sel = jnp.zeros((N, G), xf.dtype).at[jnp.arange(N)[:, None], top_group_idx].set(1.0)
        group_mask = sel[:, expert_to_group]
        masked = expert_scores * group_mask + (1.0 - group_mask) * -1000000000.0
        top_scores, top_idx = jax.lax.top_k(masked, K)
        gates = jax.nn.softmax(top_scores, axis=-1)
        capacity = max(1, int(N / E * K * CAP_FACTOR))
        flat_e = top_idx.reshape(-1)
        flat_g = gates.reshape(-1)
        tok = jnp.repeat(jnp.arange(N), K)
        onehot = jax.nn.one_hot(flat_e, E, dtype=jnp.int32)
        pos = jnp.cumsum(onehot, axis=0)[jnp.arange(N * K), flat_e] - 1
        keep = pos < capacity
        e_s = jnp.where(keep, flat_e, E)
        p_s = jnp.where(keep, pos, 0)
        buf = jnp.zeros((E + 1, capacity, d), xf.dtype).at[e_s, p_s].set(xf[tok])[:E]
        h = jax.nn.silu(jnp.einsum('ecd,edh->ech', buf, wg)) * jnp.einsum('ecd,edh->ech', buf, wu)
        out_e = jnp.einsum('ech,ehd->ecd', h, wd)
        gathered = out_e[flat_e, jnp.minimum(pos, capacity - 1)]
        contrib = gathered * (flat_g * keep.astype(xf.dtype))[:, None]
        routed = jnp.zeros_like(xf).at[tok].add(contrib)
        return (shared + routed).reshape(b, s, d)

    def _L1_attn_ref(hidden_states, Wq, bq, Wk, bk, Wv, bv, Wo, bo):
        import jax, jax.numpy as jnp
        import numpy as np
        H = 16
        GRID = 16
        TOK_PER_FRAME = GRID * GRID

        def _rope(x, pos, dim):
            half = dim // 2
            omega = jnp.arange(half, dtype=x.dtype) / (dim / 2.0)
            inv = 1.0 / 10000.0 ** omega
            freq = pos.astype(x.dtype)[:, None] * inv
            sin = jnp.concatenate([jnp.sin(freq), jnp.sin(freq)], axis=-1)
            cos = jnp.concatenate([jnp.cos(freq), jnp.cos(freq)], axis=-1)
            y = x.reshape(*x.shape[:-1], half, 2)
            y1, y2 = (y[..., 0], y[..., 1])
            rot = jnp.stack((-y2, y1), axis=-1).reshape(x.shape)
            return x * cos + rot * sin

        def _apply_3d_rope(qk, f_ids, h_ids, w_ids, d_dim):
            s = 0
            parts = []
            for pos in (f_ids, h_ids, w_ids):
                parts.append(_rope(qk[..., s:s + d_dim], pos, d_dim))
                s += d_dim
            if s < qk.shape[-1]:
                parts.append(qk[..., s:])
            return jnp.concatenate(parts, axis=-1)
        B, N, D = hidden_states.shape
        hd = D // H
        d_dim = 2 * (hd // 3 // 2)

        def heads(x):
            return x.reshape(B, N, H, hd).transpose(0, 2, 1, 3)
        q = heads(hidden_states @ Wq + bq)
        k = heads(hidden_states @ Wk + bk)
        v = heads(hidden_states @ Wv + bv)
        ids = jnp.arange(N)
        f_ids = ids // TOK_PER_FRAME
        rem = ids - TOK_PER_FRAME * f_ids
        h_ids = rem // GRID
        w_ids = rem - GRID * h_ids
        q = _apply_3d_rope(q, f_ids, h_ids, w_ids, d_dim)
        k = _apply_3d_rope(k, f_ids, h_ids, w_ids, d_dim)
        scale = hd ** (-0.5)
        attn = jnp.einsum('bhqd,bhkd->bhqk', q, k) * scale
        attn = jax.nn.softmax(attn.astype(jnp.float32), axis=-1).astype(q.dtype)
        ctx = jnp.einsum('bhqk,bhkd->bhqd', attn, v)
        ctx = ctx.transpose(0, 2, 1, 3).reshape(B, N, D)
        return ctx @ Wo + bo

    def _L1_xattn_ref(x_q, x_k, x_v, attn_mask, Wq, bq, Wk, bk, Wv, bv, Wo, bo, n_heads):
        import jax, jax.numpy as jnp
        import numpy as np
        B, TQ, TK, D, H = (2, 512, 512, 256, 16)
        Bv, Tq, Dm = x_q.shape
        Tk = x_k.shape[1]
        dh = Dm // n_heads
        Q = (jnp.einsum('btd,od->bto', x_q, Wq) + bq).reshape(Bv, Tq, n_heads, dh).transpose(0, 2, 1, 3)
        K = (jnp.einsum('btd,od->bto', x_k, Wk) + bk).reshape(Bv, Tk, n_heads, dh).transpose(0, 2, 1, 3)
        V = (jnp.einsum('btd,od->bto', x_v, Wv) + bv).reshape(Bv, Tk, n_heads, dh).transpose(0, 2, 1, 3)
        scale = 1.0 / np.sqrt(dh).astype(np.float32)
        scores = jnp.einsum('bhqd,bhkd->bhqk', Q, K) * scale
        scores = jnp.where(attn_mask[:, None, :, :], -jnp.inf, scores)
        A = jax.nn.softmax(scores, axis=-1)
        out = jnp.einsum('bhqk,bhkd->bhqd', A, V)
        out = out.transpose(0, 2, 1, 3).reshape(Bv, Tq, Dm)
        return jnp.einsum('btd,od->bto', out, Wo) + bo

    def _L1_ffn_ref(x, gate_w, gate_b, expert_bias, w1, b1, w2, b2):
        import jax, jax.numpy as jnp
        import numpy as np
        D_MODEL = 256
        D_FF = 1024
        NUM_EXPERTS = 8
        gate_logits = jnp.einsum('bsd,ed->bse', x, gate_w) + gate_b + expert_bias
        top_idx = jnp.argmax(gate_logits, axis=-1)
        out = jnp.zeros_like(x)
        for e in range(NUM_EXPERTS):
            mask = (top_idx == e)[..., None].astype(x.dtype)
            h = jax.nn.relu(jnp.einsum('bsd,df->bsf', x, w1[e]) + b1[e])
            y = jnp.einsum('bsf,fd->bsd', h, w2[e]) + b2[e]
            out = out + mask * y
        return out
    x = x + _L0_attn_ref(_layernorm(x, axis=-1), L0_attn_w_in, L0_attn_w_out, L0_attn_w_gate, L0_attn_b_gate, L0_attn_log_decay, L0_attn_frequency, L0_attn_coupling, L0_attn_w_mlp1, L0_attn_b_mlp1, L0_attn_w_mlp2, L0_attn_b_mlp2, L0_attn_ln1_g, L0_attn_ln1_b, L0_attn_ln2_g, L0_attn_ln2_b)
    x = x + _L0_xattn_ref(_layernorm(x, axis=-1), ctx_1024, ctx_1024, L0_xattn_Wq, L0_xattn_bq, L0_xattn_Wk, L0_xattn_bk, L0_xattn_Wv, L0_xattn_bv, L0_xattn_Wo, L0_xattn_bo)
    x = x + _L0_ffn_ref(_layernorm(x, axis=-1), L0_ffn_group_centroids, L0_ffn_expert_centroids, L0_ffn_bias, L0_ffn_wg, L0_ffn_wu, L0_ffn_wd, L0_ffn_sg, L0_ffn_su, L0_ffn_sd)
    x = x + _L1_attn_ref(_layernorm(x, axis=-1), L1_attn_Wq, L1_attn_bq, L1_attn_Wk, L1_attn_bk, L1_attn_Wv, L1_attn_bv, L1_attn_Wo, L1_attn_bo)
    x = x + _L1_xattn_ref(_layernorm(x, axis=-1), ctx_1024, ctx_1024, mask_BxSxS2_bk1, L1_xattn_Wq, L1_xattn_bq, L1_xattn_Wk, L1_xattn_bk, L1_xattn_Wv, L1_xattn_bv, L1_xattn_Wo, L1_xattn_bo, 16)
    x = x + _L1_ffn_ref(_layernorm(x, axis=-1), L1_ffn_gate_w, L1_ffn_gate_b, L1_ffn_expert_bias, L1_ffn_w1, L1_ffn_b1, L1_ffn_w2, L1_ffn_b2)
    return x

_drawn_inputs = setup_inputs


def setup_inputs(seed=0):
    import zlib

    import numpy as np

    out = dict(_drawn_inputs(seed))
    spreads = {'L0_attn_b_gate': (-2.0, 0.2),
     'L0_attn_b_mlp1': (0.0, 0.1),
     'L0_attn_b_mlp2': (0.0, 0.1),
     'L0_attn_ln1_g': (1.0, 0.2),
     'L0_attn_ln1_b': (0.0, 0.273),
     'L0_attn_ln2_g': (1.0, 0.2),
     'L0_attn_ln2_b': (0.0, 0.1),
     'L0_ffn_bias': (0.0, 0.1),
     'L1_attn_bq': (0.0, 0.8),
     'L1_attn_bk': (0.0, 0.8),
     'L1_attn_bv': (0.0, 0.409),
     'L1_attn_bo': (0.0, 0.1),
     'L1_xattn_bq': (0.0, 0.516),
     'L1_xattn_bk': (0.0, 0.8),
     'L1_xattn_bv': (0.0, 0.1),
     'L1_xattn_bo': (0.0, 0.1),
     'L1_ffn_expert_bias': (0.0, 0.1)}
    factors = {'L0_xattn_bq': 4.085,
     'L0_xattn_bk': 8.0,
     'L1_attn_Wq': 8.0,
     'L1_attn_Wk': 8.0,
     'L1_attn_Wv': 3.673,
     'L1_ffn_b1': 8.0,
     'L1_ffn_b2': 7.278}
    for name, (base, spread) in spreads.items():
        noise = np.random.default_rng([zlib.crc32(name.encode()), seed]).standard_normal(out[name].shape)
        drawn = base * np.exp(spread * noise) if base else spread * noise
        out[name] = jnp.asarray(drawn.astype(out[name].dtype))
    for name, factor in factors.items():
        out[name] = (out[name] * factor).astype(out[name].dtype)
    return out
```

```python
from contextlib import contextmanager

import numpy as np

import concourse.bass as bass
from concourse import mybir
from concourse.alu_op_type import AluOpType as ALU

F32 = mybir.dt.float32
BF16 = mybir.dt.bfloat16
I32 = mybir.dt.int32
U32 = mybir.dt.uint32
U8 = mybir.dt.uint8
ACT = mybir.ActivationFunctionType
AX = mybir.AxisListType

P = 128
B, T, D = 16, 100, 256
G = 4
NG = B // G
GT = G * T
S2 = 361
H, DH = 16, 16
KD = D // P
EPS = 1e-5
CHUNK = 64
MLP = 1024
NSTATE = 64
E0, NGRP, TOPK, CAP = 32, 8, 4, 250
HID = 512
E1, FF = 8, 1024
N = B * T
E1_ROWS = P
MAX_E1_TILES = -(-N // E1_ROWS)
TILES1 = (N + E1 * (E1_ROWS - 1)) // E1_ROWS
SLOTS0 = E0 * CAP
BIG = -1e30
FLOOR = -1e25
TWO_PI = 6.283185307179586

WIDTHS = [
    ("ident", P),
    ("chunk_keep", GT), ("tidx", CHUNK), ("rot_sign", 1), ("freq", 1), ("log_decay", 1),
    ("w_in", KD * P), ("w_in_swap", KD * P), ("w_gate", KD * D), ("w_out", D),
    ("coupling", P), ("coupling_swap", P),
    ("ln1_g", KD), ("ln1_b", KD), ("ln2_g", KD), ("ln2_b", KD),
    ("b_gate_row", D), ("w_mlp1", KD * MLP), ("b_mlp1", MLP // P),
    ("w_mlp2", MLP // P * D), ("b_mlp2_row", D),
    ("x0_wq", KD * D), ("x0_bq", KD), ("x0_wk", KD * D), ("x0_bk", KD), ("x0_wv", KD * D),
    ("x0_bv_row", D), ("x0_wo", KD * D), ("x0_bo_row", D),
    ("x1_wq", KD * D), ("x1_bq", KD), ("x1_wk", KD * D), ("x1_bk", KD), ("x1_wv", KD * D),
    ("x1_bv_row", D), ("x1_wo", KD * D), ("x1_bo_row", D),
    ("s_wq", KD * D), ("s_wq_rot", KD * D), ("s_bq", KD), ("s_bq_rot", KD),
    ("s_wk", KD * D), ("s_wk_rot", KD * D), ("s_bk", KD), ("s_bk_rot", KD),
    ("s_wv", KD * D), ("s_bv_row", D), ("s_wo", KD * D), ("s_bo_row", D),
    ("rope_cos", T), ("rope_sin", T),
    ("centroids", D), ("f0_bias_row", E0), ("f0_sg", KD * HID), ("f0_su", KD * HID),
    ("f0_sd", HID // P * D), ("iota_e", E0), ("spare_row", B * TOPK),
    ("f1_gate_w", KD * E1), ("f1_gate_b_row", E1), ("f1_ebias_row", E1), ("tok_id", B),
    ("tile_floor", E1 * MAX_E1_TILES), ("tile_no", TILES1), ("prefix_keep", E1 * B),
]
START = {}
_at = 0
for _name, _width in WIDTHS:
    START[_name] = (_at, _width)
    _at += _width
TOTAL = _at

BWIDTHS = [("ident_b", P), ("big_diag", G * T), ("head_sel", H), ("before", T), ("ones_b", T)]
BSTART = {}
_at = 0
for _name, _width in BWIDTHS:
    BSTART[_name] = (_at, _width)
    _at += _width
BTOTAL = _at

Q_PARTS = [0, 0, 1, 0, 2, 1]
K_PARTS = [0, 1, 0, 2, 0, 1]
SHIFT_ROW = 6 * DH
ROPE_PAIR = 2


def rope_tables():
    grid, dim = 16, 2 * (DH // 3 // 2)
    half = dim // 2
    ids = np.arange(T)
    frames = ids // (grid * grid)
    rem = ids - grid * grid * frames
    rows = rem // grid
    cols = rem - grid * rows
    inv = (1.0 / 10000.0 ** (np.arange(half, dtype=np.float32) / (dim / 2.0))).astype(np.float32)
    cos = np.ones((DH, T), np.float32)
    sin = np.zeros((DH, T), np.float32)
    for k, pos in enumerate((frames, rows, cols)):
        freq = pos.astype(np.float32)[:, None] * inv
        for j in range(dim):
            cos[k * dim + j] = np.cos(freq[:, j % half])
            sin[k * dim + j] = np.sin(freq[:, j % half]) * (-1.0 if j % 2 == 0 else 1.0)
    return np.repeat(cos, P // DH, axis=0), np.repeat(sin, P // DH, axis=0)


def host_layout(inp):
    def k_major(w):
        return w.reshape(w.shape[0] // P, P, w.shape[1]).transpose(1, 0, 2).reshape(P, -1)

    def col(v):
        return v.reshape(-1, P).T

    def row(v):
        return np.broadcast_to(v[None, :], (P, v.shape[0]))

    def rows_to(a, width):
        out = np.zeros((P, width), np.float32)
        out[:a.shape[0]] = a
        return out

    swap = np.r_[NSTATE:2 * NSTATE, 0:NSTATE]
    by_dim = np.arange(D).reshape(2, H // 2, DH).transpose(0, 2, 1).reshape(-1)
    w_in_t = inp["L0_attn_w_in"].T
    bd = np.zeros((P, P), np.float32)
    for part in range(2):
        for h in range(4):
            at = part * NSTATE + 16 * h
            bd[at:at + 16, at:at + 16] = inp["L0_attn_coupling"][h]
    t = np.arange(T)
    keep = np.ones(T, np.float32)
    keep[[CHUNK - 1, T - 1]] = 0.0
    cos, sin = rope_tables()
    a = {
        "ident": np.eye(P, dtype=np.float32),
        "chunk_keep": np.tile(row(keep), (1, G)),
        "tidx": row(np.arange(CHUNK, dtype=np.float32)),
        "rot_sign": np.repeat(np.array([-1.0, 1.0], np.float32), NSTATE)[:, None],
        "freq": np.tile(inp["L0_attn_frequency"], 2)[:, None],
        "log_decay": np.tile(inp["L0_attn_log_decay"], 2)[:, None],
        "w_in": k_major(w_in_t), "w_in_swap": k_major(w_in_t[:, swap]),
        "w_gate": k_major(inp["L0_attn_w_gate"].T), "w_out": inp["L0_attn_w_out"].T,
        "coupling": bd, "coupling_swap": bd[:, swap],
        "ln1_g": col(inp["L0_attn_ln1_g"]), "ln1_b": col(inp["L0_attn_ln1_b"]),
        "ln2_g": col(inp["L0_attn_ln2_g"]), "ln2_b": col(inp["L0_attn_ln2_b"]),
        "b_gate_row": row(inp["L0_attn_b_gate"]),
        "w_mlp1": k_major(inp["L0_attn_w_mlp1"].T), "b_mlp1": col(inp["L0_attn_b_mlp1"]),
        "w_mlp2": k_major(inp["L0_attn_w_mlp2"].T), "b_mlp2_row": row(inp["L0_attn_b_mlp2"]),
        "rope_cos": cos, "rope_sin": sin,
        "centroids": rows_to(np.concatenate([inp["L0_ffn_expert_centroids"],
                                             inp["L0_ffn_group_centroids"]]), D),
        "f0_bias_row": row(inp["L0_ffn_bias"]),
        "f0_sg": k_major(inp["L0_ffn_sg"]), "f0_su": k_major(inp["L0_ffn_su"]),
        "f0_sd": k_major(inp["L0_ffn_sd"]), "iota_e": row(np.arange(E0, dtype=np.float32)),
        "f1_gate_w": k_major(inp["L1_ffn_gate_w"].T), "f1_gate_b_row": row(inp["L1_ffn_gate_b"]),
        "f1_ebias_row": row(inp["L1_ffn_expert_bias"]),
        "spare_row": (SLOTS0 + np.arange(P)[:, None] % T + T * np.arange(B * TOPK)[None, :]).astype(np.float32),
        "tile_floor": row(np.tile(np.arange(MAX_E1_TILES, dtype=np.float32) * E1_ROWS, E1)),
        "tile_no": row(np.arange(TILES1, dtype=np.float32)),
        "prefix_keep": row(np.tile((np.arange(B) > 0).astype(np.float32), E1)),
        "tok_id": (np.arange(P)[:, None] + T * np.arange(B)[None, :]).astype(np.float32),
    }
    for x, name in (("x0", "L0_xattn"), ("x1", "L1_xattn")):
        for m in "qkvo":
            w, b = inp[f"{name}_W{m}"].T, inp[f"{name}_b{m}"]
            a[f"{x}_w{m}"] = k_major(w if m in "vo" else w[:, by_dim])
            a.update({f"{x}_b{m}_row": row(b)} if m in "vo" else {f"{x}_b{m}": col(b[by_dim])})
    for m in "qkvo":
        w, b = inp[f"L1_attn_W{m}"], inp[f"L1_attn_b{m}"]
        if m in "qk":
            a[f"s_w{m}"] = k_major(w[:, by_dim])
            a[f"s_b{m}"] = col(b[by_dim])
            a[f"s_w{m}_rot"] = k_major(w[:, by_dim ^ 1])
            a[f"s_b{m}_rot"] = col(b[by_dim ^ 1])
        else:
            a[f"s_w{m}"] = k_major(w)
            a[f"s_b{m}_row"] = row(b)
    packed = np.concatenate([a[n] for n, _ in WIDTHS], axis=1)
    assert packed.shape == (P, TOTAL) and all(a[n].shape[1] == w for n, w in WIDTHS)

    bf = mybir.dt.np(BF16)
    big = np.zeros((P, G, T), np.float32)
    big[t, :, t] = BIG
    head_sel = np.zeros((P, H), np.float32)
    for part in range(2):
        head_sel[SHIFT_ROW + part * H + np.arange(H), np.arange(H)] = 1.0
    before = np.zeros((P, T), np.float32)
    before[:T] = (t[:, None] < t[None, :])
    c = {"ident_b": np.eye(P), "big_diag": big.reshape(P, -1), "head_sel": head_sel,
         "before": before, "ones_b": np.ones((P, T))}
    consts = np.concatenate([np.asarray(c[n], np.float32) for n, _ in BWIDTHS], axis=1).astype(bf)
    ctx = inp["ctx_1024"]
    return {
        "x": inp["x"],
        "ctx_t": ctx.reshape(B, S2, KD, P).transpose(0, 3, 2, 1),
        "mask": inp["mask_BxSxS2_bk1"],
        "packed": packed,
        "consts": consts,
        "wg": inp["L0_ffn_wg"].reshape(E0, KD, P, HID).transpose(0, 2, 1, 3),
        "wu": inp["L0_ffn_wu"].reshape(E0, KD, P, HID).transpose(0, 2, 1, 3),
        "wd": inp["L0_ffn_wd"].reshape(E0, HID // P, P, D).transpose(0, 2, 1, 3),
        "w1": inp["L1_ffn_w1"].reshape(E1, KD, P, FF).transpose(0, 2, 1, 3),
        "b1": inp["L1_ffn_b1"].reshape(E1, FF // P, P).transpose(0, 2, 1),
        "w2": inp["L1_ffn_w2"].reshape(E1, FF // P, P, D).transpose(0, 2, 1, 3),
        "b2": inp["L1_ffn_b2"],
    }


class Program:

    def __init__(self, nc, ins, out):
        self.nc = nc
        self.ins = ins
        self.out = out

        def dram(name, shape, dt=F32):
            return nc.dram_tensor(name, shape, dt, kind="Internal").ap()

        self.x = [ins["x"]] + [dram(f"x_after_{k}", [B, T, D]) for k in range(5)]
        self.q_stack = [dram(f"q_stack_{l}", [B, 2, 6, P, T], BF16) for l in range(3)]
        self.k_stack = [dram(f"k_stack_{l}", [B, 2, 6, P, n], BF16) for l, n in enumerate((S2, T, S2))]
        self.xn_t = dram("xn_t_self", [B, P, KD, T])
        self.ln_rows = [dram(f"ln_rows_{l}", [N, D]) for l in range(2)]
        self.row_token = [dram("row_token_0", [SLOTS0 + N * TOPK, 1], I32),
                          dram("row_token_1", [TILES1 * E1_ROWS, 1], I32)]
        self.expert_out = [dram("expert_out_0", [SLOTS0, D]), dram("expert_out_1", [TILES1 * E1_ROWS, D])]
        self.choice_row = dram("choice_row", [B, T, TOPK], I32)
        self.choice_gate = dram("choice_gate", [B, T, TOPK])
        self.x_shared = dram("x_shared", [B, T, D])
        self.route1_rows = 13
        self.row1 = nc.alloc_sbuf_tensor("row1", [T, B], I32)
        self.tile_expert = nc.alloc_sbuf_tensor("tile_expert", [1, TILES1], I32)
        self.packed = nc.alloc_sbuf_tensor("packed_sb", [P, TOTAL], F32)
        self.consts = nc.alloc_sbuf_tensor("consts_sb", [P, BTOTAL], BF16)
        self.rot_cos = nc.alloc_sbuf_tensor("rot_cos", [P, GT], F32)
        self.rot_sin = nc.alloc_sbuf_tensor("rot_sin", [P, GT], F32)
        self.decay = nc.alloc_sbuf_tensor("decay", [P, GT], F32)
        self.w_mix = nc.alloc_sbuf_tensor("w_mix", [P, 2, D], F32)
        self.half_neg = nc.alloc_sbuf_tensor("half_neg", [P, G], F32)
        self.cent_t = nc.alloc_sbuf_tensor("cent_t", [P, KD, E0 + NGRP], F32)

    def w(self, name, k=None):
        at, width = START[name]
        ap = self.packed[:, at:at + width]
        return ap if k is None else ap.rearrange("p (k n) -> p k n", k=k)

    def c(self, name):
        at, width = BSTART[name]
        return self.consts[:, at:at + width]


@contextmanager
def stage(nc, label):
    made, cms = [], []

    def sem(name):
        made.append(nc.alloc_semaphore(f"{label}_{name}"))
        return made[-1]

    def sbuf(name, shape, dt=F32):
        cm = nc.sbuf_tensor(f"{label}_{name}", shape, dt)
        cms.append(cm)
        return cm.__enter__()

    def psum(name, shape, dt=F32):
        cm = nc.psum_tensor(f"{label}_{name}", shape, dt)
        cms.append(cm)
        return cm.__enter__()

    yield sem, sbuf, psum
    for cm in reversed(cms):
        cm.__exit__(None, None, None)
    nc.clear_and_free_semaphores(made)
    nc.all_engine_barrier()


def stage_setup(prog):
    nc = prog.nc
    with stage(nc, "setup") as (sem, sbuf, psum):
        loaded, consts_in = sem("packed_loaded"), sem("consts_loaded")
        v_done, a_done, pe_done, g_done = (sem(n) for n in ("v_done", "a_done", "pe_done", "g_done"))
        ang = sbuf("ang", [P, CHUNK])
        turns = sbuf("turns", [P, CHUNK])
        halfa = sbuf("halfa", [P, CHUNK])
        sn = sbuf("sn", [P, CHUNK])
        sh = sbuf("sh", [P, CHUNK])
        mag = sbuf("mag", [P, 2])
        cent = sbuf("cent", [P, D])
        cst = sbuf("cst", [P, 4])
        ps_mix = psum("ps_mix", [P, 2, D])
        ps_cent = psum("ps_cent", [P, KD, P])
        NC_ = E0 + NGRP
        order = {}

        with nc.Block() as block:
            @block.sync
            def _(sp):
                sp.dma_start(prog.consts[:], prog.ins["consts"]).then_inc(consts_in, 16)
                sp.dma_start(prog.packed[:], prog.ins["packed"]).then_inc(loaded, 16)
                sp.wait_ge(consts_in, 16)

            @block.vector
            def _(v):
                n = [0]

                def step(ins):
                    n[0] += 1
                    ins.then_inc(v_done, 1)
                    v.wait_ge(v_done, n[0])

                step(nc.vector.memset(prog.half_neg[:], -0.5))
                step(nc.vector.memset(cst[:, 3:4], 0.5))
                v.wait_ge(loaded, 16)
                step(nc.vector.tensor_scalar(ang[:], prog.w("tidx"), prog.w("freq"), None, ALU.mult))
                step(nc.vector.tensor_scalar(turns[:], ang[:], 1.0 / TWO_PI, 12582912.0, ALU.mult, ALU.add))
                step(nc.vector.tensor_scalar(turns[:], turns[:], -12582912.0, None, ALU.add))
                for c in (6.28125, 0.0019340515136718750, 1.2556659146019e-06):
                    step(nc.vector.scalar_tensor_tensor(ang[:], turns[:], -c, ang[:], ALU.mult, ALU.add))
                step(nc.vector.tensor_scalar(ang[:], ang[:], 3.1415925, -3.1415925, ALU.min, ALU.max))
                step(nc.vector.tensor_scalar(halfa[:], ang[:], 0.5, None, ALU.mult))
                order["angles"] = n[0]
                v.wait_ge(a_done, 2)
                step(nc.vector.scalar_tensor_tensor(halfa[:], sh[:], -2.0, sh[:], ALU.mult, ALU.mult))
                step(nc.vector.tensor_scalar(halfa[:], halfa[:], 1.0, None, ALU.add))
                step(nc.vector.tensor_scalar(sn[:], sn[:], prog.w("rot_sign"), None, ALU.mult))
                for table, by_pos in ((prog.rot_cos, halfa), (prog.rot_sin, sn)):
                    view = table[:].rearrange("p (g t) -> p g t", g=G)
                    for at in (0, CHUNK):
                        width = min(CHUNK, T - at)
                        step(nc.vector.tensor_copy(
                            view[:, :, at:at + width],
                            by_pos[:, 0:width].unsqueeze(1).broadcast_to([P, G, width])))
                v.wait_ge(a_done, 3)
                step(nc.vector.tensor_scalar(mag[:, 0:1], mag[:, 0:1], 1.0, None, ALU.add))
                step(nc.vector.reciprocal(mag[:, 1:2], mag[:, 0:1]))
                step(nc.vector.tensor_scalar(prog.decay[:], prog.w("chunk_keep"), mag[:, 1:2], None, ALU.mult))
                step(nc.vector.tensor_tensor_reduce(cent[0:NC_, :], prog.w("centroids")[0:NC_, :],
                                                    prog.w("centroids")[0:NC_, :], 1.0, 0.0,
                                                    ALU.mult, ALU.add, cst[0:NC_, 0:1]))
                order["sums of squares"] = n[0]
                v.wait_ge(g_done, 1)
                step(nc.vector.tensor_scalar(cst[0:NC_, 1:2], cst[0:NC_, 1:2], 1e-12, None, ALU.max))
                step(nc.vector.reciprocal(cst[0:NC_, 2:3], cst[0:NC_, 1:2]))
                step(nc.vector.tensor_scalar(cent[0:NC_, :], prog.w("centroids")[0:NC_, :],
                                             cst[0:NC_, 2:3], None, ALU.mult))
                order["centroids scaled"] = n[0]
                v.wait_ge(pe_done, 1)
                step(nc.vector.tensor_copy(prog.w_mix[:], ps_mix[:]))
                v.wait_ge(pe_done, 2)
                step(nc.vector.tensor_copy(prog.cent_t[:], ps_cent[:, :, 0:NC_]))

            @block.scalar
            def _(act):
                act.wait_ge(v_done, order["angles"])
                nc.scalar.activation(sn[:], ang[:], ACT.Sin).then_inc(a_done, 1)
                nc.scalar.activation(sh[:], halfa[:], ACT.Sin).then_inc(a_done, 1)
                nc.scalar.activation(mag[:, 0:1], prog.w("log_decay"), ACT.Exp, scale=-1.0).then_inc(a_done, 1)

            @block.gpsimd
            def _(g):
                g.wait_ge(v_done, order["sums of squares"])
                nc.gpsimd.tensor_tensor(cst[0:NC_, 1:2], cst[0:NC_, 0:1], cst[0:NC_, 3:4],
                                        ALU.pow).then_inc(g_done, 1)

            @block.tensor
            def _(pe):
                pe.wait_ge(loaded, 16)
                for s, name in enumerate(("coupling", "coupling_swap")):
                    ins = nc.tensor.matmul(ps_mix[:, s, :], prog.w(name), prog.w("w_out"),
                                           start=True, stop=True)
                ins.then_inc(pe_done, 1)
                pe.wait_ge(v_done, order["centroids scaled"])
                for k in range(KD):
                    ins = nc.tensor.transpose(ps_cent[:, k, 0:NC_], cent[0:NC_, k * P:(k + 1) * P],
                                              prog.w("ident")[0:NC_, 0:NC_])
                ins.then_inc(pe_done, 1)


def stage_mixer(prog):
    nc = prog.nc
    x_dram, out_dram = prog.x[0], prog.x[1]
    NM = MLP // P
    with stage(nc, "mixer") as (sem, sbuf, psum):
        x_in = sem("x_in")
        x_free = sem("x_free")
        v_stat = [sem(f"v_stat{k}") for k in range(3)]
        g_rstd = [sem(f"g_rstd{k}") for k in range(3)]
        v_link = [sem(f"v_link{k}") for k in range(10)]
        v_norm = [sem(f"v_norm{k}") for k in range(3)]
        pe_xt = sem("pe_xt")
        xt_ready = sem("xt_ready")
        pe_beta, pe_gate, pe_h = sem("pe_beta"), sem("pe_gate"), sem("pe_h")
        v_z, a_tanh = sem("v_z"), sem("a_tanh")
        v_states = sem("v_states")
        v_gh, v_x1 = sem("v_gh"), sem("v_x1")
        g_base = sem("g_base")
        pe_x2t, x2t_ready = sem("pe_x2t"), sem("x2t_ready")
        pe_up = [sem(f"pe_up{m}") for m in range(NM)]
        a_up = [sem(f"a_up{m}") for m in range(NM)]
        pe_down = sem("pe_down")
        v_out = sem("v_out")
        out_stored = sem("out_stored")

        xg = sbuf("xg", [T, G, D])
        stats = sbuf("stats", [T, G, 6])
        mv = sbuf("mv", [T, 3, G, 2])
        var = sbuf("var", [T, 3, G])
        rstd = sbuf("rstd", [T, 3, G])
        xin = sbuf("xin", [T, G, D])
        xh = sbuf("xh", [T, G, D])
        xt = sbuf("xt", [P, KD, GT])
        u1 = sbuf("u1", [P, GT])
        u2 = sbuf("u2", [P, GT])
        v = sbuf("v", [P, GT])
        sa = sbuf("sa", [P, GT])
        sb_ = sbuf("sb_", [P, GT])
        z = sbuf("z", [T, G, D])
        x1 = sbuf("x1", [T, G, D])
        base = sbuf("base", [T, G, D])
        xo = sbuf("xo", [T, G, D])
        up = sbuf("up", [P, NM, GT])
        bank = [psum(f"bank{k}", [P, 512]) for k in range(8)]
        ident = prog.w("ident")

        def tok(banks, j):
            return banks[j // 2][0:T, (j % 2) * D:(j % 2 + 1) * D]

        with nc.Block() as block:
            @block.sync
            def _(sp):
                with sp.Fori(1, NG + 1) as i:
                    sp.wait_ge(x_free, i)
                    src = x_dram[bass.ds((i - 1) * G, G)].rearrange("g t d -> t g d")
                    sp.dma_start(xg[:], src).then_inc(x_in, 16)
                    sp.wait_ge(v_out, i)
                    dst = out_dram[bass.ds((i - 1) * G, G)].rearrange("g t d -> t g d")
                    sp.dma_start(dst, xo[:]).then_inc(out_stored, 16)
                sp.wait_ge(out_stored, 16 * NG)

            @block.vector
            def _(ve):
                def moments(k, src, i):
                    for j in range(G):
                        ins = nc.vector.bn_stats(stats[:, j, :], src[:, j, :])
                    ins.then_inc(v_link[2 * k], 1)
                    ve.wait_ge(v_link[2 * k], i)
                    ve.sem_inc(v_link[2 * k + 1], 1)
                    for j in range(G):
                        ins = nc.vector.bn_aggr(mv[:, k, j, :], stats[:, j, :])
                    ins.then_inc(v_link[2 * k + 1], 1)
                    ve.wait_ge(v_link[2 * k + 1], i * 2)
                    nc.vector.tensor_scalar(var[:, k, :], mv[:, k, :, 1], EPS, None, ALU.add).then_inc(v_stat[k], 1)

                def normalise(k, dst, src, i):
                    ve.wait_ge(g_rstd[k], i)
                    for j in range(G):
                        ins = nc.vector.tensor_scalar(dst[:, j, :], src[:, j, :], mv[:, k, j, 0:1],
                                                      rstd[:, k, j:j + 1], ALU.subtract, ALU.mult)
                    ins.then_inc(v_norm[k], 1)
                    ve.wait_ge(v_norm[k], i)

                nc.vector.memset(sa[:, 0:1], 0.0).then_inc(x_free, 1)
                with ve.Fori(1, NG + 1) as i:
                    ve.wait_ge(x_in, i * 16)
                    moments(0, xg, i)
                    normalise(0, xin, xg, i)
                    moments(1, xin, i)
                    normalise(1, xh, xin, i)
                    ve.wait_ge(pe_xt, i)
                    nc.vector.tensor_scalar(xt[:, 1, :], bank[1][:, 0:GT], prog.w("ln1_g")[:, 1:2],
                                            prog.w("ln1_b")[:, 1:2], ALU.mult, ALU.add).then_inc(xt_ready, 1)
                    ve.wait_ge(pe_beta, i)
                    nc.vector.tensor_tensor(u1[:], bank[2][:, 0:GT], prog.rot_cos[:], ALU.mult)
                    nc.vector.tensor_tensor(u2[:], bank[3][:, 0:GT], prog.rot_sin[:], ALU.mult).then_inc(v_link[6], 1)
                    ve.wait_ge(v_link[6], i)
                    nc.vector.tensor_tensor(u1[:], u1[:], u2[:], ALU.add).then_inc(v_link[7], 1)
                    ve.wait_ge(v_link[7], i)
                    nc.vector.tensor_tensor_scan(v[:, ::-1], prog.decay[:, ::-1], u1[:, ::-1], 0.0,
                                                 ALU.mult, ALU.add).then_inc(v_link[8], 1)
                    ve.wait_ge(v_link[8], i)
                    by_seq = v[:].rearrange("p (g t) -> p g t", g=G)
                    beta_seq = bank[2][:, 0:GT].rearrange("p (g t) -> p g t", g=G)
                    nc.vector.tensor_tensor(by_seq[:, :, CHUNK], by_seq[:, :, CHUNK],
                                            beta_seq[:, :, CHUNK - 1], ALU.add).then_inc(v_link[9], 1)
                    ve.wait_ge(v_link[9], i)
                    nc.vector.tensor_tensor(sa[:], v[:], prog.rot_cos[:], ALU.mult)
                    nc.vector.tensor_tensor(sb_[:], v[:], prog.rot_sin[:], ALU.mult).then_inc(v_states, 1)
                    ve.wait_ge(pe_gate, i)
                    for h in range(2):
                        ins = nc.vector.tensor_tensor(
                            z[:, 2 * h:2 * h + 2, :], bank[4 + h][0:T, :].rearrange("p (g d) -> p g d", g=2),
                            prog.w("b_gate_row")[0:T].unsqueeze(1).broadcast_to([T, 2, D]), ALU.add)
                    ins.then_inc(v_z, 1)
                    ve.wait_ge(a_tanh, i)
                    ve.wait_ge(pe_h, i)
                    for h in range(2):
                        ins = nc.vector.scalar_tensor_tensor(
                            z[:, 2 * h:2 * h + 2, :], z[:, 2 * h:2 * h + 2, :], 1.0,
                            bank[6 + h][0:T, :].rearrange("p (g d) -> p g d", g=2), ALU.add, ALU.mult)
                    ins.then_inc(v_gh, 1)
                    ve.wait_ge(v_gh, i)
                    nc.vector.scalar_tensor_tensor(x1[:], z[:], 0.5, xin[:], ALU.mult, ALU.add).then_inc(v_x1, 1)
                    ve.wait_ge(v_x1, i)
                    moments(2, x1, i)
                    normalise(2, xh, x1, i)
                    ve.wait_ge(pe_x2t, i)
                    nc.vector.tensor_scalar(xt[:, 1, :], bank[1][:, 0:GT], prog.w("ln2_g")[:, 1:2],
                                            prog.w("ln2_b")[:, 1:2], ALU.mult, ALU.add).then_inc(x2t_ready, 1)
                    ve.wait_ge(pe_down, i)
                    ve.wait_ge(g_base, i)
                    for h in range(2):
                        ins = nc.vector.tensor_tensor(
                            xo[:, 2 * h:2 * h + 2, :], bank[6 + h][0:T, :].rearrange("p (g d) -> p g d", g=2),
                            base[:, 2 * h:2 * h + 2, :], ALU.add)
                    ins.then_inc(v_out, 1)

            @block.gpsimd
            def _(g):
                def inverse_root(k, i):
                    g.wait_ge(v_stat[k], i)
                    nc.gpsimd.tensor_tensor(rstd[:, k, :], var[:, k, :], prog.half_neg[0:T, :],
                                            ALU.pow).then_inc(g_rstd[k], 1)

                with g.Fori(1, NG + 1) as i:
                    inverse_root(0, i)
                    inverse_root(1, i)
                    g.wait_ge(v_x1, i)
                    nc.gpsimd.tensor_tensor(base[:], xg[:], x1[:], ALU.add).then_inc(x_free, 1)
                    inverse_root(2, i)
                    g.wait_ge(x_free, i + 1)
                    nc.gpsimd.tensor_tensor(base[:], base[:],
                                            prog.w("b_mlp2_row")[0:T].unsqueeze(1).broadcast_to([T, G, D]),
                                            ALU.add).then_inc(g_base, 1)

            @block.scalar
            def _(act):
                with act.Fori(1, NG + 1) as i:
                    act.wait_ge(pe_xt, i)
                    nc.scalar.activation(xt[:, 0, :], bank[0][:, 0:GT], ACT.Identity,
                                         scale=prog.w("ln1_g")[:, 0:1], bias=prog.w("ln1_b")[:, 0:1]
                                         ).then_inc(xt_ready, 1)
                    act.wait_ge(v_z, i)
                    nc.scalar.activation(z[:], z[:], ACT.Tanh, scale=0.5).then_inc(a_tanh, 1)
                    act.wait_ge(pe_x2t, i)
                    nc.scalar.activation(xt[:, 0, :], bank[0][:, 0:GT], ACT.Identity,
                                         scale=prog.w("ln2_g")[:, 0:1], bias=prog.w("ln2_b")[:, 0:1]
                                         ).then_inc(x2t_ready, 1)
                    for m in range(NM):
                        act.wait_ge(pe_up[m], i)
                        nc.scalar.activation(up[:, m, :], bank[2 + m % 4][:, 0:GT], ACT.Silu,
                                             bias=prog.w("b_mlp1")[:, m:m + 1]).then_inc(a_up[m], 1)

            @block.tensor
            def _(pe):
                def transpose_rows(done):
                    for c in range(KD):
                        for j in range(G):
                            ins = nc.tensor.transpose(bank[c][:, j * T:(j + 1) * T],
                                                      xh[:, j, c * P:(c + 1) * P], ident[0:T, 0:T])
                    ins.then_inc(done, 1)

                with pe.Fori(1, NG + 1) as i:
                    pe.wait_ge(v_norm[1], i)
                    transpose_rows(pe_xt)
                    pe.wait_ge(xt_ready, i * 2)
                    for s, name in enumerate(("w_in", "w_in_swap")):
                        for k in range(KD):
                            ins = nc.tensor.matmul(bank[2 + s][:, 0:GT], prog.w(name, KD)[:, k, :], xt[:, k, :],
                                                   start=(k == 0), stop=(k == KD - 1))
                    ins.then_inc(pe_beta, 1)
                    for j in range(G):
                        for k in range(KD):
                            ins = nc.tensor.matmul(tok(bank[4:6], j), xt[:, k, j * T:(j + 1) * T],
                                                   prog.w("w_gate", KD)[:, k, :], start=(k == 0), stop=(k == KD - 1))
                    ins.then_inc(pe_gate, 1)
                    pe.wait_ge(v_states, i)
                    for j in range(G):
                        for s, states in enumerate((sa, sb_)):
                            ins = nc.tensor.matmul(tok(bank[6:8], j), states[:, j * T:(j + 1) * T],
                                                   prog.w_mix[:, s, :], start=(s == 0), stop=(s == 1))
                    ins.then_inc(pe_h, 1)
                    pe.wait_ge(v_norm[2], i)
                    transpose_rows(pe_x2t)
                    pe.wait_ge(x2t_ready, i * 2)
                    for m in range(NM):
                        if m >= 4:
                            pe.wait_ge(a_up[m - 4], i)
                        for k in range(KD):
                            ins = nc.tensor.matmul(bank[2 + m % 4][:, 0:GT],
                                                   prog.w("w_mlp1", KD)[:, k, m * P:(m + 1) * P], xt[:, k, :],
                                                   start=(k == 0), stop=(k == KD - 1))
                        ins.then_inc(pe_up[m], 1)
                    pe.wait_ge(a_up[NM - 1], i)
                    for j in range(G):
                        for m in range(NM):
                            ins = nc.tensor.matmul(tok(bank[6:8], j), up[:, m, j * T:(j + 1) * T],
                                                   prog.w("w_mlp2", NM)[:, m, :], start=(m == 0), stop=(m == NM - 1))
                    ins.then_inc(pe_down, 1)


def stage_context_keys(prog):
    nc = prog.nc
    LAYERS = ((0, "x0"), (2, "x1"))
    SLOTS = 2
    ROUNDS = B // SLOTS
    with stage(nc, "ctx") as (sem, sbuf, psum):
        def per_slot(name):
            return [[sem(f"{name}_{s}_{l}") for l in range(2)] for s in range(SLOTS)]

        ctx_in = [sem(f"ctx_in{s}") for s in range(SLOTS)]
        pe_k = per_slot("pe_k")
        a_full = per_slot("a_full")
        a_part1 = per_slot("a_part1")
        v_rest = per_slot("v_rest")
        a_part2 = per_slot("a_part2")
        v_part3 = per_slot("v_part3")
        stored = per_slot("stored")
        part_free = per_slot("part_free")
        ctx = [sbuf(f"ctx{s}", [P, KD, S2]) for s in range(SLOTS)]
        full = [[sbuf(f"full{s}_{l}", [P, KD, S2]) for l in range(2)] for s in range(SLOTS)]
        rest = [[sbuf(f"rest{s}_{l}", [P, KD, S2]) for l in range(2)] for s in range(SLOTS)]
        part = [[sbuf(f"part{s}_{l}", [P, 3, KD, S2], BF16) for l in range(2)] for s in range(SLOTS)]
        bank = [[[psum(f"bank{s}_{l}_{m}", [P, 512]) for m in range(KD)] for l in range(2)]
                for s in range(SLOTS)]

        with nc.Block() as block:
            @block.sync
            def _(sp):
                for s in range(SLOTS):
                    for l in range(2):
                        sp.sem_inc(part_free[s][l], 1)
                with sp.Fori(1, ROUNDS + 1) as i:
                    for s in range(SLOTS):
                        for l, (layer, _) in enumerate(LAYERS):
                            sp.wait_ge(v_part3[s][l], i + 1)
                            dst = prog.k_stack[layer][bass.ds(i * SLOTS + (s - SLOTS), 1)]
                            for g in range(6):
                                sp.dma_start(dst[:, :, g].rearrange("b m p n -> p (b m) n"),
                                             part[s][l][:, K_PARTS[g]]).then_inc(stored[s][l], 16)
                    for s in range(SLOTS):
                        for l in range(2):
                            sp.wait_ge(stored[s][l], i * 96)
                            sp.sem_inc(part_free[s][l], 1)

            @block.tensor
            def _(pe):
                for s in range(SLOTS):
                    for l in range(2):
                        pe.sem_inc(pe_k[s][l], 1)
                with pe.Fori(1, ROUNDS + 1) as i:
                    for s in range(SLOTS):
                        pe.wait_ge(ctx_in[s], i * 16)
                        for l, (_, x) in enumerate(LAYERS):
                            pe.wait_ge(a_full[s][l], i)
                            for m in range(KD):
                                for k in range(KD):
                                    ins = nc.tensor.matmul(bank[s][l][m][:, 0:S2],
                                                           prog.w(f"{x}_wk", KD)[:, k, m * P:(m + 1) * P],
                                                           ctx[s][:, k, :], start=(k == 0), stop=(k == KD - 1))
                            ins.then_inc(pe_k[s][l], 1)

            @block.scalar
            def _(act):
                for s in range(SLOTS):
                    for l in range(2):
                        act.sem_inc(a_full[s][l], 1)
                with act.Fori(1, ROUNDS + 1) as i:
                    for s in range(SLOTS):
                        for l, (_, x) in enumerate(LAYERS):
                            act.wait_ge(pe_k[s][l], i + 1)
                            act.wait_ge(v_part3[s][l], i)
                            for m in range(KD):
                                ins = nc.scalar.activation(full[s][l][:, m, :], bank[s][l][m][:, 0:S2],
                                                           ACT.Identity, bias=prog.w(f"{x}_bk")[:, m:m + 1])
                            ins.then_inc(a_full[s][l], 1)
                            act.wait_ge(a_full[s][l], i + 1)
                            act.wait_ge(part_free[s][l], i)
                            nc.scalar.copy(part[s][l][:, 0], full[s][l][:]).then_inc(a_part1[s][l], 1)
                        for l in range(2):
                            act.wait_ge(v_rest[s][l], i)
                            nc.scalar.copy(part[s][l][:, 1], rest[s][l][:]).then_inc(a_part2[s][l], 1)

            @block.vector
            def _(ve):
                for s in range(SLOTS):
                    for l in range(2):
                        ve.sem_inc(v_part3[s][l], 1)
                with ve.Fori(1, ROUNDS + 1) as i:
                    for s in range(SLOTS):
                        for l in range(2):
                            ve.wait_ge(a_part1[s][l], i)
                            nc.vector.tensor_tensor(rest[s][l][:], full[s][l][:], part[s][l][:, 0],
                                                    ALU.subtract).then_inc(v_rest[s][l], 1)
                        for l in range(2):
                            ve.wait_ge(a_part2[s][l], i)
                            nc.vector.tensor_tensor(part[s][l][:, 2], rest[s][l][:], part[s][l][:, 1],
                                                    ALU.subtract).then_inc(v_part3[s][l], 1)

            @block.gpsimd
            def _(g):
                with g.Fori(1, ROUNDS + 1) as i:
                    for s in range(SLOTS):
                        g.wait_ge(pe_k[s][1], i)
                        g.dma_start(ctx[s][:], prog.ins["ctx_t"][bass.ds(i * SLOTS + (s - SLOTS), 1)]
                                    .rearrange("b p k n -> p (b k) n")).then_inc(ctx_in[s], 16)


def stage_queries(prog, layer, with_keys):
    nc = prog.nc
    name = ("x0", "s", "x1")[layer]
    x_dram = prog.x[(1, 3, 4)[layer]]
    KINDS = [("q", prog.q_stack[layer], Q_PARTS)]
    if with_keys:
        KINDS.append(("k", prog.k_stack[layer], K_PARTS))
    NK = len(KINDS)
    with stage(nc, f"queries{layer}") as (sem, sbuf, psum):
        x_in, v_stat, g_rstd, v_norm = sem("x_in"), sem("v_stat"), sem("g_rstd"), sem("v_norm")
        v_link = [sem(f"v_link{k}") for k in range(2 + NK)]
        x_free = sem("x_free")
        pe_xt, a_xt, v_xt = sem("pe_xt"), sem("a_xt"), sem("v_xt")
        pe_k = [sem(f"pe_{k[0]}") for k in KINDS]
        full_ready = [sem(f"full_ready_{k[0]}") for k in KINDS]
        v_turn = [sem(f"v_turn_{k[0]}") for k in KINDS]
        a_part1 = [sem(f"a_part1_{k[0]}") for k in KINDS]
        v_rest = [sem(f"v_rest_{k[0]}") for k in KINDS]
        a_part2 = [sem(f"a_part2_{k[0]}") for k in KINDS]
        v_part3 = [sem(f"v_part3_{k[0]}") for k in KINDS]
        stored = [sem(f"stored_{k[0]}") for k in KINDS]
        part_free = [sem(f"part_free_{k[0]}") for k in KINDS]
        xt_stored, xt_free = sem("xt_stored"), sem("xt_free")

        xg = sbuf("xg", [T, G, D])
        stats = sbuf("stats", [T, G, 6])
        mv = sbuf("mv", [T, G, 2])
        var = sbuf("var", [T, G])
        rstd = sbuf("rstd", [T, G])
        xh = sbuf("xh", [T, G, D])
        xt = sbuf("xt", [P, KD, GT])
        full = [sbuf(f"full_{k[0]}", [P, KD, GT]) for k in KINDS]
        turned = [sbuf(f"turned_{k[0]}", [P, KD, GT]) for k in KINDS] if with_keys else None
        rest = [sbuf(f"rest_{k[0]}", [P, KD, GT]) for k in KINDS]
        part = [sbuf(f"part_{k[0]}", [P, 3, KD, GT], BF16) for k in KINDS]
        bank = [psum(f"bank{k}", [P, 512]) for k in range(8)]

        def banks_of(kind, rot, m):
            return bank[(2 + 4 * kind + 2 * rot + m) % 8][:, 0:GT]

        with nc.Block() as block:
            @block.sync
            def _(sp):
                for n in range(NK):
                    sp.sem_inc(part_free[n], 1)
                sp.sem_inc(xt_free, 1)
                with sp.Fori(1, NG + 1) as i:
                    sp.wait_ge(x_free, i)
                    sp.dma_start(xg[:], x_dram[bass.ds((i - 1) * G, G)].rearrange("g t d -> t g d")
                                 ).then_inc(x_in, 16)
                    if with_keys:
                        sp.wait_ge(a_xt, i)
                        sp.wait_ge(v_xt, i)
                        for k in range(KD):
                            sp.dma_start(prog.xn_t[bass.ds((i - 1) * G, G), :, k].rearrange("g p t -> p g t"),
                                         xt[:, k, :].rearrange("p (g t) -> p g t", g=G)).then_inc(xt_stored, 16)
                    for n, (_, stack, parts) in enumerate(KINDS):
                        sp.wait_ge(v_part3[n], i)
                        for m in range(KD):
                            for g in range(6):
                                sp.dma_start(stack[bass.ds((i - 1) * G, G), m, g].rearrange("b p t -> p b t"),
                                             part[n][:, parts[g], m].rearrange("p (b t) -> p b t", b=G)
                                             ).then_inc(stored[n], 16)
                    for n in range(NK):
                        sp.wait_ge(stored[n], i * (12 * 16))
                        sp.sem_inc(part_free[n], 1)
                    if with_keys:
                        sp.wait_ge(xt_stored, i * (KD * 16))
                    sp.sem_inc(xt_free, 1)

            @block.vector
            def _(ve):
                ve.sem_inc(x_free, 1)
                with ve.Fori(1, NG + 1) as i:
                    ve.wait_ge(x_in, i * 16)
                    for j in range(G):
                        ins = nc.vector.bn_stats(stats[:, j, :], xg[:, j, :])
                    ins.then_inc(v_link[0], 1)
                    ve.wait_ge(v_link[0], i)
                    ve.sem_inc(v_link[1], 1)
                    for j in range(G):
                        ins = nc.vector.bn_aggr(mv[:, j, :], stats[:, j, :])
                    ins.then_inc(v_link[1], 1)
                    ve.wait_ge(v_link[1], i * 2)
                    nc.vector.tensor_scalar(var[:], mv[:, :, 1], EPS, None, ALU.add).then_inc(v_stat, 1)
                    ve.wait_ge(g_rstd, i)
                    for j in range(G):
                        ins = nc.vector.tensor_scalar(xh[:, j, :], xg[:, j, :], mv[:, j, 0:1], rstd[:, j:j + 1],
                                                      ALU.subtract, ALU.mult)
                    ins.then_inc(v_norm, 1)
                    ve.wait_ge(v_norm, i)
                    ve.sem_inc(x_free, 1)
                    ve.wait_ge(pe_xt, i)
                    ve.wait_ge(xt_free, i)
                    nc.vector.tensor_copy(xt[:, 1, :], bank[1][:, 0:GT]).then_inc(v_xt, 1)
                    for n, (kind, _, _) in enumerate(KINDS):
                        ve.wait_ge(pe_k[n], i)
                        for m in range(KD):
                            if not with_keys:
                                ins = nc.vector.tensor_scalar(full[n][:, m, :], banks_of(n, 0, m),
                                                              prog.w(f"{name}_b{kind}")[:, m:m + 1], None, ALU.add)
                                continue
                            for rot, (dst, table) in enumerate(((full[n], "rope_cos"), (turned[n], "rope_sin"))):
                                bias = prog.w(f"{name}_b{kind}" + ("_rot" if rot else ""))[:, m:m + 1]
                                ins = nc.vector.scalar_tensor_tensor(
                                    dst[:, m, :].rearrange("p (g t) -> p g t", g=G),
                                    banks_of(n, rot, m).rearrange("p (g t) -> p g t", g=G), bias,
                                    prog.w(table).unsqueeze(1).broadcast_to([P, G, T]), ALU.add, ALU.mult)
                        if with_keys:
                            ins.then_inc(v_turn[n], 1)
                            ve.wait_ge(v_turn[n], i)
                            ins = nc.vector.tensor_tensor(full[n][:], full[n][:], turned[n][:], ALU.add)
                        ins.then_inc(full_ready[n], 1)
                    for n in range(NK):
                        ve.wait_ge(a_part1[n], i)
                        nc.vector.tensor_tensor(rest[n][:], full[n][:], part[n][:, 0], ALU.subtract
                                                ).then_inc(v_rest[n], 1)
                    for n in range(NK):
                        ve.wait_ge(a_part2[n], i)
                        nc.vector.tensor_tensor(part[n][:, 2], rest[n][:], part[n][:, 1], ALU.subtract
                                                ).then_inc(v_part3[n], 1)

            @block.gpsimd
            def _(g):
                with g.Fori(1, NG + 1) as i:
                    g.wait_ge(v_stat, i)
                    nc.gpsimd.tensor_tensor(rstd[:], var[:], prog.half_neg[0:T, :], ALU.pow).then_inc(g_rstd, 1)

            @block.scalar
            def _(act):
                with act.Fori(1, NG + 1) as i:
                    act.wait_ge(pe_xt, i)
                    act.wait_ge(xt_free, i)
                    nc.scalar.copy(xt[:, 0, :], bank[0][:, 0:GT]).then_inc(a_xt, 1)
                    for n in range(NK):
                        act.wait_ge(full_ready[n], i)
                        act.wait_ge(part_free[n], i)
                        nc.scalar.copy(part[n][:, 0], full[n][:]).then_inc(a_part1[n], 1)
                    for n in range(NK):
                        act.wait_ge(v_rest[n], i)
                        nc.scalar.copy(part[n][:, 1], rest[n][:]).then_inc(a_part2[n], 1)

            @block.tensor
            def _(pe):
                with pe.Fori(1, NG + 1) as i:
                    pe.wait_ge(v_norm, i)
                    for c in range(KD):
                        for j in range(G):
                            ins = nc.tensor.transpose(bank[c][:, j * T:(j + 1) * T], xh[:, j, c * P:(c + 1) * P],
                                                      prog.w("ident")[0:T, 0:T])
                    ins.then_inc(pe_xt, 1)
                    pe.wait_ge(a_xt, i)
                    pe.wait_ge(v_xt, i)
                    for n, (kind, _, _) in enumerate(KINDS):
                        for rot in range(2 if with_keys else 1):
                            weights = prog.w(f"{name}_w{kind}" + ("_rot" if rot else ""), KD)
                            for m in range(KD):
                                for k in range(KD):
                                    ins = nc.tensor.matmul(banks_of(n, rot, m), weights[:, k, m * P:(m + 1) * P],
                                                           xt[:, k, :], start=(k == 0), stop=(k == KD - 1))
                        ins.then_inc(pe_k[n], 1)


def stage_attention(prog, layer):
    nc = prog.nc
    name = ("x0", "s", "x1")[layer]
    masked = layer == 2
    NK = (S2, T, S2)[layer]
    x_dram, out_dram = prog.x[(1, 3, 4)[layer]], prog.x[(2, 4, 5)[layer]]
    v_src = prog.xn_t if layer == 1 else prog.ins["ctx_t"]
    NKT = -(-NK // P)
    size = -(-NK // NKT)
    KEYS = [(k * size, min(size, NK - k * size)) for k in range(NKT)]
    HB = min(512 // NK, 4)
    NU = H // (2 * HB)
    NQ = H // G
    NPU = NQ * NKT
    HH = H // 2
    at_unit = {-(-(u + 1) * NPU // NU) - 1: u for u in range(NU)}
    if NKT > 1:
        LAST_AV, SHIFT_B, ROWS, TURN, OUT, SHIFT_A = 1, 2, 3, 5, 7, 9
        av_at = {3 * g + 4: g for g in range(NQ - 1)}
    else:
        LAST_AV, SHIFT_B, ROWS, TURN, OUT, SHIFT_A = 0, 0, 1, 2, 3, 3
        av_at = {g + 1: g for g in range(NQ - 1)}

    with stage(nc, f"attn{layer}") as (sem, sbuf, psum):
        def pair(label):
            return [sem(f"{label}{s}") for s in range(2)]

        half_in = [pair(f"half_in{h}_") for h in range(2)]
        src_in, x_in, mask_in = pair("src_in"), pair("x_in"), pair("mask_in")
        g_base, g_mask = pair("g_base"), pair("g_mask")
        pe_score, v_max = pair("pe_score"), pair("v_max")
        v_split = [pair(f"v_split{h}_") for h in range(2)]
        pe_shift = [pair(f"pe_shift{h}_") for h in range(2)]
        v_shift = [pair(f"v_shift{h}_") for h in range(2)]
        g_shift = [pair(f"g_shift{h}_") for h in range(2)]
        pe_val, v_val = pair("pe_val"), pair("v_val")
        pe_prob, a_prob = pair("pe_prob"), pair("a_prob")
        pe_av = pair("pe_av")
        a_acc = pair("a_acc")
        pe_rows, v_rows, pe_turn, v_turn, pe_out, v_out = (
            pair(n) for n in ("pe_rows", "v_rows", "pe_turn", "v_turn", "pe_out", "v_out"))
        v_link = [pair(f"v_link{k}_") for k in range(6)]
        stored, out_free = pair("stored"), pair("out_free")
        consts_set = sem("consts_set")
        g_order = sem("g_order")

        q_sb = [sbuf(f"q{s}", [P, 2, HH, T], BF16) for s in range(2)]
        k_sb = [sbuf(f"k{s}", [P, 2, HH, NK], BF16) for s in range(2)]
        src = [sbuf(f"src{s}", [P, KD, NK]) for s in range(2)]
        xin = [sbuf(f"xin{s}", [T, D]) for s in range(2)]
        base = [sbuf(f"base{s}", [T, D]) for s in range(2)]
        xo = [sbuf(f"xo{s}", [T, D]) for s in range(2)]
        val = [sbuf(f"val{s}", [P, NKT, H, 2 * DH]) for s in range(2)]
        prob = sbuf("prob", [P, 2, NKT, GT])
        nmax = [sbuf(f"nmax{s}", [T, H]) for s in range(2)]
        split = [[sbuf(f"split{h}_{s}", [T, 2, H], BF16) for s in range(2)] for h in range(2)]
        shift = [sbuf(f"shift{h}", [P, T], BF16) for h in range(2)]
        acc = sbuf("acc", [P, GT])
        rden = sbuf("rden", [T, H])
        rows = sbuf("rows", [T, H, DH])
        turned = sbuf("turned", [P, KD, T])
        if masked:
            mask8 = [sbuf(f"mask8_{s}", [T, NK], U8) for s in range(2)]
            mask = [sbuf(f"mask{s}", [T, NK], BF16) for s in range(2)]
        ps_score = psum("ps_score", [P, 4, 512])
        ps_prob = [psum(f"ps_prob{k}", [P, 512]) for k in range(2)]
        ps_acc = psum("ps_acc", [P, 512])
        ps_misc = psum("ps_misc", [P, 512])
        ident, ident_b = prog.w("ident"), prog.c("ident_b")

        def seq(s, n):
            return n * 2 + (s - 2)

        def run(engine, head, step, tail):
            head(0, 1, None)
            step(0, 1, None, 1)
            with engine.Fori(1, 7) as i:
                step(1, i, i, i + 1)
                step(0, i + 1, i, i + 1)
            step(1, 7, 7, 8)
            step(0, 8, 7, 8)
            step(1, 8, 8, None)
            tail(1, 8)

        with nc.Block() as block:
            @block.sync
            def _(sp):
                def load_half(s, n, h):
                    b = seq(s, n)
                    for dst, stack in ((q_sb[s], prog.q_stack[layer]), (k_sb[s], prog.k_stack[layer])):
                        sp.dma_start(dst[0:SHIFT_ROW, h].rearrange("p h n -> p (h n)"),
                                     stack[bass.ds(b, 1), h].rearrange("b g (d h) n -> (b g d) (h n)", h=HH)
                                     ).then_inc(half_in[h][s], 16)

                def load_src(s, n):
                    sp.dma_start(src[s][:], v_src[bass.ds(seq(s, n), 1)].rearrange("b p k n -> p (b k) n")
                                 ).then_inc(src_in[s], 16)

                def load_x(s, n):
                    sp.dma_start(xin[s][:], x_dram[bass.ds(seq(s, n), 1)].rearrange("b t d -> t (b d)")
                                 ).then_inc(x_in[s], 16)

                def load_mask(s, n):
                    sp.dma_start(mask8[s][:], prog.ins["mask"][bass.ds(seq(s, n), 1)].rearrange("b t n -> t (b n)")
                                 ).then_inc(mask_in[s], 16)

                def store(s, n):
                    sp.wait_ge(v_out[s], n)
                    sp.dma_start(out_dram[bass.ds(seq(s, n), 1)].rearrange("b t d -> t (b d)"), xo[s][:]
                                 ).then_inc(stored[s], 16)
                    sp.wait_ge(stored[s], n * 16)
                    sp.sem_inc(out_free[s], 1)

                def step(s, n, n_prev, n_next, more=True):
                    if more:
                        if masked:
                            sp.wait_ge(g_mask[s], n)
                            load_mask(s, n + 1)
                        sp.wait_ge(pe_val[s], n)
                        load_src(s, n + 1)
                        sp.wait_ge(g_base[s], n)
                        load_x(s, n + 1)
                        sp.wait_ge(pe_prob[s], n * NPU - NPU // 2)
                        load_half(s, n + 1, 0)
                    if n_prev is not None:
                        store(1 - s, n_prev)
                    if more:
                        sp.wait_ge(pe_prob[s], n * NPU)
                        load_half(s, n + 1, 1)

                for s in range(2):
                    sp.sem_inc(out_free[s], 1)
                    load_half(s, 1, 0)
                    if masked:
                        load_mask(s, 1)
                    load_half(s, 1, 1)
                    load_src(s, 1)
                    load_x(s, 1)
                step(0, 1, None, 1)
                with sp.Fori(1, 7) as i:
                    step(1, i, i, i + 1)
                    step(0, i + 1, i, i + 1)
                step(1, 7, 7, 8)
                step(0, 8, 7, 8, more=False)
                step(1, 8, 8, None, more=False)
                store(1, 8)

            @block.tensor
            def _(pe):
                def score_unit(s, n, u, n_cur):
                    if u == 0 or u == NU // 2:
                        pe.wait_ge(half_in[2 * u // NU][s], n * 32)
                    if u == 0 and masked:
                        pe.wait_ge(g_mask[s], n)
                    if u >= 2:
                        pe.wait_ge(v_max[s], n * NU - NU + u - 1)
                    elif n_cur is not None:
                        pe.wait_ge(v_val[1 - s], n_cur)
                    for j in range(2):
                        for hh in range(HB):
                            h = (u * 2 + j) * HB + hh
                            out = ps_score[0:T, (u % 2) * 2 + j, hh * NK:(hh + 1) * NK]
                            if masked:
                                nc.tensor.matmul(out, prog.c("big_diag")[0:T, 0:T], mask[s][:], start=True, stop=False)
                            ins = nc.tensor.matmul(out, q_sb[s][0:SHIFT_ROW, h // HH, h % HH, :],
                                                   k_sb[s][0:SHIFT_ROW, h // HH, h % HH, :],
                                                   start=not masked, stop=True)
                    ins.then_inc(pe_score[s], 1)

                def values(s, n):
                    pe.wait_ge(src_in[s], n * 16)
                    pe.wait_ge(v_max[s], n * NU)
                    for t, (at, rows_) in enumerate(KEYS):
                        for k in range(KD):
                            ins = nc.tensor.matmul(ps_score[0:rows_, t, 0:D], src[s][:, k, at:at + rows_],
                                                   prog.w(f"{name}_wv", KD)[:, k, :], start=(k == 0), stop=(k == KD - 1))
                    ins.then_inc(pe_val[s], 1)

                def shift_rows(s, n, h):
                    pe.wait_ge(v_split[h][s], n)
                    nc.tensor.transpose(ps_misc[:].bitcast(BF16)[SHIFT_ROW:P, 0:T],
                                        split[h][s][:].rearrange("t a h -> t (a h)"), ident_b[0:T, 0:T]
                                        ).then_inc(pe_shift[h][s], 1)

                def prob_unit(s, n, k, n_prev):
                    q4, t = k // NKT, k % NKT
                    at, rows_ = KEYS[t]
                    if k % (NPU // 2) == 0:
                        pe.wait_ge(g_shift[2 * k // NPU][s], n)
                    if k >= 2:
                        pe.wait_ge(a_prob[s], n * NPU - NPU + k - 1)
                    elif n_prev is not None:
                        pe.wait_ge(a_prob[1 - s], n_prev * NPU + k - 1)
                    out = ps_prob[k % 2]
                    if masked:
                        nc.tensor.matmul(out[0:rows_, 0:GT], mask[s][:, at:at + rows_], prog.c("big_diag")[0:T, :],
                                         start=True, stop=False)
                    for j in range(G):
                        h = q4 * G + j
                        ins = nc.tensor.matmul(out[0:rows_, j * T:(j + 1) * T],
                                               k_sb[s][:, h // HH, h % HH, at:at + rows_],
                                               q_sb[s][:, h // HH, h % HH, :], start=not masked,
                                               stop=not masked or j == G - 1)
                    ins.then_inc(pe_prob[s], 1)

                def weigh_values(s, n, q4, n_prev):
                    pe.wait_ge(a_prob[s], n * NPU - NPU + (q4 + 1) * NKT)
                    if q4 == 0:
                        pe.wait_ge(v_val[s], n)
                        if n_prev is not None:
                            pe.wait_ge(a_acc[1 - s], n_prev)
                    for t, (_, rows_) in enumerate(KEYS):
                        for j in range(G):
                            ins = nc.tensor.matmul(ps_acc[32 * j:32 * j + 32, q4 * T:(q4 + 1) * T],
                                                   val[s][0:rows_, t, q4 * G + j, :],
                                                   prob[0:rows_, q4 % 2, t, j * T:(j + 1) * T],
                                                   start=(t == 0), stop=(t == NKT - 1))
                    ins.then_inc(pe_av[s], 1)

                def to_rows(s, n):
                    pe.wait_ge(a_acc[s], n)
                    for q4 in range(NQ):
                        ins = nc.tensor.transpose(ps_misc[0:T, q4 * P:(q4 + 1) * P], acc[:, q4 * T:(q4 + 1) * T], ident)
                    ins.then_inc(pe_rows[s], 1)

                def turn(s, n):
                    pe.wait_ge(v_rows[s], n)
                    for k in range(KD):
                        ins = nc.tensor.transpose(ps_misc[:, k * T:(k + 1) * T],
                                                  rows[:].rearrange("t h d -> t (h d)")[:, k * P:(k + 1) * P],
                                                  ident[0:T, 0:T])
                    ins.then_inc(pe_turn[s], 1)

                def project(s, n):
                    pe.wait_ge(v_turn[s], n)
                    for k in range(KD):
                        ins = nc.tensor.matmul(ps_misc[0:T, 0:D], turned[:, k, :], prog.w(f"{name}_wo", KD)[:, k, :],
                                               start=(k == 0), stop=(k == KD - 1))
                    ins.then_inc(pe_out[s], 1)

                def head(s, n, n_cur):
                    for u in range(NU):
                        score_unit(s, n, u, n_cur)
                    shift_rows(s, n, 0)
                    values(s, n)

                def step(s, n, n_prev, n_next):
                    for k in range(NPU):
                        prob_unit(s, n, k, n_prev)
                        if k == LAST_AV and n_prev is not None:
                            weigh_values(1 - s, n_prev, NQ - 1, None)
                        if k in av_at:
                            weigh_values(s, n, av_at[k], n_prev)
                        if k == SHIFT_B:
                            pe.wait_ge(v_shift[0][s], n)
                            shift_rows(s, n, 1)
                        if n_prev is not None:
                            if k == ROWS:
                                pe.wait_ge(v_shift[1][s], n)
                                to_rows(1 - s, n_prev)
                            if k == TURN:
                                turn(1 - s, n_prev)
                            if k == OUT:
                                project(1 - s, n_prev)
                        if n_next is not None:
                            if k in at_unit:
                                score_unit(1 - s, n_next, at_unit[k], n)
                            if k == SHIFT_A:
                                if n_prev is not None:
                                    pe.wait_ge(v_out[1 - s], n_prev)
                                else:
                                    pe.wait_ge(v_shift[1][s], n)
                                shift_rows(1 - s, n_next, 0)
                    if n_next is not None:
                        values(1 - s, n_next)

                def tail(s, n):
                    weigh_values(s, n, NQ - 1, None)
                    pe.wait_ge(v_out[1 - s], n)
                    to_rows(s, n)
                    turn(s, n)
                    project(s, n)

                pe.wait_ge(consts_set, 1)
                run(pe, head, step, tail)

            @block.scalar
            def _(act):
                def step(s, n, n_prev, n_next):
                    for k in range(NPU):
                        q4, t = k // NKT, k % NKT
                        rows_ = KEYS[t][1]
                        act.wait_ge(pe_prob[s], n * NPU - NPU + k + 1)
                        if t == 0:
                            if q4 >= 2:
                                act.wait_ge(pe_av[s], n * NQ - NQ + q4 - 1)
                            elif n_prev is not None:
                                act.wait_ge(pe_av[1 - s], n_prev * NQ + q4 - 1)
                        nc.scalar.activation(prob[0:rows_, q4 % 2, t, :], ps_prob[k % 2][0:rows_, 0:GT], ACT.Exp,
                                             scale=DH ** -0.5).then_inc(a_prob[s], 1)
                        if k == LAST_AV and n_prev is not None:
                            tail(1 - s, n_prev)

                def tail(s, n):
                    act.wait_ge(pe_av[s], n * NQ)
                    nc.scalar.copy(acc[:], ps_acc[:, 0:GT]).then_inc(a_acc[s], 1)

                run(act, lambda *a: None, step, tail)

            @block.vector
            def _(ve):
                def score_unit(s, n, u):
                    ve.wait_ge(pe_score[s], n * NU - NU + u + 1)
                    scores = ps_score[0:T, (u % 2) * 2:(u % 2) * 2 + 2, 0:HB * NK].rearrange("p b (h n) -> p b h n", h=HB)
                    nc.vector.tensor_reduce(nmax[s][:, u * 2 * HB:(u + 1) * 2 * HB].rearrange("p (b h) -> p b h", b=2),
                                            scores, AX.X, ALU.max, negate=True).then_inc(v_max[s], 1)
                    if (u + 1) % (NU // 2) == 0:
                        split_shift(s, n, (u + 1) * 2 // NU - 1)

                def split_shift(s, n, h):
                    here = nmax[s][:, h * HH:(h + 1) * HH]
                    ve.wait_ge(v_max[s], n * NU - NU + (h + 1) * NU // 2)
                    if masked:
                        nc.vector.tensor_scalar(here, here, -FLOOR, None, ALU.min).then_inc(v_link[h][s], 1)
                        ve.wait_ge(v_link[h][s], n)
                    nc.vector.tensor_copy(split[h][s][:, 0, h * HH:(h + 1) * HH], here).then_inc(v_link[2 + h][s], 1)
                    ve.wait_ge(v_link[2 + h][s], n)
                    nc.vector.tensor_tensor(split[h][s][:, 1, h * HH:(h + 1) * HH], here,
                                            split[h][s][:, 0, h * HH:(h + 1) * HH], ALU.subtract
                                            ).then_inc(v_split[h][s], 1)

                def shift_rows(s, n, h):
                    ve.wait_ge(pe_shift[h][s], n)
                    nc.vector.tensor_copy(shift[h][SHIFT_ROW:P, :], ps_misc[:].bitcast(BF16)[SHIFT_ROW:P, 0:T]
                                          ).then_inc(v_shift[h][s], 1)

                def values(s, n):
                    ve.wait_ge(pe_val[s], n)
                    for t, (_, rows_) in enumerate(KEYS):
                        ins = nc.vector.tensor_tensor(
                            val[s][0:rows_, t, :, 0:DH], ps_score[0:rows_, t, 0:D].rearrange("p (h d) -> p h d", h=H),
                            prog.w(f"{name}_bv_row")[0:rows_].rearrange("p (h d) -> p h d", h=H), ALU.add)
                    ins.then_inc(v_val[s], 1)

                def to_rows(s, n):
                    ve.wait_ge(pe_rows[s], n)
                    heads = ps_misc[0:T, :].rearrange("p (h d) -> p h d", h=H)
                    nc.vector.reciprocal(rden[:], heads[:, :, DH]).then_inc(v_link[4][s], 1)
                    ve.wait_ge(v_link[4][s], n)
                    nc.vector.tensor_tensor(rows[:], heads[:, :, 0:DH], rden[:].unsqueeze(2).broadcast_to([T, H, DH]),
                                            ALU.mult).then_inc(v_rows[s], 1)

                def turn(s, n):
                    ve.wait_ge(pe_turn[s], n)
                    nc.vector.tensor_copy(turned[:].rearrange("p k t -> p (k t)"), ps_misc[:, 0:KD * T]
                                          ).then_inc(v_turn[s], 1)

                def project(s, n):
                    ve.wait_ge(g_base[s], n)
                    ve.wait_ge(out_free[s], n)
                    ve.wait_ge(pe_out[s], n)
                    nc.vector.tensor_tensor(xo[s][:], ps_misc[0:T, 0:D], base[s][:], ALU.add).then_inc(v_out[s], 1)

                def head(s, n, _):
                    for u in range(NU):
                        score_unit(s, n, u)
                    shift_rows(s, n, 0)
                    values(s, n)

                def step(s, n, n_prev, n_next):
                    for k in range(NPU):
                        if k == SHIFT_B:
                            shift_rows(s, n, 1)
                        if n_prev is not None:
                            if k == ROWS:
                                to_rows(1 - s, n_prev)
                            if k == TURN:
                                turn(1 - s, n_prev)
                            if k == OUT:
                                project(1 - s, n_prev)
                        if n_next is not None:
                            if k in at_unit:
                                score_unit(1 - s, n_next, at_unit[k])
                            if k == SHIFT_A:
                                shift_rows(1 - s, n_next, 0)
                    if n_next is not None:
                        values(1 - s, n_next)

                def tail(s, n):
                    to_rows(s, n)
                    turn(s, n)
                    project(s, n)

                for s in range(2):
                    nc.vector.memset(val[s][:, :, :, DH:DH + 1], 1.0)
                    nc.vector.memset(val[s][:, :, :, DH + 1:], 0.0)
                    for h in range(2):
                        nc.vector.memset(split[h][s][:], 0.0)
                    ins = nc.vector.memset(k_sb[s][SHIFT_ROW:P], 1.0)
                ins.then_inc(consts_set, 1)
                ve.wait_ge(consts_set, 1)
                run(ve, head, step, tail)

            @block.gpsimd
            def _(g):
                def shift_rows(s, n, h, before):
                    g.wait_ge(*before)
                    g.wait_ge(v_shift[h][s], n)
                    nc.gpsimd.tensor_tensor(
                        q_sb[s][SHIFT_ROW:P, h], shift[h][SHIFT_ROW:P, :].unsqueeze(1).broadcast_to([32, HH, T]),
                        prog.c("head_sel")[SHIFT_ROW:P, h * HH:(h + 1) * HH].unsqueeze(2).broadcast_to([32, HH, T]),
                        ALU.mult).then_inc(g_shift[h][s], 1)

                def set_base(s, n, before):
                    if before is not None:
                        g.wait_ge(*before)
                    if not (isinstance(n, int) and n == 1):
                        g.wait_ge(v_out[s], n - 1)
                    g.wait_ge(x_in[s], n * 16)
                    nc.gpsimd.tensor_tensor(base[s][:], xin[s][:], prog.w(f"{name}_bo_row")[0:T], ALU.add
                                            ).then_inc(g_base[s], 1)

                def set_mask(s, n, n_prev, before):
                    if before is not None:
                        g.wait_ge(*before)
                    if n_prev is not None:
                        g.wait_ge(pe_prob[s], n_prev * NPU)
                    g.wait_ge(mask_in[s], n * 16)
                    g.sem_inc(g_order, 1)
                    nc.gpsimd.tensor_copy(mask[s][:], mask8[s][:]).then_inc(g_mask[s], 1)

                def head(s, n, _):
                    if masked:
                        set_mask(s, n, None, None)
                    set_base(s, n, (g_mask[s], n) if masked else None)
                    shift_rows(s, n, 0, (g_base[s], n))

                def step(s, n, n_prev, n_next):
                    masks = masked and n_next is not None
                    if masks:
                        set_mask(1 - s, n_next, n_prev, (g_shift[0][s], n))
                    shift_rows(s, n, 1, (g_mask[1 - s], n_next) if masks else (g_shift[0][s], n))
                    if n_next is not None:
                        set_base(1 - s, n_next, (g_shift[1][s], n))
                        shift_rows(1 - s, n_next, 0, (g_base[1 - s], n_next))

                run(g, head, step, lambda *a: None)


def stage_route0(prog):
    nc = prog.nc
    x_dram = prog.x[2]
    NM = HID // P
    NC_ = E0 + NGRP
    with stage(nc, "route0") as (sem, sbuf, psum):
        x_in, v_stat, g_rstd, v_norm = sem("x_in"), sem("v_stat"), sem("g_rstd"), sem("v_norm")
        v_link = [sem(f"v_link{k}") for k in range(30)]
        pe_xt, a_xt, v_xt = sem("pe_xt"), sem("a_xt"), sem("v_xt")
        v_square, g_length = sem("v_square"), sem("g_length")
        pe_logits, v_logits = sem("pe_logits"), sem("v_logits")
        v_gap, a_exp = sem("v_gap"), sem("a_exp")
        v_hot, pe_pos, v_apart, v_rows = sem("v_hot"), sem("pe_pos"), sem("v_apart"), sem("v_rows")
        pe_up = [sem(f"pe_up{m}") for m in range(NM)]
        a_up = [sem(f"a_up{m}") for m in range(NM)]
        v_up = [sem(f"v_up{m}") for m in range(NM)]
        pe_down, v_out = sem("pe_down"), sem("v_out")
        stored, buf_free, x_free = sem("stored"), sem("buf_free"), sem("x_free")
        zero_set, zeroed, ids_set = sem("zero_set"), sem("zeroed"), sem("ids_set")
        scattered, scatter_free, g_ready = sem("scattered"), sem("scatter_free"), sem("g_ready")

        xg = sbuf("xg", [T, G, D])
        stats = sbuf("stats", [T, G, 6])
        mv = sbuf("mv", [T, G, 2])
        var = sbuf("var", [T, G])
        rstd = sbuf("rstd", [T, G])
        xf = sbuf("xf", [T, G, D])
        sq = sbuf("sq", [T, D])
        xt = sbuf("xt", [P, KD, GT])
        length = sbuf("length", [T, 4, G])
        sc = sbuf("sc", [T, G, NC_])
        gtop = sbuf("gtop", [T, G, 8])
        gidx = sbuf("gidx", [T, G, 8], U32)
        gidf = sbuf("gidf", [T, G, 8])
        geq = sbuf("geq", [T, G, 4, NGRP])
        gsel = sbuf("gsel", [T, G, NGRP])
        gneg = sbuf("gneg", [T, G, NGRP])
        es = sbuf("es", [T, G, E0])
        etop = sbuf("etop", [T, G, 8])
        eidx = sbuf("eidx", [T, G, 8], U32)
        eidf = sbuf("eidf", [T, G, 8])
        gap = sbuf("gap", [T, G, TOPK])
        esum = sbuf("esum", [T, 2, G])
        gates = sbuf("gates", [T, G, TOPK])
        hot = sbuf("hot", [T, G, TOPK, E0])
        any_hot = sbuf("any_hot", [T, G, E0], BF16)
        prior = sbuf("prior", [T, E0], BF16)
        prior_add = sbuf("prior_add", [T, E0])
        prod = sbuf("prod", [T, G, TOPK, E0])
        pos = sbuf("pos", [T, G, TOPK])
        keep = sbuf("keep", [T, G, TOPK])
        rowf = sbuf("rowf", [T, 2, G, TOPK])
        row_get = sbuf("row_get", [T, G, TOPK], I32)
        row_put = sbuf("row_put", [T, G * TOPK], I32)
        spare = sbuf("spare", [T, G * TOPK])
        ids = sbuf("ids", [T, B], I32)
        ids_now = sbuf("ids_now", [T, G], I32)
        zeros = sbuf("zeros", [T, SLOTS0 // T], I32)
        act_ = sbuf("act_", [P, NM, GT])
        up = sbuf("up", [P, NM, GT])
        xo = sbuf("xo", [T, G, D])
        bank = [psum(f"bank{k}", [P, 512]) for k in range(8)]
        LEFT = [4, 6]

        with nc.Block() as block:
            @block.sync
            def _(sp):
                sp.wait_ge(zero_set, 1)
                sp.dma_start(prog.row_token[0][0:SLOTS0].rearrange("(p n) o -> p (n o)", p=T), zeros[:]).then_inc(zeroed, 16)
                sp.sem_inc(buf_free, 1)
                with sp.Fori(1, NG + 1) as i:
                    def group(dram):
                        return dram[bass.ds((i - 1) * G, G)].rearrange("g t d -> t g d")

                    sp.wait_ge(x_free, i)
                    sp.dma_start(xg[:], group(x_dram)).then_inc(x_in, 16)
                    sp.wait_ge(v_norm, i)
                    sp.dma_start(group(prog.ln_rows[0].rearrange("(b t) d -> b t d", t=T)), xf[:]).then_inc(stored, 16)
                    sp.wait_ge(v_rows, i)
                    sp.dma_start(group(prog.choice_row), row_get[:]).then_inc(stored, 16)
                    sp.dma_start(group(prog.choice_gate), gates[:]).then_inc(stored, 16)
                    sp.wait_ge(v_out, i)
                    sp.dma_start(group(prog.x_shared), xo[:]).then_inc(stored, 16)
                    sp.wait_ge(stored, i * 64)
                    sp.sem_inc(buf_free, 1)

            @block.gpsimd
            def _(g):
                g.wait_ge(zeroed, 16)
                with g.Fori(1, NG + 1) as i:
                    g.wait_ge(v_stat, i)
                    nc.gpsimd.tensor_tensor(rstd[:], var[:], prog.half_neg[0:T, :], ALU.pow).then_inc(g_rstd, 1)
                    g.wait_ge(v_square, i)
                    nc.gpsimd.tensor_tensor(length[:, 1, :], length[:, 0, :], length[:, 3, :], ALU.pow
                                            ).then_inc(g_length, 1)
                    g.wait_ge(v_rows, i)
                    g.sem_inc(g_ready, 1)
                    for c in range(G * TOPK):
                        g.indirect_dma_start(prog.row_token[0], bass.IndirectOffsetOnAxis(row_put[:, c:c + 1], 0),
                                             ids_now[:, c // TOPK:c // TOPK + 1], None).then_inc(scattered, 16)
                    g.wait_ge(scattered, i * (16 * G * TOPK))
                    g.sem_inc(scatter_free, 1)

            @block.vector
            def _(ve):
                nc.vector.memset(zeros[:], 0).then_inc(zero_set, 1)
                nc.vector.memset(length[:, 3, :], 0.5)
                nc.vector.memset(prior[:], 0.0)
                nc.vector.tensor_copy(ids[:], prog.w("tok_id")[0:T]).then_inc(ids_set, 1)
                ve.sem_inc(x_free, 1)
                ve.sem_inc(scatter_free, 1)
                ve.wait_ge(ids_set, 1)
                with ve.Fori(1, NG + 1) as i:
                    used = [0]

                    def link(ins):
                        ins.then_inc(v_link[used[0]], 1)
                        ve.wait_ge(v_link[used[0]], i)
                        used[0] += 1

                    def link_apart(ins):
                        link(ins)
                        ve.sem_inc(v_apart, 1)

                    ve.wait_ge(x_in, i * 16)
                    ve.wait_ge(buf_free, i)
                    for j in range(G):
                        ins = nc.vector.bn_stats(stats[:, j, :], xg[:, j, :])
                    link_apart(ins)
                    for j in range(G):
                        ins = nc.vector.bn_aggr(mv[:, j, :], stats[:, j, :])
                    link(ins)
                    nc.vector.tensor_scalar(var[:], mv[:, :, 1], EPS, None, ALU.add).then_inc(v_stat, 1)
                    ve.wait_ge(g_rstd, i)
                    for j in range(G):
                        ins = nc.vector.tensor_scalar(xf[:, j, :], xg[:, j, :], mv[:, j, 0:1], rstd[:, j:j + 1],
                                                      ALU.subtract, ALU.mult)
                    ins.then_inc(v_norm, 1)
                    ve.wait_ge(v_norm, i)
                    for j in range(G):
                        link(nc.vector.tensor_tensor_reduce(sq[:], xf[:, j, :], xf[:, j, :], 1.0, 0.0, ALU.mult,
                                                            ALU.add, length[:, 0, j:j + 1]))
                    ve.sem_inc(v_square, 1)
                    ve.wait_ge(pe_xt, i)
                    nc.vector.tensor_copy(xt[:, 1, :], bank[1][:, 0:GT]).then_inc(v_xt, 1)
                    ve.wait_ge(g_length, i)
                    link(nc.vector.tensor_scalar(length[:, 2, :], length[:, 1, :], 1e-12, None, ALU.max))
                    link(nc.vector.reciprocal(length[:, 0, :], length[:, 2, :]))
                    ve.wait_ge(pe_logits, i)
                    link_apart(nc.vector.tensor_tensor(sc[:], bank[2][0:T, 0:G * NC_].rearrange("p (g c) -> p g c", g=G),
                                                 length[:, 0, :].unsqueeze(2).broadcast_to([T, G, NC_]), ALU.mult))
                    for j in range(G):
                        ins = nc.vector.max(gtop[:, j, :], sc[:, j, E0:NC_])
                    link_apart(ins)
                    for j in range(G):
                        ins = nc.vector.max_index(gidx[:, j, :], gtop[:, j, :], sc[:, j, E0:NC_])
                    link(nc.vector.tensor_tensor(
                        es[:], sc[:, :, 0:E0], prog.w("f0_bias_row")[0:T].unsqueeze(1).broadcast_to([T, G, E0]), ALU.add))
                    link(nc.vector.tensor_copy(gidf[:], gidx[:]))
                    link(nc.vector.tensor_tensor(
                        geq[:], prog.w("iota_e")[0:T, 0:NGRP].unsqueeze(1).unsqueeze(1).broadcast_to([T, G, 4, NGRP]),
                        gidf[:, :, 0:4].unsqueeze(3).broadcast_to([T, G, 4, NGRP]), ALU.is_equal))
                    link(nc.vector.tensor_reduce(gsel[:], geq[:].rearrange("p g k n -> p g n k"), AX.X, ALU.add))
                    per_group = "p g (n e) -> p (g n) e"
                    nc.vector.tensor_scalar(gneg[:], gsel[:], 1e9, -1e9, ALU.mult, ALU.add)
                    link(nc.vector.tensor_tensor(
                        es[:].rearrange(per_group, n=NGRP), es[:].rearrange(per_group, n=NGRP),
                        gsel[:].rearrange("p g n -> p (g n)").unsqueeze(2).broadcast_to([T, G * NGRP, E0 // NGRP]),
                        ALU.mult))
                    link_apart(nc.vector.tensor_tensor(
                        es[:].rearrange(per_group, n=NGRP), es[:].rearrange(per_group, n=NGRP),
                        gneg[:].rearrange("p g n -> p (g n)").unsqueeze(2).broadcast_to([T, G * NGRP, E0 // NGRP]),
                        ALU.add))
                    for j in range(G):
                        ins = nc.vector.max(etop[:, j, :], es[:, j, :])
                    link_apart(ins)
                    for j in range(G):
                        ins = nc.vector.max_index(eidx[:, j, :], etop[:, j, :], es[:, j, :])
                    link(ins)
                    nc.vector.tensor_tensor(gap[:], etop[:, :, 0:TOPK],
                                            etop[:, :, 0:1].broadcast_to([T, G, TOPK]), ALU.subtract).then_inc(v_gap, 1)
                    link(nc.vector.tensor_copy(eidf[:], eidx[:]))
                    link(nc.vector.tensor_tensor(
                        hot[:], prog.w("iota_e")[0:T].unsqueeze(1).unsqueeze(1).broadcast_to([T, G, TOPK, E0]),
                        eidf[:, :, 0:TOPK].unsqueeze(3).broadcast_to([T, G, TOPK, E0]), ALU.is_equal))
                    with nc.allow_low_precision("sums of a few ones are exact in bfloat16"):
                        nc.vector.tensor_reduce(any_hot[:], hot[:].rearrange("p g k e -> p g e k"), AX.X, ALU.add
                                                ).then_inc(v_hot, 1)
                    ve.wait_ge(a_exp, i)
                    link(nc.vector.tensor_reduce(esum[:, 0, :], gates[:], AX.X, ALU.add))
                    link(nc.vector.reciprocal(esum[:, 1, :], esum[:, 0, :]))
                    link(nc.vector.tensor_tensor(gates[:], gates[:],
                                                 esum[:, 1, :].unsqueeze(2).broadcast_to([T, G, TOPK]), ALU.mult))
                    ve.wait_ge(pe_pos, i)
                    nc.vector.tensor_reduce(prior_add[:], any_hot[:].rearrange("p g e -> p e g"), AX.X, ALU.add)
                    link(nc.vector.tensor_tensor(
                        prod[:], hot[:],
                        bank[3][0:T, 0:G * E0].rearrange("p (g e) -> p g e", g=G).unsqueeze(2)
                        .broadcast_to([T, G, TOPK, E0]), ALU.mult))
                    nc.vector.tensor_tensor(prior[:], prior[:], prior_add[:], ALU.add)
                    link(nc.vector.tensor_reduce(pos[:], prod[:], AX.X, ALU.add))
                    nc.vector.tensor_scalar(keep[:], pos[:], float(CAP), None, ALU.is_lt)
                    link(nc.vector.tensor_scalar(pos[:], pos[:], float(CAP - 1), None, ALU.min))
                    link(nc.vector.scalar_tensor_tensor(rowf[:, 0], eidf[:, :, 0:TOPK], float(CAP), pos[:],
                                                        ALU.mult, ALU.add))
                    ve.wait_ge(scatter_free, i)
                    nc.vector.tensor_tensor(gates[:], gates[:], keep[:], ALU.mult)
                    nc.vector.tensor_copy(row_get[:], rowf[:, 0])
                    nc.vector.tensor_copy(ids_now[:], ids[:, bass.ds((i - 1) * G, G)])
                    link(nc.vector.tensor_copy(spare[:], prog.w("spare_row")[0:T, bass.ds((i - 1) * (G * TOPK), G * TOPK)]))
                    flat = "p g k -> p (g k)"
                    link(nc.vector.tensor_tensor(rowf[:, 1], rowf[:, 0], spare[:].rearrange("p (g k) -> p g k", g=G),
                                                 ALU.subtract))
                    link(nc.vector.tensor_tensor(rowf[:, 1], rowf[:, 1], keep[:], ALU.mult))
                    nc.vector.tensor_tensor(row_put[:], rowf[:, 1].rearrange(flat), spare[:], ALU.add).then_inc(v_rows, 1)
                    for m in range(NM):
                        ve.wait_ge(a_up[m], i)
                        nc.vector.tensor_tensor(up[:, m, :], act_[:, m, :], bank[LEFT[m % 2] + 1][:, 0:GT], ALU.mult
                                                ).then_inc(v_up[m], 1)
                    ve.wait_ge(pe_down, i)
                    for h in range(2):
                        ins = nc.vector.tensor_tensor(
                            xo[:, 2 * h:2 * h + 2, :], bank[h][0:T, :].rearrange("p (g d) -> p g d", g=2),
                            xg[:, 2 * h:2 * h + 2, :], ALU.add)
                    ins.then_inc(v_out, 1)
                    ve.wait_ge(v_out, i)
                    ve.sem_inc(x_free, 1)

            @block.scalar
            def _(act):
                with act.Fori(1, NG + 1) as i:
                    act.wait_ge(pe_xt, i)
                    nc.scalar.copy(xt[:, 0, :], bank[0][:, 0:GT]).then_inc(a_xt, 1)
                    act.wait_ge(v_gap, i)
                    nc.scalar.activation(gates[:], gap[:], ACT.Exp).then_inc(a_exp, 1)
                    for m in range(NM):
                        act.wait_ge(pe_up[m], i)
                        nc.scalar.activation(act_[:, m, :], bank[LEFT[m % 2]][:, 0:GT], ACT.Silu).then_inc(a_up[m], 1)

            @block.tensor
            def _(pe):
                with pe.Fori(1, NG + 1) as i:
                    pe.wait_ge(v_norm, i)
                    for c in range(KD):
                        for j in range(G):
                            ins = nc.tensor.transpose(bank[c][:, j * T:(j + 1) * T], xf[:, j, c * P:(c + 1) * P],
                                                      prog.w("ident")[0:T, 0:T])
                    ins.then_inc(pe_xt, 1)
                    pe.wait_ge(a_xt, i)
                    pe.wait_ge(v_xt, i)
                    for j in range(G):
                        for k in range(KD):
                            ins = nc.tensor.matmul(bank[2][0:T, j * NC_:(j + 1) * NC_], xt[:, k, j * T:(j + 1) * T],
                                                   prog.cent_t[:, k, :], start=(k == 0), stop=(k == KD - 1))
                    ins.then_inc(pe_logits, 1)
                    for m in range(NM):
                        if m >= 2:
                            pe.wait_ge(v_up[m - 2], i)
                        for side, name in enumerate(("f0_sg", "f0_su")):
                            for k in range(KD):
                                ins = nc.tensor.matmul(bank[LEFT[m % 2] + side][:, 0:GT],
                                                       prog.w(name, KD)[:, k, m * P:(m + 1) * P], xt[:, k, :],
                                                       start=(k == 0), stop=(k == KD - 1))
                        ins.then_inc(pe_up[m], 1)
                        if m == 1:
                            pe.wait_ge(v_hot, i)
                            for j in range(G):
                                out = bank[3][0:T, j * E0:(j + 1) * E0]
                                nc.tensor.matmul(out, prog.c("before")[0:T, :], any_hot[:, j, :], start=True, stop=False)
                                for before in range(j):
                                    nc.tensor.matmul(out, prog.c("ones_b")[0:T, :], any_hot[:, before, :],
                                                     start=False, stop=False)
                                ins = nc.tensor.matmul(out, prog.c("ones_b")[0:T, :], prior[:], start=False, stop=True)
                            ins.then_inc(pe_pos, 1)
                    for j in range(G):
                        for m in range(NM):
                            if j == 0:
                                pe.wait_ge(v_up[m], i)
                            ins = nc.tensor.matmul(bank[j // 2][0:T, (j % 2) * D:(j % 2 + 1) * D],
                                                   up[:, m, j * T:(j + 1) * T], prog.w("f0_sd", NM)[:, m, :],
                                                   start=(m == 0), stop=(m == NM - 1))
                    ins.then_inc(pe_down, 1)


def stage_experts0(prog):
    nc = prog.nc
    NM = HID // P
    HALF = CAP // 2
    ROUNDS = E0 // 2
    with stage(nc, "experts0") as (sem, sbuf, psum):
        def pair(label):
            return [sem(f"{label}{s}") for s in range(2)]

        ids_in, v_idf, pe_id, v_id = sem("ids_in"), sem("v_idf"), sem("pe_id"), sem("v_id")
        g_order = sem("g_order")
        w_in = [pair(f"w_in{k}_") for k in range(3)]
        v_now = pair("v_now")
        rows_in, pe_xt, v_xt = pair("rows_in"), pair("pe_xt"), pair("v_xt")
        pe_up = [pair(f"pe_up{m}_") for m in range(NM)]
        a_up = [pair(f"a_up{m}_") for m in range(NM)]
        v_up = [pair(f"v_up{m}_") for m in range(NM)]
        pe_down, a_out, stored = pair("pe_down"), pair("a_out"), pair("stored")

        ids = sbuf("ids", [2 * E0, HALF], I32)
        idf = sbuf("idf", [2 * E0, HALF])
        token = sbuf("token", [HALF, 2 * E0 + 4], I32)
        now = [sbuf(f"now{s}", [HALF, 2], I32) for s in range(2)]
        wg = [sbuf(f"wg{s}", [P, KD, HID]) for s in range(2)]
        wu = [sbuf(f"wu{s}", [P, KD, HID]) for s in range(2)]
        wd = [sbuf(f"wd{s}", [P, NM, D]) for s in range(2)]
        xe = [sbuf(f"xe{s}", [HALF, 2, D]) for s in range(2)]
        xt = [sbuf(f"xt{s}", [P, KD, CAP]) for s in range(2)]
        act_ = sbuf("act_", [P, 2, CAP])
        up = [sbuf(f"up{s}", [P, NM, CAP]) for s in range(2)]
        ye = [sbuf(f"ye{s}", [HALF, 2, D]) for s in range(2)]
        ps_xt = psum("ps_xt", [P, 512])
        ps_id = psum("ps_id", [P, 512])
        ps_up = [psum(f"ps_up{k}", [P, 2, 256]) for k in range(NM)]
        ps_out = psum("ps_out", [P, 2, D])

        def earlier(engine, semaphore, n, per=1):
            if not (isinstance(n, int) and n == 1):
                engine.wait_ge(semaphore, n * per - per)

        def run(engine, body):
            body(1, False)
            with engine.Fori(2, ROUNDS) as i:
                body(i, False)
            body(ROUNDS, True)

        with nc.Block() as block:
            @block.sync
            def _(sp):
                sp.dma_start(ids[:], prog.row_token[0][0:SLOTS0].rearrange("(c p) o -> c (p o)", p=HALF)
                             ).then_inc(ids_in, 16)

                def body(n, last):
                    for s in range(2):
                        e = n * 2 + (s - 2)
                        earlier(sp, pe_up[NM - 1][s], n)
                        for k, (dst, name) in enumerate(((wg, "wg"), (wu, "wu"))):
                            sp.dma_start(dst[s][:], prog.ins[name][bass.ds(e, 1)].rearrange("e p k h -> p (e k) h")
                                         ).then_inc(w_in[k][s], 16)
                        earlier(sp, pe_down[s], n)
                        sp.dma_start(wd[s][:], prog.ins["wd"][bass.ds(e, 1)].rearrange("e p k h -> p (e k) h")
                                     ).then_inc(w_in[2][s], 16)

                run(sp, body)

            @block.gpsimd
            def _(g):
                with g.Fori(1, ROUNDS + 1) as i:
                    for s in range(2):
                        g.wait_ge(v_now[s], i)
                        g.sem_inc(g_order, 1)
                        for t in range(2):
                            g.indirect_dma_start(xe[s][:, t, :], None, prog.ln_rows[0],
                                                 bass.IndirectOffsetOnAxis(now[s][:, t:t + 1], 0)).then_inc(rows_in[s], 16)

            @block.tensor
            def _(pe):
                def turn(s, n):
                    pe.wait_ge(rows_in[s], n * 32)
                    if s == 1:
                        pe.wait_ge(v_xt[0], n)
                    else:
                        earlier(pe, v_xt[1], n)
                    for c in range(KD):
                        for t in range(2):
                            ins = nc.tensor.transpose(ps_xt[:, c * CAP + t * HALF:c * CAP + (t + 1) * HALF],
                                                      xe[s][:, t, c * P:(c + 1) * P], prog.w("ident")[0:HALF, 0:HALF])
                    ins.then_inc(pe_xt[s], 1)

                def half(s, n, last):
                    pe.wait_ge(v_xt[s], n)
                    for k in range(2):
                        pe.wait_ge(w_in[k][s], n * 16)
                    for m in range(NM):
                        if s == 1:
                            pe.wait_ge(v_up[m][0], n)
                        else:
                            earlier(pe, v_up[m][1], n)
                        for side, w in enumerate((wg, wu)):
                            for k in range(KD):
                                ins = nc.tensor.matmul(ps_up[m][:, side, 0:CAP], w[s][:, k, m * P:(m + 1) * P],
                                                       xt[s][:, k, :], start=(k == 0), stop=(k == KD - 1))
                        ins.then_inc(pe_up[m][s], 1)
                    if not last:
                        turn(1 - s, n + s)
                    pe.wait_ge(w_in[2][s], n * 16)
                    if s == 1:
                        pe.wait_ge(a_out[0], n)
                    else:
                        earlier(pe, a_out[1], n)
                    for m in range(NM):
                        pe.wait_ge(v_up[m][s], n)
                    for t in range(2):
                        for m in range(NM):
                            ins = nc.tensor.matmul(ps_out[0:HALF, t, :], up[s][:, m, t * HALF:(t + 1) * HALF],
                                                   wd[s][:, m, :], start=(m == 0), stop=(m == NM - 1))
                    ins.then_inc(pe_down[s], 1)

                pe.wait_ge(v_idf, 1)
                nc.tensor.transpose(ps_id[0:HALF, 0:2 * E0], idf[:], prog.w("ident")[0:2 * E0, 0:2 * E0]
                                    ).then_inc(pe_id, 1)
                turn(0, 1)

                def body(n, last):
                    half(0, n, False)
                    half(1, n, last)

                run(pe, body)

            @block.scalar
            def _(act):
                def body(n, last):
                    for s in range(2):
                        for m in range(NM):
                            if m >= 2:
                                act.wait_ge(v_up[m - 2][s], n)
                            elif s == 1:
                                act.wait_ge(v_up[m + 2][0], n)
                            else:
                                earlier(act, v_up[m + 2][1], n)
                            act.wait_ge(pe_up[m][s], n)
                            nc.scalar.activation(act_[:, m % 2, :], ps_up[m][:, 0, 0:CAP], ACT.Silu
                                                 ).then_inc(a_up[m][s], 1)
                        earlier(act, stored[s], n, 16)
                        act.wait_ge(pe_down[s], n)
                        nc.scalar.copy(ye[s][:], ps_out[0:HALF]).then_inc(a_out[s], 1)
                        act.wait_ge(a_out[s], n)
                        e = n * 2 + (s - 2)
                        act.dma_start(prog.expert_out[0].rearrange("(e t p) d -> e p t d", t=2, p=HALF)[bass.ds(e, 1)]
                                      .rearrange("e p t d -> p (e t) d"), ye[s][:]).then_inc(stored[s], 16)

                run(act, body)
                for s in range(2):
                    act.wait_ge(stored[s], ROUNDS * 16)

            @block.vector
            def _(ve):
                nc.vector.memset(token[:], 0)
                ve.wait_ge(ids_in, 16)
                nc.vector.tensor_copy(idf[:], ids[:]).then_inc(v_idf, 1)
                ve.wait_ge(v_idf, 1)
                ve.wait_ge(pe_id, 1)
                nc.vector.tensor_copy(token[:, 0:2 * E0], ps_id[0:HALF, 0:2 * E0]).then_inc(v_id, 1)
                ve.wait_ge(v_id, 1)
                for s in range(2):
                    nc.vector.tensor_copy(now[s][:], token[:, 2 * s:2 * s + 2]).then_inc(v_now[s], 1)

                def turn(s, n):
                    ve.wait_ge(pe_xt[s], n)
                    nc.vector.tensor_copy(xt[s][:], ps_xt[:, 0:KD * CAP].rearrange("p (k c) -> p k c", k=KD)
                                          ).then_inc(v_xt[s], 1)
                    nc.vector.tensor_copy(now[s][:], token[:, bass.ds(n * 4 + 2 * s, 2)]).then_inc(v_now[s], 1)

                def body(n, last):
                    for s in range(2):
                        for m in range(NM):
                            ve.wait_ge(a_up[m][s], n)
                            if m == 0:
                                earlier(ve, pe_down[s], n)
                            nc.vector.tensor_tensor(up[s][:, m, :], act_[:, m % 2, :], ps_up[m][:, 1, 0:CAP], ALU.mult
                                                    ).then_inc(v_up[m][s], 1)
                        if not (last and s == 1):
                            turn(1 - s, n + s)

                turn(0, 1)
                run(ve, body)


def stage_combine0(prog):
    nc = prog.nc
    with stage(nc, "combine0") as (sem, sbuf, psum):
        def pair(label):
            return [sem(f"{label}{s}") for s in range(2)]

        idx_in, x_in, got_in, v_out, stored = (pair(n) for n in ("idx_in", "x_in", "got_in", "v_out", "stored"))
        v_add = [pair(f"v_add{k}_") for k in range(TOPK)]
        v_free, out_free, g_order = pair("v_free"), pair("out_free"), sem("g_order")
        idx = [sbuf(f"idx{s}", [T, G, TOPK], I32) for s in range(2)]
        gate = [sbuf(f"gate{s}", [T, G, TOPK]) for s in range(2)]
        got = [sbuf(f"got{s}", [T, G, TOPK, D]) for s in range(2)]
        acc = [sbuf(f"acc{s}", [T, G, D]) for s in range(2)]
        ROUNDS = NG // 2

        with nc.Block() as block:
            @block.sync
            def _(sp):
                with sp.Fori(1, ROUNDS + 1) as i:
                    def group(dram, s):
                        return dram[bass.ds(i * (2 * G) + (s - 2) * G, G)].rearrange("g t d -> t g d")

                    for s in range(2):
                        sp.wait_ge(v_free[s], i)
                        sp.dma_start(idx[s][:], group(prog.choice_row, s)).then_inc(idx_in[s], 16)
                        sp.dma_start(gate[s][:], group(prog.choice_gate, s)).then_inc(x_in[s], 16)
                        sp.dma_start(acc[s][:], group(prog.x_shared, s)).then_inc(x_in[s], 16)
                    for s in range(2):
                        sp.wait_ge(v_out[s], i)
                        sp.dma_start(group(prog.x[3], s), acc[s][:]).then_inc(stored[s], 16)
                    for s in range(2):
                        sp.wait_ge(stored[s], i * 16)
                        sp.sem_inc(v_free[s], 1)

            @block.gpsimd
            def _(g):
                with g.Fori(1, ROUNDS + 1) as i:
                    for s in range(2):
                        g.wait_ge(idx_in[s], i * 16)
                        g.sem_inc(g_order, 1)
                        for c in range(G * TOPK):
                            g.indirect_dma_start(got[s][:, c // TOPK, c % TOPK, :], None, prog.expert_out[0],
                                                 bass.IndirectOffsetOnAxis(idx[s][:, c // TOPK, c % TOPK:c % TOPK + 1], 0)
                                                 ).then_inc(got_in[s], 16)

            @block.vector
            def _(ve):
                for s in range(2):
                    ve.sem_inc(v_free[s], 1)
                with ve.Fori(1, ROUNDS + 1) as i:
                    for s in range(2):
                        ve.wait_ge(x_in[s], i * 32)
                        ve.wait_ge(got_in[s], i * (16 * G * TOPK))
                        for k in range(TOPK):
                            for j in range(G):
                                ins = nc.vector.scalar_tensor_tensor(acc[s][:, j, :], got[s][:, j, k, :],
                                                                     gate[s][:, j, k:k + 1], acc[s][:, j, :],
                                                                     ALU.mult, ALU.add)
                            ins.then_inc(v_add[k][s], 1)
                            ve.wait_ge(v_add[k][s], i)
                        ve.sem_inc(v_out[s], 1)


def stage_route1(prog):
    nc = prog.nc
    x_dram = prog.x[5]
    with stage(nc, "route1") as (sem, sbuf, psum):
        x_in, v_stat, g_rstd, v_norm = sem("x_in"), sem("v_stat"), sem("g_rstd"), sem("v_norm")
        v_link = [sem(f"v_link{k}") for k in range(7)]
        v_apart, v_count = sem("v_apart"), sem("v_count")
        pe_xt, a_xt, v_xt, pe_logits = sem("pe_xt"), sem("a_xt"), sem("v_xt"), sem("pe_logits")
        buf_free, stored, v_hot, v_bf = sem("buf_free"), sem("stored"), sem("v_hot"), sem("v_bf")
        pe_count, zero_set, zeroed, scattered = sem("pe_count"), sem("zero_set"), sem("zeroed"), sem("scattered")

        xg = sbuf("xg", [T, G, D])
        stats = sbuf("stats", [T, G, 6])
        mv = sbuf("mv", [T, G, 2])
        var = sbuf("var", [T, G])
        rstd = sbuf("rstd", [T, G])
        xf = sbuf("xf", [T, G, D])
        xt = sbuf("xt", [P, KD, GT])
        logits = sbuf("logits", [T, G, E1])
        top = sbuf("top", [T, G, 8])
        arg = sbuf("arg", [T, G, 8], U32)
        argf = sbuf("argf", [T, G, 8])
        hot = sbuf("hot", [T, B, E1])
        hot_b = sbuf("hot_b", [T, B, E1], BF16)
        upto = sbuf("upto", [T, E1, B])
        start = sbuf("start", [T, E1, B])
        full = sbuf("full", [T, E1, MAX_E1_TILES])
        tiles = sbuf("tiles", [T, E1])
        ends = sbuf("ends", [T, E1])
        ones = sbuf("ones", [T, E1])
        first = sbuf("first", [T, E1])
        rank = sbuf("rank", [T, B, E1])
        rowf = sbuf("rowf", [T, B])
        past = sbuf("past", [T, TILES1, E1])
        tile_f = sbuf("tile_f", [T, TILES1])
        ids = sbuf("ids", [T, B], I32)
        zeros = sbuf("zeros", [P, TILES1 * E1_ROWS // P], I32)
        bank = [psum(f"bank{k}", [P, 512]) for k in range(4)]

        with nc.Block() as block:
            @block.sync
            def _(sp):
                sp.wait_ge(zero_set, 1)
                sp.dma_start(prog.row_token[1].rearrange("(p n) o -> p (n o)", p=P), zeros[:]).then_inc(zeroed, 16)
                sp.sem_inc(buf_free, 1)
                with sp.Fori(1, NG + 1) as i:
                    def group(dram):
                        return dram[bass.ds((i - 1) * G, G)].rearrange("g t d -> t g d")

                    sp.wait_ge(buf_free, i)
                    sp.dma_start(xg[:], group(x_dram)).then_inc(x_in, 16)
                    sp.wait_ge(v_norm, i)
                    sp.dma_start(group(prog.ln_rows[1].rearrange("(b t) d -> b t d", t=T)), xf[:]).then_inc(stored, 16)
                    sp.wait_ge(stored, i * 16)
                    sp.sem_inc(buf_free, 1)

            @block.gpsimd
            def _(g):
                with g.Fori(1, NG + 1) as i:
                    g.wait_ge(v_stat, i)
                    nc.gpsimd.tensor_tensor(rstd[:], var[:], prog.half_neg[0:T, :], ALU.pow).then_inc(g_rstd, 1)
                g.wait_ge(zeroed, 16)
                g.wait_ge(v_count, prog.route1_rows)
                for b in range(B):
                    g.indirect_dma_start(prog.row_token[1], bass.IndirectOffsetOnAxis(prog.row1[:, b:b + 1], 0),
                                         ids[:, b:b + 1], None).then_inc(scattered, 16)
                g.wait_ge(scattered, B * 16)

            @block.scalar
            def _(act):
                with act.Fori(1, NG + 1) as i:
                    act.wait_ge(pe_xt, i)
                    nc.scalar.copy(xt[:, 0, :], bank[0][:, 0:GT]).then_inc(a_xt, 1)

            @block.tensor
            def _(pe):
                with pe.Fori(1, NG + 1) as i:
                    pe.wait_ge(v_norm, i)
                    for c in range(KD):
                        for j in range(G):
                            ins = nc.tensor.transpose(bank[c][:, j * T:(j + 1) * T], xf[:, j, c * P:(c + 1) * P],
                                                      prog.w("ident")[0:T, 0:T])
                    ins.then_inc(pe_xt, 1)
                    pe.wait_ge(a_xt, i)
                    pe.wait_ge(v_xt, i)
                    for j in range(G):
                        for k in range(KD):
                            ins = nc.tensor.matmul(bank[2][0:T, j * E1:(j + 1) * E1], xt[:, k, j * T:(j + 1) * T],
                                                   prog.w("f1_gate_w", KD)[:, k, :], start=(k == 0), stop=(k == KD - 1))
                    ins.then_inc(pe_logits, 1)
                pe.wait_ge(v_bf, 1)
                for at, name in enumerate(("ones_b", "before")):
                    ins = nc.tensor.matmul(bank[3][0:T, at * B * E1:(at + 1) * B * E1], prog.c(name)[0:T, :],
                                           hot_b[:].rearrange("t b e -> t (b e)"), start=True, stop=True)
                ins.then_inc(pe_count, 1)

            @block.vector
            def _(ve):
                nc.vector.memset(zeros[:], 0).then_inc(zero_set, 1)
                nc.vector.memset(ones[:], 1.0)
                nc.vector.tensor_copy(ids[:], prog.w("tok_id")[0:T])
                with ve.Fori(1, NG + 1) as i:
                    used = [0]

                    def link(ins, apart=False):
                        ins.then_inc(v_link[used[0]], 1)
                        ve.wait_ge(v_link[used[0]], i)
                        used[0] += 1
                        if apart:
                            ve.sem_inc(v_apart, 1)

                    ve.wait_ge(x_in, i * 16)
                    for j in range(G):
                        ins = nc.vector.bn_stats(stats[:, j, :], xg[:, j, :])
                    link(ins, apart=True)
                    for j in range(G):
                        ins = nc.vector.bn_aggr(mv[:, j, :], stats[:, j, :])
                    link(ins)
                    nc.vector.tensor_scalar(var[:], mv[:, :, 1], EPS, None, ALU.add).then_inc(v_stat, 1)
                    ve.wait_ge(g_rstd, i)
                    for j in range(G):
                        ins = nc.vector.tensor_scalar(xf[:, j, :], xg[:, j, :], mv[:, j, 0:1], rstd[:, j:j + 1],
                                                      ALU.subtract, ALU.mult)
                    ins.then_inc(v_norm, 1)
                    ve.wait_ge(pe_xt, i)
                    nc.vector.tensor_copy(xt[:, 1, :], bank[1][:, 0:GT]).then_inc(v_xt, 1)
                    ve.wait_ge(pe_logits, i)
                    link(nc.vector.tensor_tensor(
                        logits[:], bank[2][0:T, 0:G * E1].rearrange("p (g e) -> p g e", g=G),
                        prog.w("f1_gate_b_row")[0:T].unsqueeze(1).broadcast_to([T, G, E1]), ALU.add))
                    link(nc.vector.tensor_tensor(
                        logits[:], logits[:], prog.w("f1_ebias_row")[0:T].unsqueeze(1).broadcast_to([T, G, E1]),
                        ALU.add), apart=True)
                    for j in range(G):
                        ins = nc.vector.max(top[:, j, :], logits[:, j, :])
                    link(ins, apart=True)
                    for j in range(G):
                        ins = nc.vector.max_index(arg[:, j, :], top[:, j, :], logits[:, j, :])
                    link(ins)
                    link(nc.vector.tensor_copy(argf[:], arg[:]))
                    nc.vector.tensor_tensor(
                        hot[:, bass.ds((i - 1) * G, G), :],
                        prog.w("iota_e")[0:T, 0:E1].unsqueeze(1).broadcast_to([T, G, E1]),
                        argf[:, :, 0:1].broadcast_to([T, G, E1]), ALU.is_equal).then_inc(v_hot, 1)
                ve.wait_ge(v_hot, NG)
                nc.vector.tensor_copy(hot_b[:], hot[:]).then_inc(v_bf, 1)
                n = [0]

                def step(ins):
                    n[0] += 1
                    ins.then_inc(v_count, 1)
                    ve.wait_ge(v_count, n[0])

                def by_expert(at):
                    return bank[3][0:T, at * B * E1:(at + 1) * B * E1].rearrange("t (b e) -> t e b", b=B)

                ve.wait_ge(pe_count, 1)
                step(nc.vector.tensor_copy(start[:], by_expert(0)))
                step(nc.vector.tensor_tensor_scan(upto[:].rearrange("t e b -> t (e b)"), prog.w("prefix_keep")[0:T],
                                                  start[:].rearrange("t e b -> t (e b)"), 0.0, ALU.mult, ALU.add))
                step(nc.vector.tensor_tensor(
                    full[:], upto[:, :, B - 1:B].broadcast_to([T, E1, MAX_E1_TILES]),
                    prog.w("tile_floor")[0:T].rearrange("t (e m) -> t e m", e=E1), ALU.is_gt))
                step(nc.vector.tensor_reduce(tiles[:], full[:], AX.X, ALU.add))
                step(nc.vector.tensor_tensor_scan(ends[:], ones[:], tiles[:], 0.0, ALU.mult, ALU.add))
                step(nc.vector.tensor_tensor(first[:], ends[:], tiles[:], ALU.subtract))
                step(nc.vector.tensor_scalar(first[:], first[:], float(E1_ROWS), None, ALU.mult))
                step(nc.vector.tensor_tensor(start[:], upto[:], start[:], ALU.subtract))
                step(nc.vector.tensor_tensor(start[:], start[:], first[:].unsqueeze(2).broadcast_to([T, E1, B]), ALU.add))
                step(nc.vector.tensor_tensor(rank[:].rearrange("t b e -> t e b"), by_expert(1), start[:], ALU.add))
                step(nc.vector.tensor_tensor(rank[:], rank[:], hot[:], ALU.mult))
                step(nc.vector.tensor_reduce(rowf[:], rank[:], AX.X, ALU.add))
                step(nc.vector.tensor_copy(prog.row1[:], rowf[:]))
                assert n[0] == prog.route1_rows
                step(nc.vector.tensor_tensor(
                    past[:], ends[:].unsqueeze(1).broadcast_to([T, TILES1, E1]),
                    prog.w("tile_no")[0:T].unsqueeze(2).broadcast_to([T, TILES1, E1]), ALU.is_le))
                step(nc.vector.tensor_reduce(tile_f[:], past[:], AX.X, ALU.add))
                step(nc.vector.tensor_scalar(tile_f[:], tile_f[:], float(E1 - 1), None, ALU.min))
                step(nc.vector.tensor_copy(prog.tile_expert[:], tile_f[0:1]))


def stage_experts1(prog):
    nc = prog.nc
    NM = FF // P
    HM = NM // 2
    ROUNDS = TILES1 // 2
    with stage(nc, "experts1") as (sem, sbuf, psum):
        def pair(label):
            return [sem(f"{label}{s}") for s in range(2)]

        ids_in, v_idf, pe_id, v_id = sem("ids_in"), sem("v_idf"), sem("pe_id"), sem("v_id")
        order = sem("order")
        w1_in, b1_in, w2_in, b2_in = pair("w1_in"), pair("b1_in"), pair("w2_in"), pair("b2_in")
        v_now, rows_in, pe_xt, v_xt = pair("v_now"), pair("rows_in"), pair("pe_xt"), pair("v_xt")
        pe_h = [pair(f"pe_h{q}_") for q in range(2)]
        a_h = [pair(f"a_h{q}_") for q in range(2)]
        pe_down, v_out, stored = pair("pe_down"), pair("v_out"), pair("stored")

        ids = sbuf("ids", [TILES1, P], I32)
        idf = sbuf("idf", [TILES1, P])
        token = sbuf("token", [P, TILES1 + 2], I32)
        now = [sbuf(f"now{s}", [P, 1], I32) for s in range(2)]
        w1 = [sbuf(f"w1_{s}", [P, KD, FF]) for s in range(2)]
        b1 = [sbuf(f"b1_{s}", [P, NM]) for s in range(2)]
        w2 = [sbuf(f"w2_{s}", [P, NM, D]) for s in range(2)]
        b2 = [sbuf(f"b2_{s}", [P, D]) for s in range(2)]
        xe = [sbuf(f"xe{s}", [P, D]) for s in range(2)]
        xt = [sbuf(f"xt{s}", [P, KD, P]) for s in range(2)]
        h = [sbuf(f"h{s}", [P, NM, P]) for s in range(2)]
        ye = [sbuf(f"ye{s}", [P, D]) for s in range(2)]
        ps_xt = psum("ps_xt", [P, 512])
        ps_id = psum("ps_id", [P, 512])
        ps_h = [[psum(f"ps_h{q}_{s}", [P, HM, P]) for s in range(2)] for q in range(2)]
        ps_out = [psum(f"ps_out{s}", [P, 512]) for s in range(2)]

        def earlier(engine, semaphore, n, per=1):
            if not (isinstance(n, int) and n == 1):
                engine.wait_ge(semaphore, n * per - per)

        def run(engine, body):
            body(1, False)
            with engine.Fori(2, ROUNDS) as i:
                body(i, False)
            body(ROUNDS, True)

        with nc.Block() as block:
            @block.sync
            def _(sp):
                sp.dma_start(ids[:], prog.row_token[1].rearrange("(c p) o -> c (p o)", p=P)).then_inc(ids_in, 16)

                def body(n, last):
                    for s in range(2):
                        tile = n * 2 + (s - 2)
                        e = sp.value_load(prog.tile_expert[0:1, bass.ds(tile, 1)], min_val=0, max_val=E1 - 1)
                        earlier(sp, pe_h[1][s], n)
                        sp.dma_start(w1[s][:], prog.ins["w1"][bass.ds(e, 1)].rearrange("e p k f -> p (e k) f")
                                     ).then_inc(w1_in[s], 16)
                        earlier(sp, a_h[1][s], n)
                        sp.dma_start(b1[s][:], prog.ins["b1"][bass.ds(e, 1)].rearrange("e p m -> p (e m)")
                                     ).then_inc(b1_in[s], 16)
                        earlier(sp, pe_down[s], n)
                        sp.dma_start(w2[s][:], prog.ins["w2"][bass.ds(e, 1)].rearrange("e p k d -> p (e k) d")
                                     ).then_inc(w2_in[s], 16)
                        earlier(sp, v_out[s], n)
                        sp.dma_start(b2[s][:], prog.ins["b2"][bass.ds(e, 1)].broadcast_to([P, D])
                                     ).then_inc(b2_in[s], 16)

                run(sp, body)

            @block.gpsimd
            def _(g):
                with g.Fori(1, ROUNDS + 1) as i:
                    for s in range(2):
                        g.wait_ge(v_now[s], i)
                        g.sem_inc(order, 1)
                        g.indirect_dma_start(xe[s][:], None, prog.ln_rows[1],
                                             bass.IndirectOffsetOnAxis(now[s][:], 0)).then_inc(rows_in[s], 16)

            @block.tensor
            def _(pe):
                def turn(s, n):
                    pe.wait_ge(rows_in[s], n * 16)
                    if s == 1:
                        pe.wait_ge(v_xt[0], n)
                    else:
                        earlier(pe, v_xt[1], n)
                    for c in range(KD):
                        ins = nc.tensor.transpose(ps_xt[:, c * P:(c + 1) * P], xe[s][:, c * P:(c + 1) * P],
                                                  prog.w("ident"))
                    ins.then_inc(pe_xt[s], 1)

                def tile(s, n, last):
                    pe.wait_ge(v_xt[s], n)
                    pe.wait_ge(w1_in[s], n * 16)
                    for q in range(2):
                        earlier(pe, a_h[q][s], n)
                        for m in range(q * HM, (q + 1) * HM):
                            for k in range(KD):
                                ins = nc.tensor.matmul(ps_h[q][s][:, m % HM, :], w1[s][:, k, m * P:(m + 1) * P],
                                                       xt[s][:, k, :], start=(k == 0), stop=(k == KD - 1))
                        ins.then_inc(pe_h[q][s], 1)
                    if not last:
                        turn(1 - s, n + s)
                    pe.wait_ge(w2_in[s], n * 16)
                    earlier(pe, v_out[s], n)
                    for m in range(NM):
                        if m % HM == 0:
                            pe.wait_ge(a_h[m // HM][s], n)
                        ins = nc.tensor.matmul(ps_out[s][:, 0:D], h[s][:, m, :], w2[s][:, m, :],
                                               start=(m == 0), stop=(m == NM - 1))
                    ins.then_inc(pe_down[s], 1)

                pe.wait_ge(v_idf, 1)
                nc.tensor.transpose(ps_id[:, 0:TILES1], idf[:], prog.w("ident")[0:TILES1, 0:TILES1]).then_inc(pe_id, 1)
                turn(0, 1)

                def body(n, last):
                    tile(0, n, False)
                    tile(1, n, last)

                run(pe, body)

            @block.scalar
            def _(act):
                def body(n, last):
                    for s in range(2):
                        act.wait_ge(b1_in[s], n * 16)
                        earlier(act, pe_down[s], n)
                        for q in range(2):
                            act.wait_ge(pe_h[q][s], n)
                            for m in range(q * HM, (q + 1) * HM):
                                ins = nc.scalar.activation(h[s][:, m, :], ps_h[q][s][:, m % HM, :], ACT.Relu,
                                                           bias=b1[s][:, m:m + 1])
                            ins.then_inc(a_h[q][s], 1)
                        if s == 1:
                            store(0, n)
                        elif not (isinstance(n, int) and n == 1):
                            store(1, n - 1)

                def store(s, n):
                    act.wait_ge(v_out[s], n)
                    act.dma_start(prog.expert_out[1].rearrange("(c p) d -> c p d", p=P)[bass.ds(n * 2 + (s - 2), 1)]
                                  .rearrange("c p d -> p (c d)"), ye[s][:]).then_inc(stored[s], 16)

                run(act, body)
                store(1, ROUNDS)
                for s in range(2):
                    act.wait_ge(stored[s], ROUNDS * 16)

            @block.vector
            def _(ve):
                nc.vector.memset(token[:], 0)
                ve.wait_ge(ids_in, 16)
                nc.vector.tensor_copy(idf[:], ids[:]).then_inc(v_idf, 1)
                ve.wait_ge(v_idf, 1)
                ve.wait_ge(pe_id, 1)
                nc.vector.tensor_copy(token[:, 0:TILES1], ps_id[:, 0:TILES1]).then_inc(v_id, 1)
                ve.wait_ge(v_id, 1)
                for s in range(2):
                    nc.vector.tensor_copy(now[s][:], token[:, s:s + 1]).then_inc(v_now[s], 1)

                def turn(s, n):
                    ve.wait_ge(pe_xt[s], n)
                    nc.vector.tensor_copy(xt[s][:], ps_xt[:, 0:KD * P].rearrange("p (k c) -> p k c", k=KD)
                                          ).then_inc(v_xt[s], 1)
                    nc.vector.tensor_copy(now[s][:], token[:, bass.ds(n * 2 + s, 1)]).then_inc(v_now[s], 1)

                def body(n, last):
                    for s in range(2):
                        if not (last and s == 1):
                            turn(1 - s, n + s)
                        ve.wait_ge(pe_down[s], n)
                        ve.wait_ge(b2_in[s], n * 16)
                        earlier(ve, stored[s], n, 16)
                        nc.vector.tensor_tensor(ye[s][:], ps_out[s][:, 0:D], b2[s][:], ALU.add).then_inc(v_out[s], 1)

                turn(0, 1)
                run(ve, body)


def stage_combine1(prog):
    nc = prog.nc
    with stage(nc, "combine1") as (sem, sbuf, psum):
        x_in, got_in, v_now, v_out, stored, v_free, g_order = (
            sem(n) for n in ("x_in", "got_in", "v_now", "v_out", "stored", "v_free", "g_order"))
        now = sbuf("now", [T, G], I32)
        got = sbuf("got", [T, G, D])
        acc = sbuf("acc", [T, G, D])
        res = sbuf("res", [T, G, D])

        with nc.Block() as block:
            @block.sync
            def _(sp):
                with sp.Fori(1, NG + 1) as i:
                    def group(dram):
                        return dram[bass.ds((i - 1) * G, G)].rearrange("g t d -> t g d")

                    sp.wait_ge(v_free, i)
                    sp.dma_start(acc[:], group(prog.x[5])).then_inc(x_in, 16)
                    sp.wait_ge(v_out, i)
                    sp.dma_start(group(prog.out), res[:]).then_inc(stored, 16)
                    sp.wait_ge(stored, i * 16)
                    sp.sem_inc(v_free, 1)

            @block.gpsimd
            def _(g):
                with g.Fori(1, NG + 1) as i:
                    g.wait_ge(v_now, i)
                    g.sem_inc(g_order, 1)
                    for j in range(G):
                        g.indirect_dma_start(got[:, j, :], None, prog.expert_out[1],
                                             bass.IndirectOffsetOnAxis(now[:, j:j + 1], 0)).then_inc(got_in, 16)

            @block.vector
            def _(ve):
                ve.sem_inc(v_free, 1)
                with ve.Fori(1, NG + 1) as i:
                    ve.wait_ge(v_free, i)
                    nc.vector.tensor_copy(now[:], prog.row1[:, bass.ds((i - 1) * G, G)]).then_inc(v_now, 1)
                    ve.wait_ge(x_in, i * 16)
                    ve.wait_ge(got_in, i * (16 * G))
                    nc.vector.tensor_tensor(res[:], got[:], acc[:], ALU.add).then_inc(v_out, 1)


def build(nc, ins, out):
    prog = Program(nc, ins, out)
    stage_setup(prog)
    stage_mixer(prog)
    stage_context_keys(prog)
    stage_queries(prog, 0, with_keys=False)
    stage_attention(prog, 0)
    stage_route0(prog)
    stage_experts0(prog)
    stage_combine0(prog)
    stage_queries(prog, 1, with_keys=True)
    stage_attention(prog, 1)
    stage_queries(prog, 2, with_keys=False)
    stage_attention(prog, 2)
    stage_route1(prog)
    stage_experts1(prog)
    stage_combine1(prog)


def kernel(**inputs):
    import concourse.bacc as bacc
    from concourse.bass_utils import run_bass_kernel_spmd

    arrays = {f"in_{name}": np.ascontiguousarray(a)
              for name, a in host_layout({k: np.asarray(v) for k, v in inputs.items()}).items()}
    nc = bacc.Bacc("TRN2", target_bir_lowering=False, num_devices=1)
    ins = {name[3:]: nc.dram_tensor(name, a.shape, mybir.dt.from_np(a.dtype), kind="ExternalInput").ap()
           for name, a in arrays.items()}
    out = nc.dram_tensor("out", [B, T, D], F32, kind="ExternalOutput").ap()
    build(nc, ins, out)
    r = run_bass_kernel_spmd(nc, [arrays], core_ids=[0])
    return r.results[0]["out"]
```

```python
from contextlib import contextmanager

import numpy as np

import concourse.bass as bass
from concourse import mybir
from concourse.alu_op_type import AluOpType as ALU

F32 = mybir.dt.float32
BF16 = mybir.dt.bfloat16
I32 = mybir.dt.int32
U32 = mybir.dt.uint32
U8 = mybir.dt.uint8
ACT = mybir.ActivationFunctionType
AX = mybir.AxisListType

P = 128
B, T, D = 16, 100, 256
G = 4
NG = B // G
GT = G * T
S2 = 361
H, DH = 16, 16
KD = D // P
EPS = 1e-5
CHUNK = 64
MLP = 1024
NSTATE = 64
E0, NGRP, TOPK, CAP = 32, 8, 4, 250
HID = 512
E1, FF = 8, 1024
N = B * T
E1_ROWS = P
MAX_E1_TILES = -(-N // E1_ROWS)
TILES1 = (N + E1 * (E1_ROWS - 1)) // E1_ROWS
SLOTS0 = E0 * CAP
BIG = -1e30
FLOOR = -1e25
TWO_PI = 6.283185307179586

WIDTHS = [
    ("ident", P),
    ("chunk_keep", GT), ("tidx", CHUNK), ("rot_sign", 1), ("freq", 1), ("log_decay", 1),
    ("w_in", KD * P), ("w_in_swap", KD * P), ("w_gate", KD * D), ("w_out", D),
    ("coupling", P), ("coupling_swap", P),
    ("ln1_g", KD), ("ln1_b", KD), ("ln2_g", KD), ("ln2_b", KD),
    ("b_gate_row", D), ("centroids", D),
    ("x0_wk", KD * D), ("x0_bk", KD), ("x1_wk", KD * D), ("x1_bk", KD),
    ("w_mlp1", KD * MLP), ("b_mlp1", MLP // P),
    ("w_mlp2", MLP // P * D), ("b_mlp2_row", D),
    ("x0_wq", KD * D), ("x0_bq", KD), ("x0_wv", KD * D),
    ("x0_bv_row", D), ("x0_wo", KD * D), ("x0_bo_row", D),
    ("x1_wq", KD * D), ("x1_bq", KD), ("x1_wv", KD * D),
    ("x1_bv_row", D), ("x1_wo", KD * D), ("x1_bo_row", D),
    ("s_wq", KD * D), ("s_wq_rot", KD * D), ("s_bq", KD), ("s_bq_rot", KD),
    ("s_wk", KD * D), ("s_wk_rot", KD * D), ("s_bk", KD), ("s_bk_rot", KD),
    ("s_wv", KD * D), ("s_bv_row", D), ("s_wo", KD * D), ("s_bo_row", D),
    ("rope_cos", T), ("rope_sin", T),
    ("f0_bias_row", E0), ("f0_sg", KD * HID), ("f0_su", KD * HID),
    ("f0_sd", HID // P * D), ("iota_e", E0), ("spare_row", B * TOPK),
    ("f1_gate_w", KD * E1), ("f1_gate_b_row", E1), ("f1_ebias_row", E1), ("tok_id", B),
    ("tile_floor", E1 * MAX_E1_TILES), ("tile_no", TILES1), ("prefix_keep", E1 * B),
]
START = {}
_at = 0
for _name, _width in WIDTHS:
    START[_name] = (_at, _width)
    _at += _width
TOTAL = _at
SEGMENTS = [(0, START["x0_wk"][0]), (START["x0_wk"][0], START["x0_wq"][0]), (START["x0_wq"][0], TOTAL)]

BWIDTHS = [("ident_b", P), ("big_diag", G * T), ("head_sel", H), ("before", T), ("ones_b", T)]
BSTART = {}
_at = 0
for _name, _width in BWIDTHS:
    BSTART[_name] = (_at, _width)
    _at += _width
BTOTAL = _at

Q_PARTS = [(0, 0, 3, 1), (1, 3, 6, 2), (2, 4, 5, 1)]
K_PARTS = [(0, 2, 5, 1), (1, 0, 6, 5), (2, 1, 2, 1)]
SHIFT_ROW = 6 * DH
ROPE_PAIR = 2


def rope_tables():
    grid, dim = 16, 2 * (DH // 3 // 2)
    half = dim // 2
    ids = np.arange(T)
    frames = ids // (grid * grid)
    rem = ids - grid * grid * frames
    rows = rem // grid
    cols = rem - grid * rows
    inv = (1.0 / 10000.0 ** (np.arange(half, dtype=np.float32) / (dim / 2.0))).astype(np.float32)
    cos = np.ones((DH, T), np.float32)
    sin = np.zeros((DH, T), np.float32)
    for k, pos in enumerate((frames, rows, cols)):
        freq = pos.astype(np.float32)[:, None] * inv
        for j in range(dim):
            cos[k * dim + j] = np.cos(freq[:, j % half])
            sin[k * dim + j] = np.sin(freq[:, j % half]) * (-1.0 if j % 2 == 0 else 1.0)
    return np.repeat(cos, P // DH, axis=0), np.repeat(sin, P // DH, axis=0)


def host_layout(inp):
    def k_major(w):
        return w.reshape(w.shape[0] // P, P, w.shape[1]).transpose(1, 0, 2).reshape(P, -1)

    def col(v):
        return v.reshape(-1, P).T

    def row(v):
        return np.broadcast_to(v[None, :], (P, v.shape[0]))

    def rows_to(a, width):
        out = np.zeros((P, width), np.float32)
        out[:a.shape[0]] = a
        return out

    swap = np.r_[NSTATE:2 * NSTATE, 0:NSTATE]
    by_dim = np.arange(D).reshape(2, H // 2, DH).transpose(0, 2, 1).reshape(-1)
    w_in_t = inp["L0_attn_w_in"].T
    bd = np.zeros((P, P), np.float32)
    for part in range(2):
        for h in range(4):
            at = part * NSTATE + 16 * h
            bd[at:at + 16, at:at + 16] = inp["L0_attn_coupling"][h]
    t = np.arange(T)
    keep = np.ones(T, np.float32)
    keep[[CHUNK - 1, T - 1]] = 0.0
    cos, sin = rope_tables()
    a = {
        "ident": np.eye(P, dtype=np.float32),
        "chunk_keep": np.tile(row(keep), (1, G)),
        "tidx": row(np.arange(CHUNK, dtype=np.float32)),
        "rot_sign": np.repeat(np.array([-1.0, 1.0], np.float32), NSTATE)[:, None],
        "freq": np.tile(inp["L0_attn_frequency"], 2)[:, None],
        "log_decay": np.tile(inp["L0_attn_log_decay"], 2)[:, None],
        "w_in": k_major(w_in_t), "w_in_swap": k_major(w_in_t[:, swap]),
        "w_gate": k_major(inp["L0_attn_w_gate"].T), "w_out": inp["L0_attn_w_out"].T,
        "coupling": bd, "coupling_swap": bd[:, swap],
        "ln1_g": col(inp["L0_attn_ln1_g"]), "ln1_b": col(inp["L0_attn_ln1_b"]),
        "ln2_g": col(inp["L0_attn_ln2_g"]), "ln2_b": col(inp["L0_attn_ln2_b"]),
        "b_gate_row": row(inp["L0_attn_b_gate"]),
        "w_mlp1": k_major(inp["L0_attn_w_mlp1"].T), "b_mlp1": col(inp["L0_attn_b_mlp1"]),
        "w_mlp2": k_major(inp["L0_attn_w_mlp2"].T), "b_mlp2_row": row(inp["L0_attn_b_mlp2"]),
        "rope_cos": cos, "rope_sin": sin,
        "centroids": rows_to(np.concatenate([inp["L0_ffn_expert_centroids"],
                                             inp["L0_ffn_group_centroids"]]), D),
        "f0_bias_row": row(inp["L0_ffn_bias"]),
        "f0_sg": k_major(inp["L0_ffn_sg"]), "f0_su": k_major(inp["L0_ffn_su"]),
        "f0_sd": k_major(inp["L0_ffn_sd"]), "iota_e": row(np.arange(E0, dtype=np.float32)),
        "f1_gate_w": k_major(inp["L1_ffn_gate_w"].T), "f1_gate_b_row": row(inp["L1_ffn_gate_b"]),
        "f1_ebias_row": row(inp["L1_ffn_expert_bias"]),
        "spare_row": (SLOTS0 + np.arange(P)[:, None] % T + T * np.arange(B * TOPK)[None, :]).astype(np.float32),
        "tile_floor": row(np.tile(np.arange(MAX_E1_TILES, dtype=np.float32) * E1_ROWS, E1)),
        "tile_no": row(np.arange(TILES1, dtype=np.float32)),
        "prefix_keep": row(np.tile((np.arange(B) > 0).astype(np.float32), E1)),
        "tok_id": (np.arange(P)[:, None] + T * np.arange(B)[None, :]).astype(np.float32),
    }
    for x, name in (("x0", "L0_xattn"), ("x1", "L1_xattn")):
        for m in "qkvo":
            w, b = inp[f"{name}_W{m}"].T, inp[f"{name}_b{m}"]
            a[f"{x}_w{m}"] = k_major(w if m in "vo" else w[:, by_dim])
            a.update({f"{x}_b{m}_row": row(b)} if m in "vo" else {f"{x}_b{m}": col(b[by_dim])})
    for m in "qkvo":
        w, b = inp[f"L1_attn_W{m}"], inp[f"L1_attn_b{m}"]
        if m in "qk":
            a[f"s_w{m}"] = k_major(w[:, by_dim])
            a[f"s_b{m}"] = col(b[by_dim])
            a[f"s_w{m}_rot"] = k_major(w[:, by_dim ^ 1])
            a[f"s_b{m}_rot"] = col(b[by_dim ^ 1])
        else:
            a[f"s_w{m}"] = k_major(w)
            a[f"s_b{m}_row"] = row(b)
    packed = np.concatenate([a[n] for n, _ in WIDTHS], axis=1)
    assert packed.shape == (P, TOTAL) and all(a[n].shape[1] == w for n, w in WIDTHS)

    bf = mybir.dt.np(BF16)
    big = np.zeros((P, G, T), np.float32)
    big[t, :, t] = BIG
    head_sel = np.zeros((P, H), np.float32)
    for part in range(2):
        head_sel[SHIFT_ROW + part * H + np.arange(H), np.arange(H)] = 1.0
    before = np.zeros((P, T), np.float32)
    before[:T] = (t[:, None] < t[None, :])
    c = {"ident_b": np.eye(P), "big_diag": big.reshape(P, -1), "head_sel": head_sel,
         "before": before, "ones_b": np.ones((P, T))}
    consts = np.concatenate([np.asarray(c[n], np.float32) for n, _ in BWIDTHS], axis=1).astype(bf)
    ctx = inp["ctx_1024"]
    return {
        "x": inp["x"],
        "ctx_t": ctx.reshape(B, S2, KD, P).transpose(0, 3, 2, 1),
        "mask": inp["mask_BxSxS2_bk1"],
        "packed": packed,
        "consts": consts,
        "wg": inp["L0_ffn_wg"].reshape(E0, KD, P, HID).transpose(0, 2, 1, 3),
        "wu": inp["L0_ffn_wu"].reshape(E0, KD, P, HID).transpose(0, 2, 1, 3),
        "wd": inp["L0_ffn_wd"].reshape(E0, HID // P, P, D).transpose(0, 2, 1, 3),
        "w1": inp["L1_ffn_w1"].reshape(E1, KD, P, FF).transpose(0, 2, 1, 3),
        "b1": inp["L1_ffn_b1"].reshape(E1, FF // P, P).transpose(0, 2, 1),
        "w2": inp["L1_ffn_w2"].reshape(E1, FF // P, P, D).transpose(0, 2, 1, 3),
        "b2": inp["L1_ffn_b2"],
    }


class Program:

    def __init__(self, nc, ins, out):
        self.nc = nc
        self.ins = ins
        self.out = out

        def dram(name, shape, dt=F32):
            return nc.dram_tensor(name, shape, dt, kind="Internal").ap()

        self.x = [ins["x"]] + [dram(f"x_after_{k}", [B, T, D]) for k in range(5)]
        self.q_stack = [dram(f"q_stack_{l}", [2, 6, P, B, T], BF16) for l in range(3)]
        self.k_stack = [dram("k_stack_0", [B, 6, P, 2, S2], BF16), dram("k_stack_1", [2, 6, P, B, T], BF16),
                        dram("k_stack_2", [B, 6, P, 2, S2], BF16)]
        self.xn_t = dram("xn_t_self", [B, P, KD, T])
        self.ln_rows = dram("ln_rows", [N, D])
        self.row_token = dram("row_token", [SLOTS0 + N * TOPK, 1], I32)
        self.expert_in = dram("expert_in", [TILES1 * E1_ROWS, D])
        self.expert_out = [dram("expert_out_0", [SLOTS0, D]), dram("expert_out_1", [TILES1 * E1_ROWS, D])]
        self.x_shared = dram("x_shared", [B, T, D])
        self.route1_rows = 13
        self.choice_row = nc.alloc_sbuf_tensor("choice_row", [T, B, TOPK], I32)
        self.choice_gate = nc.alloc_sbuf_tensor("choice_gate", [T, B, TOPK], F32)
        self.row1 = nc.alloc_sbuf_tensor("row1", [T, B], I32)
        self.tile_expert = nc.alloc_sbuf_tensor("tile_expert", [1, TILES1], I32)
        self.packed = nc.alloc_sbuf_tensor("packed_sb", [P, TOTAL], F32)
        self.consts = nc.alloc_sbuf_tensor("consts_sb", [P, BTOTAL], BF16)
        self.rot_cos = nc.alloc_sbuf_tensor("rot_cos", [P, GT], F32)
        self.rot_sin = nc.alloc_sbuf_tensor("rot_sin", [P, GT], F32)
        self.decay = nc.alloc_sbuf_tensor("decay", [P, GT], F32)
        self.w_mix = nc.alloc_sbuf_tensor("w_mix", [P, 2, D], F32)
        self.half_neg = nc.alloc_sbuf_tensor("half_neg", [P, G], F32)
        self.cent_t = nc.alloc_sbuf_tensor("cent_t", [P, KD, E0 + NGRP], F32)

        self.segment_in = [nc.alloc_semaphore(f"segment_in{k}") for k in range(len(SEGMENTS))]

    def load_segment(self, engine, k):
        at, end = SEGMENTS[k]
        engine.dma_start(self.packed[:, at:end], self.ins["packed"][:, at:end]).then_inc(self.segment_in[k], 16)

    def w(self, name, k=None):
        at, width = START[name]
        ap = self.packed[:, at:at + width]
        return ap if k is None else ap.rearrange("p (k n) -> p k n", k=k)

    def c(self, name):
        at, width = BSTART[name]
        return self.consts[:, at:at + width]


@contextmanager
def stage(nc, label):
    made, cms = [], []

    def sem(name):
        made.append(nc.alloc_semaphore(f"{label}_{name}"))
        return made[-1]

    def sbuf(name, shape, dt=F32):
        cm = nc.sbuf_tensor(f"{label}_{name}", shape, dt)
        cms.append(cm)
        return cm.__enter__()

    def psum(name, shape, dt=F32):
        cm = nc.psum_tensor(f"{label}_{name}", shape, dt)
        cms.append(cm)
        return cm.__enter__()

    yield sem, sbuf, psum
    for cm in reversed(cms):
        cm.__exit__(None, None, None)
    nc.clear_and_free_semaphores(made)
    nc.all_engine_barrier()


def stage_setup(prog):
    nc = prog.nc
    with stage(nc, "setup") as (sem, sbuf, psum):
        loaded, consts_in = prog.segment_in[0], sem("consts_loaded")
        v_done, a_done, pe_done, g_done = (sem(n) for n in ("v_done", "a_done", "pe_done", "g_done"))
        ang = sbuf("ang", [P, CHUNK])
        turns = sbuf("turns", [P, CHUNK])
        halfa = sbuf("halfa", [P, CHUNK])
        sn = sbuf("sn", [P, CHUNK])
        sh = sbuf("sh", [P, CHUNK])
        mag = sbuf("mag", [P, 2])
        cent = sbuf("cent", [P, D])
        cst = sbuf("cst", [P, 4])
        ps_mix = psum("ps_mix", [P, 2, D])
        ps_cent = psum("ps_cent", [P, KD, P])
        NC_ = E0 + NGRP
        order = {}

        with nc.Block() as block:
            @block.sync
            def _(sp):
                for k in range(2):
                    prog.load_segment(sp, k)
                sp.dma_start(prog.consts[:], prog.ins["consts"]).then_inc(consts_in, 16)
                sp.wait_ge(consts_in, 16)

            @block.vector
            def _(v):
                n = [0]

                def step(ins):
                    n[0] += 1
                    ins.then_inc(v_done, 1)
                    v.wait_ge(v_done, n[0])

                step(nc.vector.memset(prog.half_neg[:], -0.5))
                step(nc.vector.memset(cst[:, 3:4], 0.5))
                v.wait_ge(loaded, 16)
                step(nc.vector.tensor_scalar(ang[:], prog.w("tidx"), prog.w("freq"), None, ALU.mult))
                step(nc.vector.tensor_scalar(turns[:], ang[:], 1.0 / TWO_PI, 12582912.0, ALU.mult, ALU.add))
                step(nc.vector.tensor_scalar(turns[:], turns[:], -12582912.0, None, ALU.add))
                for c in (6.28125, 0.0019340515136718750, 1.2556659146019e-06):
                    step(nc.vector.scalar_tensor_tensor(ang[:], turns[:], -c, ang[:], ALU.mult, ALU.add))
                step(nc.vector.tensor_scalar(ang[:], ang[:], 3.1415925, -3.1415925, ALU.min, ALU.max))
                step(nc.vector.tensor_scalar(halfa[:], ang[:], 0.5, None, ALU.mult))
                order["angles"] = n[0]
                v.wait_ge(a_done, 2)
                step(nc.vector.scalar_tensor_tensor(halfa[:], sh[:], -2.0, sh[:], ALU.mult, ALU.mult))
                step(nc.vector.tensor_scalar(halfa[:], halfa[:], 1.0, None, ALU.add))
                step(nc.vector.tensor_scalar(sn[:], sn[:], prog.w("rot_sign"), None, ALU.mult))
                for table, by_pos in ((prog.rot_cos, halfa), (prog.rot_sin, sn)):
                    view = table[:].rearrange("p (g t) -> p g t", g=G)
                    for at in (0, CHUNK):
                        width = min(CHUNK, T - at)
                        step(nc.vector.tensor_copy(
                            view[:, :, at:at + width],
                            by_pos[:, 0:width].unsqueeze(1).broadcast_to([P, G, width])))
                v.wait_ge(a_done, 3)
                step(nc.vector.tensor_scalar(mag[:, 0:1], mag[:, 0:1], 1.0, None, ALU.add))
                step(nc.vector.reciprocal(mag[:, 1:2], mag[:, 0:1]))
                step(nc.vector.tensor_scalar(prog.decay[:], prog.w("chunk_keep"), mag[:, 1:2], None, ALU.mult))
                step(nc.vector.tensor_tensor_reduce(cent[0:NC_, :], prog.w("centroids")[0:NC_, :],
                                                    prog.w("centroids")[0:NC_, :], 1.0, 0.0,
                                                    ALU.mult, ALU.add, cst[0:NC_, 0:1]))
                order["sums of squares"] = n[0]
                v.wait_ge(g_done, 1)
                step(nc.vector.tensor_scalar(cst[0:NC_, 1:2], cst[0:NC_, 1:2], 1e-12, None, ALU.max))
                step(nc.vector.reciprocal(cst[0:NC_, 2:3], cst[0:NC_, 1:2]))
                step(nc.vector.tensor_scalar(cent[0:NC_, :], prog.w("centroids")[0:NC_, :],
                                             cst[0:NC_, 2:3], None, ALU.mult))
                order["centroids scaled"] = n[0]
                v.wait_ge(pe_done, 1)
                step(nc.vector.tensor_copy(prog.w_mix[:], ps_mix[:]))
                v.wait_ge(pe_done, 2)
                step(nc.vector.tensor_copy(prog.cent_t[:], ps_cent[:, :, 0:NC_]))

            @block.scalar
            def _(act):
                act.wait_ge(v_done, order["angles"])
                nc.scalar.activation(sn[:], ang[:], ACT.Sin).then_inc(a_done, 1)
                nc.scalar.activation(sh[:], halfa[:], ACT.Sin).then_inc(a_done, 1)
                nc.scalar.activation(mag[:, 0:1], prog.w("log_decay"), ACT.Exp, scale=-1.0).then_inc(a_done, 1)

            @block.gpsimd
            def _(g):
                g.wait_ge(v_done, order["sums of squares"])
                nc.gpsimd.tensor_tensor(cst[0:NC_, 1:2], cst[0:NC_, 0:1], cst[0:NC_, 3:4],
                                        ALU.pow).then_inc(g_done, 1)

            @block.tensor
            def _(pe):
                pe.wait_ge(loaded, 16)
                for s, name in enumerate(("coupling", "coupling_swap")):
                    ins = nc.tensor.matmul(ps_mix[:, s, :], prog.w(name), prog.w("w_out"),
                                           start=True, stop=True)
                ins.then_inc(pe_done, 1)
                pe.wait_ge(v_done, order["centroids scaled"])
                for k in range(KD):
                    ins = nc.tensor.transpose(ps_cent[:, k, 0:NC_], cent[0:NC_, k * P:(k + 1) * P],
                                              prog.w("ident")[0:NC_, 0:NC_])
                ins.then_inc(pe_done, 1)


def stage_mixer(prog):
    nc = prog.nc
    x_dram, out_dram = prog.x[0], prog.x[1]
    NM = MLP // P
    LAYERS = ((0, "x0"), (2, "x1"))
    UNITS = G * len(LAYERS)
    STORED = len(K_PARTS) * 16
    with stage(nc, "mixer") as (sem, sbuf, psum):
        x_in = sem("x_in")
        x_free = sem("x_free")
        v_stat = [sem(f"v_stat{k}") for k in range(3)]
        g_rstd = [sem(f"g_rstd{k}") for k in range(3)]
        v_link = [sem(f"v_link{k}") for k in range(10)]
        v_apart, g_apart = sem("v_apart"), sem("g_apart")
        v_norm = [sem(f"v_norm{k}") for k in range(3)]
        pe_xt = sem("pe_xt")
        xt_ready = sem("xt_ready")
        pe_beta, pe_gate, pe_h = sem("pe_beta"), sem("pe_gate"), sem("pe_h")
        v_z, a_tanh = sem("v_z"), sem("a_tanh")
        v_states = sem("v_states")
        v_gh, v_x1 = sem("v_gh"), sem("v_x1")
        g_base = sem("g_base")
        pe_x2t, x2t_ready = sem("pe_x2t"), sem("x2t_ready")
        pe_up = [sem(f"pe_up{m}") for m in range(NM)]
        a_up = [sem(f"a_up{m}") for m in range(NM)]
        pe_down = sem("pe_down")
        v_out = sem("v_out")
        out_stored = sem("out_stored")
        ctx_in = [sem(f"ctx_in{s}") for s in range(2)]
        pe_key, a_key, a_part1, v_rest, a_part2, v_part3 = (
            sem(n) for n in ("pe_key", "a_key", "a_part1", "v_rest", "a_part2", "v_part3"))
        keys_stored = [sem(f"keys_stored{s}") for s in range(4)]

        xg = sbuf("xg", [T, G, D])
        stats = sbuf("stats", [T, G, 6])
        mv = sbuf("mv", [T, 3, G, 2])
        var = sbuf("var", [T, 3, G])
        rstd = sbuf("rstd", [T, 3, G])
        xin = sbuf("xin", [T, G, D])
        xh = sbuf("xh", [T, G, D])
        xt = sbuf("xt", [P, KD, GT])
        u1 = sbuf("u1", [P, GT])
        u2 = sbuf("u2", [P, GT])
        v = sbuf("v", [P, GT])
        sa = sbuf("sa", [P, GT])
        sb_ = sbuf("sb_", [P, GT])
        z = sbuf("z", [T, G, D])
        x1 = sbuf("x1", [T, G, D])
        base = sbuf("base", [T, G, D])
        xo = sbuf("xo", [T, G, D])
        up = sbuf("up", [P, NM, GT])
        ctx = [sbuf(f"ctx{s}", [P, KD, S2]) for s in range(2)]
        full = [sbuf(f"full{l}", [P, KD, S2]) for l in range(2)]
        rest = [sbuf(f"rest{l}", [P, KD, S2]) for l in range(2)]
        part = [sbuf(f"part{s}", [P, 3, KD, S2], BF16) for s in range(4)]
        bank = [psum(f"bank{k}", [P, 512]) for k in range(8)]
        ident = prog.w("ident")

        def tok(banks, j):
            return banks[j // 2][0:T, (j % 2) * D:(j % 2 + 1) * D]

        def earlier(engine, semaphore, n, per=1):
            if not (isinstance(n, int) and n == 1):
                engine.wait_ge(semaphore, n * per - per)

        def wait_unit(engine, semaphore, n, u, back=0):
            if not (isinstance(n, int) and n * UNITS + (u + 1 - UNITS - back) <= 0):
                engine.wait_ge(semaphore, n * UNITS + (u + 1 - UNITS - back))

        def run(engine, front, step):
            front(1)
            step(1, 2)
            with engine.Fori(2, NG) as i:
                step(i, i + 1)
            step(NG, None)

        def group(dram, n):
            return dram[bass.ds((n - 1) * G, G)].rearrange("g t d -> t g d")

        with nc.Block() as block:
            @block.sync
            def _(sp):
                def front(n):
                    earlier(sp, x_free, n)
                    sp.dma_start(xg[:], group(x_dram, n)).then_inc(x_in, 16)
                    if isinstance(n, int) and n == 1:
                        prog.load_segment(sp, 2)

                def step(n, n_next):
                    for u in range(UNITS):
                        layer, l = LAYERS[u % 2][0], u % 2
                        wait_unit(sp, v_part3, n, u)
                        dst = prog.k_stack[layer][bass.ds(n * G + (u // 2 - G), 1)]
                        for k, at, end, by in K_PARTS:
                            places = dst[:, at:end:by].rearrange("b g p m n -> p (b g) (m n)")
                            sp.dma_start(places, part[u % 4][:, k].rearrange("p m n -> p (m n)").unsqueeze(1)
                                         .broadcast_to(places.shape)
                                         ).then_inc(keys_stored[u % 4], 16)
                        if u == 5 and n_next is not None:
                            front(n_next)
                    sp.wait_ge(v_out, n)
                    sp.dma_start(group(out_dram, n), xo[:]).then_inc(out_stored, 16)

                run(sp, front, step)
                sp.wait_ge(out_stored, 16 * NG)
                sp.wait_ge(prog.segment_in[2], 16)
                for s in range(4):
                    sp.wait_ge(keys_stored[s], B * len(LAYERS) // 4 * STORED)

            @block.vector
            def _(ve):
                def rest_of(n, u):
                    wait_unit(ve, a_part1, n, u)
                    wait_unit(ve, v_part3, n, u, 2)
                    nc.vector.tensor_tensor(rest[u % 2][:], full[u % 2][:], part[u % 4][:, 0], ALU.subtract
                                            ).then_inc(v_rest, 1)

                def third(n, u):
                    wait_unit(ve, a_part2, n, u)
                    nc.vector.tensor_tensor(part[u % 4][:, 2], rest[u % 2][:], part[u % 4][:, 1], ALU.subtract
                                            ).then_inc(v_part3, 1)

                def moments(k, src, n):
                    for j in range(G):
                        ins = nc.vector.bn_stats(stats[:, j, :], src[:, j, :])
                    ins.then_inc(v_link[2 * k], 1)
                    ve.wait_ge(v_link[2 * k], n)
                    ve.sem_inc(v_apart, 1)
                    for j in range(G):
                        ins = nc.vector.bn_aggr(mv[:, k, j, :], stats[:, j, :])
                    ins.then_inc(v_link[2 * k + 1], 1)
                    ve.wait_ge(v_link[2 * k + 1], n)
                    nc.vector.tensor_scalar(var[:, k, :], mv[:, k, :, 1], EPS, None, ALU.add).then_inc(v_stat[k], 1)

                def normalise(k, dst, src, n):
                    ve.wait_ge(g_rstd[k], n)
                    for j in range(G):
                        ins = nc.vector.tensor_scalar(dst[:, j, :], src[:, j, :], mv[:, k, j, 0:1],
                                                      rstd[:, k, j:j + 1], ALU.subtract, ALU.mult)
                    ins.then_inc(v_norm[k], 1)

                def front(n, between=None):
                    earlier(ve, pe_x2t, n)
                    ve.wait_ge(x_in, n * 16)
                    moments(0, xg, n)
                    if between is not None:
                        rest_of(between, 6)
                    normalise(0, xin, xg, n)
                    ve.wait_ge(v_norm[0], n)
                    moments(1, xin, n)
                    if between is not None:
                        third(between, 6)
                    normalise(1, xh, xin, n)

                def step(n, n_next):
                    ve.wait_ge(pe_xt, n)
                    nc.vector.tensor_scalar(xt[:, 1, :], bank[1][:, 0:GT], prog.w("ln1_g")[:, 1:2],
                                            prog.w("ln1_b")[:, 1:2], ALU.mult, ALU.add).then_inc(xt_ready, 1)
                    rest_of(n, 0)
                    ve.wait_ge(pe_beta, n)
                    nc.vector.tensor_tensor(u1[:], bank[2][:, 0:GT], prog.rot_cos[:], ALU.mult)
                    nc.vector.tensor_tensor(u2[:], bank[3][:, 0:GT], prog.rot_sin[:], ALU.mult).then_inc(v_link[6], 1)
                    ve.wait_ge(v_link[6], n)
                    nc.vector.tensor_tensor(u1[:], u1[:], u2[:], ALU.add).then_inc(v_link[7], 1)
                    ve.wait_ge(v_link[7], n)
                    nc.vector.tensor_tensor_scan(v[:, ::-1], prog.decay[:, ::-1], u1[:, ::-1], 0.0,
                                                 ALU.mult, ALU.add).then_inc(v_link[8], 1)
                    ve.wait_ge(v_link[8], n)
                    by_seq = v[:].rearrange("p (g t) -> p g t", g=G)
                    beta_seq = bank[2][:, 0:GT].rearrange("p (g t) -> p g t", g=G)
                    nc.vector.tensor_tensor(by_seq[:, :, CHUNK], by_seq[:, :, CHUNK],
                                            beta_seq[:, :, CHUNK - 1], ALU.add).then_inc(v_link[9], 1)
                    ve.wait_ge(v_link[9], n)
                    nc.vector.tensor_tensor(sa[:], v[:], prog.rot_cos[:], ALU.mult)
                    nc.vector.tensor_tensor(sb_[:], v[:], prog.rot_sin[:], ALU.mult).then_inc(v_states, 1)
                    ve.wait_ge(pe_gate, n)
                    for h in range(2):
                        ins = nc.vector.tensor_tensor(
                            z[:, 2 * h:2 * h + 2, :], bank[4 + h][0:T, :].rearrange("p (g d) -> p g d", g=2),
                            prog.w("b_gate_row")[0:T].unsqueeze(1).broadcast_to([T, 2, D]), ALU.add)
                    ins.then_inc(v_z, 1)
                    rest_of(n, 1)
                    third(n, 0)
                    ve.wait_ge(a_tanh, n)
                    ve.wait_ge(pe_h, n)
                    for h in range(2):
                        ins = nc.vector.scalar_tensor_tensor(
                            z[:, 2 * h:2 * h + 2, :], z[:, 2 * h:2 * h + 2, :], 1.0,
                            bank[2 + h][0:T, :].rearrange("p (g d) -> p g d", g=2), ALU.add, ALU.mult)
                    ins.then_inc(v_gh, 1)
                    ve.wait_ge(v_gh, n)
                    earlier(ve, g_base, n)
                    nc.vector.scalar_tensor_tensor(x1[:], z[:], 0.5, xin[:], ALU.mult, ALU.add).then_inc(v_x1, 1)
                    ve.wait_ge(v_x1, n)
                    moments(2, x1, n)
                    third(n, 1)
                    rest_of(n, 2)
                    normalise(2, xh, x1, n)
                    rest_of(n, 3)
                    third(n, 2)
                    ve.wait_ge(pe_x2t, n)
                    nc.vector.tensor_scalar(xt[:, 1, :], bank[1][:, 0:GT], prog.w("ln2_g")[:, 1:2],
                                            prog.w("ln2_b")[:, 1:2], ALU.mult, ALU.add).then_inc(x2t_ready, 1)
                    third(n, 3)
                    for u in (4, 5):
                        rest_of(n, u)
                        third(n, u)
                    if n_next is not None:
                        front(n_next, n)
                    else:
                        rest_of(n, 6)
                        third(n, 6)
                    rest_of(n, 7)
                    third(n, 7)
                    ve.wait_ge(pe_down, n)
                    ve.wait_ge(g_base, n)
                    earlier(ve, out_stored, n, 16)
                    for h in range(2):
                        ins = nc.vector.tensor_tensor(
                            xo[:, 2 * h:2 * h + 2, :], bank[h][0:T, :].rearrange("p (g d) -> p g d", g=2),
                            base[:, 2 * h:2 * h + 2, :], ALU.add)
                    ins.then_inc(v_out, 1)

                run(ve, front, step)

            @block.gpsimd
            def _(g):
                def inverse_root(k, n):
                    g.wait_ge(v_stat[k], n)
                    nc.gpsimd.tensor_tensor(rstd[:, k, :], var[:, k, :], prog.half_neg[0:T, :],
                                            ALU.pow).then_inc(g_rstd[k], 1)

                def load_ctx(n, j):
                    g.dma_start(ctx[j % 2][:], prog.ins["ctx_t"][bass.ds(n * G + (j - G), 1)]
                                .rearrange("b p k n -> p (b k) n")).then_inc(ctx_in[j % 2], 16)

                def next_ctx(n, n_next, j):
                    if n_next is not None or j + 2 < G:
                        wait_unit(g, pe_key, n, 2 * j + 1)
                        g.sem_inc(g_apart, 1)
                        load_ctx(n, j + 2)

                def front(n):
                    if isinstance(n, int) and n == 1:
                        load_ctx(1, 0)
                        load_ctx(1, 1)
                    inverse_root(0, n)
                    inverse_root(1, n)

                def step(n, n_next):
                    next_ctx(n, n_next, 0)
                    g.wait_ge(v_x1, n)
                    earlier(g, v_out, n)
                    nc.gpsimd.tensor_tensor(base[:], xg[:], x1[:], ALU.add).then_inc(x_free, 1)
                    next_ctx(n, n_next, 1)
                    inverse_root(2, n)
                    g.wait_ge(x_free, n)
                    nc.gpsimd.tensor_tensor(base[:], base[:],
                                            prog.w("b_mlp2_row")[0:T].unsqueeze(1).broadcast_to([T, G, D]),
                                            ALU.add).then_inc(g_base, 1)
                    next_ctx(n, n_next, 2)
                    if n_next is not None:
                        front(n_next)
                    next_ctx(n, n_next, 3)

                run(g, front, step)

            @block.scalar
            def _(act):
                def key(n, u):
                    l = u % 2
                    wait_unit(act, pe_key, n, u)
                    wait_unit(act, v_rest, n, u, 2)
                    for m in range(KD):
                        ins = nc.scalar.activation(full[l][:, m, :], bank[6 + m][:, 0:S2], ACT.Identity,
                                                   bias=prog.w(f"{LAYERS[l][1]}_bk")[:, m:m + 1])
                    ins.then_inc(a_key, 1)
                    wait_unit(act, a_key, n, u)
                    if not (isinstance(n, int) and n == 1 and u < 4):
                        act.wait_ge(keys_stored[u % 4], n * (UNITS // 4 * STORED) + (u - UNITS) // 4 * STORED)
                    nc.scalar.copy(part[u % 4][:, 0], full[l][:]).then_inc(a_part1, 1)

                def second(n, u):
                    wait_unit(act, v_rest, n, u)
                    nc.scalar.copy(part[u % 4][:, 1], rest[u % 2][:]).then_inc(a_part2, 1)

                def step(n, n_next):
                    act.wait_ge(pe_xt, n)
                    nc.scalar.activation(xt[:, 0, :], bank[0][:, 0:GT], ACT.Identity,
                                         scale=prog.w("ln1_g")[:, 0:1], bias=prog.w("ln1_b")[:, 0:1]
                                         ).then_inc(xt_ready, 1)
                    key(n, 0)
                    key(n, 1)
                    second(n, 0)
                    act.wait_ge(v_z, n)
                    nc.scalar.activation(z[:], z[:], ACT.Tanh, scale=0.5).then_inc(a_tanh, 1)
                    key(n, 2)
                    second(n, 1)
                    key(n, 3)
                    second(n, 2)
                    key(n, 4)
                    act.wait_ge(pe_x2t, n)
                    nc.scalar.activation(xt[:, 0, :], bank[0][:, 0:GT], ACT.Identity,
                                         scale=prog.w("ln2_g")[:, 0:1], bias=prog.w("ln2_b")[:, 0:1]
                                         ).then_inc(x2t_ready, 1)
                    second(n, 3)
                    key(n, 5)
                    second(n, 4)
                    for m in range(NM):
                        if m == 2:
                            second(n, 5)
                        if m == 4:
                            key(n, 6)
                        act.wait_ge(pe_up[m], n)
                        if m == 0:
                            earlier(act, pe_down, n)
                        nc.scalar.activation(up[:, m, :], bank[2 + m % 4][:, 0:GT], ACT.Silu,
                                             bias=prog.w("b_mlp1")[:, m:m + 1]).then_inc(a_up[m], 1)
                    second(n, 6)
                    key(n, 7)
                    second(n, 7)

                run(act, lambda n: None, step)

            @block.tensor
            def _(pe):
                def key(n, u):
                    l, s = u % 2, (u // 2) % 2
                    if l == 0:
                        pe.wait_ge(ctx_in[s], n * (G // 2 * 16) + (u // 4 + 1 - G // 2) * 16)
                    wait_unit(pe, a_key, n, u, 1)
                    for m in range(KD):
                        for k in range(KD):
                            ins = nc.tensor.matmul(bank[6 + m][:, 0:S2],
                                                   prog.w(f"{LAYERS[l][1]}_wk", KD)[:, k, m * P:(m + 1) * P],
                                                   ctx[s][:, k, :], start=(k == 0), stop=(k == KD - 1))
                    ins.then_inc(pe_key, 1)

                def transpose_rows(done):
                    for c in range(KD):
                        for j in range(G):
                            ins = nc.tensor.transpose(bank[c][:, j * T:(j + 1) * T],
                                                      xh[:, j, c * P:(c + 1) * P], ident[0:T, 0:T])
                    ins.then_inc(done, 1)

                def step(n, n_next):
                    pe.wait_ge(v_norm[1], n)
                    earlier(pe, v_out, n)
                    transpose_rows(pe_xt)
                    key(n, 0)
                    pe.wait_ge(xt_ready, n * 2)
                    for s, name in enumerate(("w_in", "w_in_swap")):
                        for k in range(KD):
                            ins = nc.tensor.matmul(bank[2 + s][:, 0:GT], prog.w(name, KD)[:, k, :], xt[:, k, :],
                                                   start=(k == 0), stop=(k == KD - 1))
                    ins.then_inc(pe_beta, 1)
                    for j in range(G):
                        for k in range(KD):
                            ins = nc.tensor.matmul(tok(bank[4:6], j), xt[:, k, j * T:(j + 1) * T],
                                                   prog.w("w_gate", KD)[:, k, :], start=(k == 0), stop=(k == KD - 1))
                    ins.then_inc(pe_gate, 1)
                    key(n, 1)
                    pe.wait_ge(v_states, n)
                    for j in range(G):
                        for s, states in enumerate((sa, sb_)):
                            ins = nc.tensor.matmul(tok(bank[2:4], j), states[:, j * T:(j + 1) * T],
                                                   prog.w_mix[:, s, :], start=(s == 0), stop=(s == 1))
                    ins.then_inc(pe_h, 1)
                    for u in (2, 3, 4):
                        key(n, u)
                    pe.wait_ge(v_norm[2], n)
                    transpose_rows(pe_x2t)
                    key(n, 5)
                    pe.wait_ge(x2t_ready, n * 2)
                    for m in range(NM):
                        if m == 6:
                            key(n, 6)
                        if m >= 4:
                            pe.wait_ge(a_up[m - 4], n)
                        for k in range(KD):
                            ins = nc.tensor.matmul(bank[2 + m % 4][:, 0:GT],
                                                   prog.w("w_mlp1", KD)[:, k, m * P:(m + 1) * P], xt[:, k, :],
                                                   start=(k == 0), stop=(k == KD - 1))
                        ins.then_inc(pe_up[m], 1)
                    key(n, 7)
                    for j in range(G):
                        for m in range(NM):
                            if j == 0:
                                pe.wait_ge(a_up[m], n)
                            ins = nc.tensor.matmul(tok(bank[0:2], j), up[:, m, j * T:(j + 1) * T],
                                                   prog.w("w_mlp2", NM)[:, m, :], start=(m == 0), stop=(m == NM - 1))
                    ins.then_inc(pe_down, 1)

                pe.wait_ge(prog.segment_in[1], 16)
                run(pe, lambda n: None, step)


def stage_queries(prog, layer, combine):
    nc = prog.nc
    with_keys = combine
    name = ("x0", "s", "x1")[layer]
    x_dram = prog.x_shared if combine else prog.x[(1, 3, 4)[layer]]
    KINDS = [("q", prog.q_stack[layer], Q_PARTS)]
    if with_keys:
        KINDS.append(("k", prog.k_stack[layer], K_PARTS))
    NK = len(KINDS)
    STORED = KD * len(Q_PARTS) * 16
    with stage(nc, f"queries{layer}") as (sem, sbuf, psum):
        x_in, v_stat, g_rstd, v_norm = sem("x_in"), sem("v_stat"), sem("g_rstd"), sem("v_norm")
        v_link, v_apart = [sem(f"v_link{k}") for k in range(2)], sem("v_apart")
        pe_xt, a_xt, v_xt = sem("pe_xt"), sem("a_xt"), sem("v_xt")
        pe_k = [sem(f"pe_{k[0]}") for k in KINDS]
        full_ready = [sem(f"full_ready_{k[0]}") for k in KINDS]
        v_turn = [sem(f"v_turn_{k[0]}") for k in KINDS]
        a_part1 = [sem(f"a_part1_{k[0]}") for k in KINDS]
        v_rest = [sem(f"v_rest_{k[0]}") for k in KINDS]
        a_part2 = [sem(f"a_part2_{k[0]}") for k in KINDS]
        v_part3 = [sem(f"v_part3_{k[0]}") for k in KINDS]
        stored = [sem(f"stored_{k[0]}") for k in KINDS]
        xt_stored, landed = sem("xt_stored"), sem("landed")

        xg = sbuf("xg", [T, G if combine else B, D])
        stats = sbuf("stats", [T, G, 6])
        mv = sbuf("mv", [T, G, 2])
        var = sbuf("var", [T, G])
        rstd = sbuf("rstd", [T, G])
        xh = sbuf("xh", [T, G, D])
        xt = sbuf("xt", [P, KD, GT])
        full = [sbuf(f"full_{k[0]}", [P, KD, GT]) for k in KINDS]
        turned = [sbuf(f"turned_{k[0]}", [P, KD, GT]) for k in KINDS] if with_keys else None
        rest = [sbuf(f"rest_{k[0]}", [P, KD, GT]) for k in KINDS]
        part = [sbuf(f"part_{k[0]}", [P, 3, KD, GT], BF16) for k in KINDS]
        bank = [psum(f"bank{k}", [P, 512]) for k in range(8)]
        if combine:
            got = sbuf("got", [T, G, TOPK, D])
            left = sbuf("left", [T, G, D])
            gate = sbuf("gate", [T, G, TOPK])
            got_in = [sem(f"got_in{j}") for j in range(G)]
            v_add = [[sem(f"v_add{j}_{k}") for k in range(TOPK)] for j in range(2)]
            v_gate, x_stored = sem("v_gate"), sem("x_stored")

        def banks_of(kind, rot, m):
            return bank[(2 + 4 * kind + 2 * rot + m) % 8][:, 0:GT]

        def earlier(engine, semaphore, n, per=1):
            if not (isinstance(n, int) and n == 1):
                engine.wait_ge(semaphore, n * per - per)

        def run(engine, front, step):
            front(1)
            step(1, 2)
            with engine.Fori(2, NG) as i:
                step(i, i + 1)
            step(NG, None)

        def group(dram, n):
            return dram[bass.ds((n - 1) * G, G)].rearrange("g t d -> t g d")

        with nc.Block() as block:
            @block.sync
            def _(sp):
                def made(n):
                    if combine:
                        sp.wait_ge(v_add[1][TOPK - 1], n)
                        sp.dma_start(group(prog.x[3], n), xg[:]).then_inc(x_stored, 16)

                def step(n, n_next):
                    if with_keys:
                        sp.wait_ge(a_xt, n)
                        sp.wait_ge(v_xt, n)
                        for k in range(KD):
                            sp.dma_start(prog.xn_t[bass.ds((n - 1) * G, G), :, k].rearrange("g p t -> p g t"),
                                         xt[:, k, :].rearrange("p (g t) -> p g t", g=G)).then_inc(xt_stored, 16)
                    if n_next is not None:
                        made(n_next)
                    for c, (_, stack, parts) in enumerate(KINDS):
                        sp.wait_ge(v_part3[c], n)
                        for m in range(KD):
                            for k, at, end, by in parts:
                                places = stack[m, at:end:by, :, bass.ds((n - 1) * G, G)].rearrange("g p b t -> p g (b t)")
                                sp.dma_start(places, part[c][:, k, m].unsqueeze(1).broadcast_to(places.shape)
                                             ).then_inc(stored[c], 16)

                if not combine:
                    with sp.Fori(1, NG + 1) as i:
                        sp.dma_start(xg[:, bass.ds((i - 1) * G, G), :], group(x_dram, i)).then_inc(x_in, 16)
                        sp.wait_ge(x_in, i * 16)
                        sp.sem_inc(landed, 1)
                run(sp, made, step)
                for c in range(NK):
                    sp.wait_ge(stored[c], NG * STORED)
                if with_keys:
                    sp.wait_ge(xt_stored, NG * (KD * 16))
                if combine:
                    sp.wait_ge(x_stored, NG * 16)

            @block.vector
            def _(ve):
                def add_experts(n):
                    if not combine:
                        return
                    earlier(ve, v_add[1][TOPK - 1], n)
                    nc.vector.tensor_copy(gate[:], prog.choice_gate[:, bass.ds((n - 1) * G, G), :]).then_inc(v_gate, 1)
                    ve.wait_ge(v_gate, n)
                    earlier(ve, x_stored, n, 16)
                    earlier(ve, v_norm, n)
                    ve.wait_ge(x_in, n * 16)
                    for j0 in range(0, G, 2):
                        for j in (j0, j0 + 1):
                            ve.wait_ge(got_in[j], n * (16 * TOPK))
                        for k in range(TOPK):
                            for j in (j0, j0 + 1):
                                ins = nc.vector.scalar_tensor_tensor(
                                    xg[:, j, :], got[:, j, k, :], gate[:, j, k:k + 1],
                                    left[:, j, :] if k == 0 else xg[:, j, :], ALU.mult, ALU.add)
                            ins.then_inc(v_add[j0 // 2][k], 1)
                            ve.wait_ge(v_add[j0 // 2][k], n)

                def x_of(n, j):
                    if combine:
                        return xg[:, j, :]
                    return xg[:, bass.ds(n * G + (j - G), 1), :].rearrange("t b d -> t (b d)")

                def moments(n):
                    ve.wait_ge(x_in, n * 16)
                    ve.sem_inc(v_apart, 1)
                    for j in range(G):
                        ins = nc.vector.bn_stats(stats[:, j, :], x_of(n, j))
                    ins.then_inc(v_link[0], 1)
                    ve.wait_ge(v_link[0], n)
                    ve.sem_inc(v_apart, 1)
                    for j in range(G):
                        ins = nc.vector.bn_aggr(mv[:, j, :], stats[:, j, :])
                    ins.then_inc(v_link[1], 1)
                    ve.wait_ge(v_link[1], n)
                    nc.vector.tensor_scalar(var[:], mv[:, :, 1], EPS, None, ALU.add).then_inc(v_stat, 1)

                def normalise(n):
                    ve.wait_ge(g_rstd, n)
                    for j in range(G):
                        ins = nc.vector.tensor_scalar(xh[:, j, :], x_of(n, j), mv[:, j, 0:1], rstd[:, j:j + 1],
                                                      ALU.subtract, ALU.mult)
                    ins.then_inc(v_norm, 1)

                def turn(n):
                    ve.wait_ge(pe_xt, n)
                    if with_keys:
                        earlier(ve, xt_stored, n, KD * 16)
                    nc.vector.tensor_copy(xt[:, 1, :], bank[1][:, 0:GT]).then_inc(v_xt, 1)

                def biased(n, c):
                    kind = KINDS[c][0]
                    ve.wait_ge(pe_k[c], n)
                    earlier(ve, v_part3[c], n)
                    for m in range(KD):
                        if not with_keys:
                            ins = nc.vector.tensor_scalar(full[c][:, m, :], banks_of(c, 0, m),
                                                          prog.w(f"{name}_b{kind}")[:, m:m + 1], None, ALU.add)
                            continue
                        for rot, (dst, table) in enumerate(((full[c], "rope_cos"), (turned[c], "rope_sin"))):
                            bias = prog.w(f"{name}_b{kind}" + ("_rot" if rot else ""))[:, m:m + 1]
                            ins = nc.vector.scalar_tensor_tensor(
                                dst[:, m, :].rearrange("p (g t) -> p g t", g=G),
                                banks_of(c, rot, m).rearrange("p (g t) -> p g t", g=G), bias,
                                prog.w(table).unsqueeze(1).broadcast_to([P, G, T]), ALU.add, ALU.mult)
                    if with_keys:
                        ins.then_inc(v_turn[c], 1)
                        ve.wait_ge(v_turn[c], n)
                        ins = nc.vector.tensor_tensor(full[c][:], full[c][:], turned[c][:], ALU.add)
                    ins.then_inc(full_ready[c], 1)

                def rest_of(n, c):
                    ve.wait_ge(a_part1[c], n)
                    nc.vector.tensor_tensor(rest[c][:], full[c][:], part[c][:, 0], ALU.subtract).then_inc(v_rest[c], 1)

                def third(n, c):
                    ve.wait_ge(a_part2[c], n)
                    nc.vector.tensor_tensor(part[c][:, 2], rest[c][:], part[c][:, 1], ALU.subtract
                                            ).then_inc(v_part3[c], 1)

                def front(n):
                    add_experts(n)
                    moments(n)
                    normalise(n)
                    turn(n)

                def step(n, n_next):
                    if n_next is not None:
                        add_experts(n_next)
                        moments(n_next)
                        if not combine:
                            normalise(n_next)
                    biased(n, 0)
                    if combine:
                        if n_next is not None:
                            normalise(n_next)
                        biased(n, 1)
                    for c in range(NK):
                        rest_of(n, c)
                    if not combine and n_next is not None:
                        turn(n_next)
                    third(n, 0)
                    if combine:
                        if n_next is not None:
                            turn(n_next)
                        third(n, 1)

                run(ve, front, step)

            @block.gpsimd
            def _(g):
                def gather(n, half):
                    for j in (2 * half, 2 * half + 1):
                        if n > 1:
                            g.wait_ge(v_add[j // 2][TOPK - 1], n - 1)
                        for k in range(TOPK):
                            g.indirect_dma_start(
                                got[:, j, k, :], None, prog.expert_out[0],
                                bass.IndirectOffsetOnAxis(prog.choice_row[:, (n - 1) * G + j, k:k + 1], 0)
                            ).then_inc(got_in[j], 16)

                def load(n):
                    if n > 1:
                        g.wait_ge(v_add[1][0], n - 1)
                    g.dma_start(left[:], group(x_dram, n)).then_inc(x_in, 16)

                def root(n):
                    g.wait_ge(v_stat, n)
                    nc.gpsimd.tensor_tensor(rstd[:], var[:], prog.half_neg[0:T, :], ALU.pow).then_inc(g_rstd, 1)

                if combine:
                    load(1)
                    gather(1, 0)
                    gather(1, 1)
                    for n in range(1, NG):
                        gather(n + 1, 0)
                        root(n)
                        load(n + 1)
                        gather(n + 1, 1)
                    root(NG)
                else:
                    with g.Fori(1, NG + 1) as i:
                        root(i)

            @block.scalar
            def _(act):
                def turn(n):
                    act.wait_ge(pe_xt, n)
                    if with_keys:
                        earlier(act, xt_stored, n, KD * 16)
                    nc.scalar.copy(xt[:, 0, :], bank[0][:, 0:GT]).then_inc(a_xt, 1)

                def step(n, n_next):
                    for c in range(NK):
                        act.wait_ge(full_ready[c], n)
                        earlier(act, stored[c], n, STORED)
                        nc.scalar.copy(part[c][:, 0], full[c][:]).then_inc(a_part1[c], 1)
                    for c in range(NK):
                        act.wait_ge(v_rest[c], n)
                        nc.scalar.copy(part[c][:, 1], rest[c][:]).then_inc(a_part2[c], 1)
                    if n_next is not None:
                        turn(n_next)

                run(act, turn, step)

            @block.tensor
            def _(pe):
                def turn(n):
                    pe.wait_ge(v_norm, n)
                    if with_keys:
                        earlier(pe, v_turn[1], n)
                    for c in range(KD):
                        for j in range(G):
                            ins = nc.tensor.transpose(bank[c][:, j * T:(j + 1) * T], xh[:, j, c * P:(c + 1) * P],
                                                      prog.w("ident")[0:T, 0:T])
                    ins.then_inc(pe_xt, 1)

                def step(n, n_next):
                    pe.wait_ge(a_xt, n)
                    pe.wait_ge(v_xt, n)
                    for c, (kind, _, _) in enumerate(KINDS):
                        earlier(pe, full_ready[c], n)
                        for rot in range(2 if with_keys else 1):
                            weights = prog.w(f"{name}_w{kind}" + ("_rot" if rot else ""), KD)
                            for m in range(KD):
                                for k in range(KD):
                                    ins = nc.tensor.matmul(banks_of(c, rot, m), weights[:, k, m * P:(m + 1) * P],
                                                           xt[:, k, :], start=(k == 0), stop=(k == KD - 1))
                        ins.then_inc(pe_k[c], 1)
                    if n_next is not None:
                        turn(n_next)

                run(pe, turn, step)


def stage_attention(prog, layer):
    nc = prog.nc
    name = ("x0", "s", "x1")[layer]
    masked = layer == 2
    NK = (S2, T, S2)[layer]
    x_dram, out_dram = prog.x[(1, 3, 4)[layer]], prog.x[(2, 4, 5)[layer]]
    v_src = prog.xn_t if layer == 1 else prog.ins["ctx_t"]
    NKT = -(-NK // P)
    size = -(-NK // NKT)
    KEYS = [(k * size, min(size, NK - k * size)) for k in range(NKT)]
    HB = min(512 // NK, 4)
    NU = H // (2 * HB)
    NQ = H // G
    NPU = NQ * NKT
    HH = H // 2
    at_unit = {-(-(u + 1) * (NPU - (NKT > 1)) // NU) - 1: u for u in range(NU)}
    shift_by_vector = layer == 1
    if NKT > 1:
        LAST_AV, SHIFT_B, ROWS, TURN, OUT, SHIFT_A = 1, 2, 3, 5, 7, 9
        av_at = {3 * g + 4: g for g in range(NQ - 1)}
    else:
        LAST_AV, SHIFT_B, ROWS, TURN, OUT, SHIFT_A = 0, 0, 1, 2, 3, 3
        av_at = {g + 1: g for g in range(NQ - 1)}

    with stage(nc, f"attn{layer}") as (sem, sbuf, psum):
        def pair(label):
            return [sem(f"{label}{s}") for s in range(2)]

        half_in = [pair(f"half_in{h}_") for h in range(2)]
        src_in, x_in, mask_in = pair("src_in"), pair("x_in"), pair("mask_in")
        g_base, g_mask = pair("g_base"), pair("g_mask")
        pe_score, v_max = pair("pe_score"), pair("v_max")
        v_split = [pair(f"v_split{h}_") for h in range(2)]
        pe_shift = [pair(f"pe_shift{h}_") for h in range(2)]
        v_shift = [pair(f"v_shift{h}_") for h in range(2)]
        g_shift = [pair(f"g_shift{h}_") for h in range(2)]
        pe_val, v_val = pair("pe_val"), pair("v_val")
        pe_prob, a_prob = pair("pe_prob"), pair("a_prob")
        pe_av = pair("pe_av")
        a_acc = pair("a_acc")
        pe_rows, v_rows, pe_turn, v_turn, pe_out, v_out = (
            pair(n) for n in ("pe_rows", "v_rows", "pe_turn", "v_turn", "pe_out", "v_out"))
        v_link = [pair(f"v_link{k}_") for k in range(6)]
        stored, out_free = pair("stored"), pair("out_free")
        consts_set = sem("consts_set")
        ones_set = sem("ones_set")
        g_order = sem("g_order")

        q_sb = [sbuf(f"q{s}", [P, 2, HH, T], BF16) for s in range(2)]
        k_sb = [sbuf(f"k{s}", [P, 2, HH, NK], BF16) for s in range(2)]
        src = [sbuf(f"src{s}", [P, KD, NK]) for s in range(2)]
        xin = [sbuf(f"xin{s}", [T, D]) for s in range(2)]
        base = [sbuf(f"base{s}", [T, D]) for s in range(2)]
        xo = [sbuf(f"xo{s}", [T, D]) for s in range(2)]
        val = [sbuf(f"val{s}", [P, NKT, H, 2 * DH]) for s in range(2)]
        prob = sbuf("prob", [P, 2, NKT, GT])
        nmax = [sbuf(f"nmax{s}", [T, H]) for s in range(2)]
        split = [[sbuf(f"split{h}_{s}", [T, 2, H], BF16) for s in range(2)] for h in range(2)]
        shift = [sbuf(f"shift{h}", [P, T], BF16) for h in range(2)]
        acc = sbuf("acc", [P, GT])
        rden = sbuf("rden", [T, H])
        rows = sbuf("rows", [T, H, DH])
        turned = sbuf("turned", [P, KD, T])
        if masked:
            mask8 = [sbuf(f"mask8_{s}", [T, NK], U8) for s in range(2)]
            mask = [sbuf(f"mask{s}", [T, NK], BF16) for s in range(2)]
        ps_score = psum("ps_score", [P, 4, 512])
        ps_prob = [psum(f"ps_prob{k}", [P, 512]) for k in range(2)]
        ps_acc = psum("ps_acc", [P, 512])
        ps_misc = psum("ps_misc", [P, 512])
        ident, ident_b = prog.w("ident"), prog.c("ident_b")

        def seq(s, n):
            return n * 2 + (s - 2)

        def run(engine, head, step, tail):
            head(0, 1, None)
            step(0, 1, None, 1)
            with engine.Fori(1, 7) as i:
                step(1, i, i, i + 1)
                step(0, i + 1, i, i + 1)
            step(1, 7, 7, 8)
            step(0, 8, 7, 8)
            step(1, 8, 8, None)
            tail(1, 8)

        with nc.Block() as block:
            @block.sync
            def _(sp):
                def load_half(s, n, h):
                    b = seq(s, n)
                    for dst, stack, of_context in ((q_sb[s], prog.q_stack[layer], False),
                                                   (k_sb[s], prog.k_stack[layer], layer != 1)):
                        rows_of = (stack[bass.ds(b, 1), :, :, h].rearrange("b g (d h) n -> (b g d) h n", h=HH)
                                   if of_context else
                                   stack[h, :, :, bass.ds(b, 1)].rearrange("g (d h) b t -> (g d) h (b t)", h=HH))
                        sp.dma_start(dst[0:SHIFT_ROW, h], rows_of).then_inc(half_in[h][s], 16)

                def load_src(s, n):
                    sp.dma_start(src[s][:], v_src[bass.ds(seq(s, n), 1)].rearrange("b p k n -> p (b k) n")
                                 ).then_inc(src_in[s], 16)

                def load_x(s, n):
                    sp.dma_start(xin[s][:], x_dram[bass.ds(seq(s, n), 1)].rearrange("b t d -> t (b d)")
                                 ).then_inc(x_in[s], 16)

                def load_mask(s, n):
                    sp.dma_start(mask8[s][:], prog.ins["mask"][bass.ds(seq(s, n), 1)].rearrange("b t n -> t (b n)")
                                 ).then_inc(mask_in[s], 16)

                def store(s, n):
                    sp.wait_ge(v_out[s], n)
                    sp.dma_start(out_dram[bass.ds(seq(s, n), 1)].rearrange("b t d -> t (b d)"), xo[s][:]
                                 ).then_inc(stored[s], 16)
                    sp.wait_ge(stored[s], n * 16)
                    sp.sem_inc(out_free[s], 1)

                def step(s, n, n_prev, n_next, more=True):
                    if more:
                        if masked:
                            sp.wait_ge(g_mask[s], n)
                            load_mask(s, n + 1)
                        sp.wait_ge(pe_val[s], n * NKT)
                        load_src(s, n + 1)
                        sp.wait_ge(g_base[s], n)
                        load_x(s, n + 1)
                        sp.wait_ge(pe_prob[s], n * NPU - NPU // 2)
                        load_half(s, n + 1, 0)
                    if n_prev is not None:
                        store(1 - s, n_prev)
                    if more:
                        sp.wait_ge(pe_prob[s], n * NPU)
                        load_half(s, n + 1, 1)

                for s in range(2):
                    sp.sem_inc(out_free[s], 1)
                    load_half(s, 1, 0)
                    if masked:
                        load_mask(s, 1)
                    load_half(s, 1, 1)
                    load_src(s, 1)
                    load_x(s, 1)
                step(0, 1, None, 1)
                with sp.Fori(1, 7) as i:
                    step(1, i, i, i + 1)
                    step(0, i + 1, i, i + 1)
                step(1, 7, 7, 8)
                step(0, 8, 7, 8, more=False)
                step(1, 8, 8, None, more=False)
                store(1, 8)

            @block.tensor
            def _(pe):
                def score_unit(s, n, u, n_cur):
                    if u == 0 or u == NU // 2:
                        pe.wait_ge(half_in[2 * u // NU][s], n * 32)
                    if u == 0 and masked:
                        pe.wait_ge(g_mask[s], n)
                    if u >= 2:
                        pe.wait_ge(v_max[s], n * NU - NU + u - 1)
                    elif n_cur is not None:
                        pe.wait_ge(v_val[1 - s], n_cur)
                    for j in range(2):
                        for hh in range(HB):
                            h = (u * 2 + j) * HB + hh
                            out = ps_score[0:T, (u % 2) * 2 + j, hh * NK:(hh + 1) * NK]
                            if masked:
                                nc.tensor.matmul(out, prog.c("big_diag")[0:T, 0:T], mask[s][:], start=True, stop=False)
                            ins = nc.tensor.matmul(out, q_sb[s][0:SHIFT_ROW, h // HH, h % HH, :],
                                                   k_sb[s][0:SHIFT_ROW, h // HH, h % HH, :],
                                                   start=not masked, stop=True)
                    ins.then_inc(pe_score[s], 1)

                def values(s, n):
                    pe.wait_ge(src_in[s], n * 16)
                    for t, (at, rows_) in enumerate(KEYS):
                        if t % 2 == 0:
                            pe.wait_ge(v_max[s], n * NU - (1 if len(KEYS) > 2 and t < 2 else 0))
                        for k in range(KD):
                            ins = nc.tensor.matmul(ps_score[0:rows_, t, 0:D], src[s][:, k, at:at + rows_],
                                                   prog.w(f"{name}_wv", KD)[:, k, :], start=(k == 0), stop=(k == KD - 1))
                        ins.then_inc(pe_val[s], 1)

                def shift_rows(s, n, h):
                    pe.wait_ge(v_split[h][s], n)
                    nc.tensor.transpose(ps_misc[:].bitcast(BF16)[SHIFT_ROW:P, 0:T],
                                        split[h][s][:].rearrange("t a h -> t (a h)"), ident_b[0:T, 0:T]
                                        ).then_inc(pe_shift[h][s], 1)

                def prob_unit(s, n, k, n_prev):
                    q4, t = k // NKT, k % NKT
                    at, rows_ = KEYS[t]
                    if k % (NPU // 2) == 0:
                        if isinstance(n, int):
                            pe.wait_ge(ones_set, 2)
                        pe.wait_ge((v_shift if shift_by_vector else g_shift)[2 * k // NPU][s], n)
                    if k >= 2:
                        pe.wait_ge(a_prob[s], n * NPU - NPU + k - 1)
                    elif n_prev is not None:
                        pe.wait_ge(a_prob[1 - s], n_prev * NPU + k - 1)
                    out = ps_prob[k % 2]
                    if masked:
                        nc.tensor.matmul(out[0:rows_, 0:GT], mask[s][:, at:at + rows_], prog.c("big_diag")[0:T, :],
                                         start=True, stop=False)
                    for j in range(G):
                        h = q4 * G + j
                        ins = nc.tensor.matmul(out[0:rows_, j * T:(j + 1) * T],
                                               k_sb[s][:, h // HH, h % HH, at:at + rows_],
                                               q_sb[s][:, h // HH, h % HH, :], start=not masked,
                                               stop=not masked or j == G - 1)
                    ins.then_inc(pe_prob[s], 1)

                def weigh_values(s, n, q4, n_prev):
                    if q4 == 0:
                        pe.wait_ge(v_val[s], n)
                        if n_prev is not None:
                            pe.wait_ge(a_acc[1 - s], n_prev)
                    for t, (_, rows_) in enumerate(KEYS):
                        pe.wait_ge(a_prob[s], n * NPU + (q4 * NKT + t + 1 - NPU))
                        for j in range(G):
                            ins = nc.tensor.matmul(ps_acc[32 * j:32 * j + 32, q4 * T:(q4 + 1) * T],
                                                   val[s][0:rows_, t, q4 * G + j, :],
                                                   prob[0:rows_, q4 % 2, t, j * T:(j + 1) * T],
                                                   start=(t == 0), stop=(t == NKT - 1))
                    ins.then_inc(pe_av[s], 1)

                def to_rows(s, n):
                    pe.wait_ge(a_acc[s], n)
                    for q4 in range(NQ):
                        ins = nc.tensor.transpose(ps_misc[0:T, q4 * P:(q4 + 1) * P], acc[:, q4 * T:(q4 + 1) * T], ident)
                    ins.then_inc(pe_rows[s], 1)

                def turn(s, n):
                    pe.wait_ge(v_rows[s], n)
                    for k in range(KD):
                        ins = nc.tensor.transpose(ps_misc[:, k * T:(k + 1) * T],
                                                  rows[:].rearrange("t h d -> t (h d)")[:, k * P:(k + 1) * P],
                                                  ident[0:T, 0:T])
                    ins.then_inc(pe_turn[s], 1)

                def project(s, n):
                    pe.wait_ge(v_turn[s], n)
                    for k in range(KD):
                        ins = nc.tensor.matmul(ps_misc[0:T, 0:D], turned[:, k, :], prog.w(f"{name}_wo", KD)[:, k, :],
                                               start=(k == 0), stop=(k == KD - 1))
                    ins.then_inc(pe_out[s], 1)

                def head(s, n, n_cur):
                    for u in range(NU):
                        score_unit(s, n, u, n_cur)
                    shift_rows(s, n, 0)
                    values(s, n)

                def step(s, n, n_prev, n_next):
                    for k in range(NPU):
                        prob_unit(s, n, k, n_prev)
                        if k == LAST_AV and n_prev is not None:
                            weigh_values(1 - s, n_prev, NQ - 1, None)
                        if k in av_at:
                            weigh_values(s, n, av_at[k], n_prev)
                        if k == SHIFT_B:
                            pe.wait_ge(v_shift[0][s], n)
                            shift_rows(s, n, 1)
                        if n_prev is not None:
                            if k == ROWS:
                                pe.wait_ge(v_shift[1][s], n)
                                to_rows(1 - s, n_prev)
                            if k == TURN:
                                turn(1 - s, n_prev)
                            if k == OUT:
                                project(1 - s, n_prev)
                        if n_next is not None:
                            if k in at_unit:
                                score_unit(1 - s, n_next, at_unit[k], n)
                            if k == SHIFT_A:
                                if n_prev is not None:
                                    pe.wait_ge(v_out[1 - s], n_prev)
                                else:
                                    pe.wait_ge(v_shift[1][s], n)
                                shift_rows(1 - s, n_next, 0)
                    if n_next is not None:
                        values(1 - s, n_next)

                def tail(s, n):
                    weigh_values(s, n, NQ - 1, None)
                    pe.wait_ge(v_out[1 - s], n)
                    to_rows(s, n)
                    turn(s, n)
                    project(s, n)

                pe.wait_ge(consts_set, 1)
                run(pe, head, step, tail)

            @block.scalar
            def _(act):
                def step(s, n, n_prev, n_next):
                    for k in range(NPU):
                        q4, t = k // NKT, k % NKT
                        rows_ = KEYS[t][1]
                        act.wait_ge(pe_prob[s], n * NPU - NPU + k + 1)
                        if t == 0:
                            if q4 >= 2:
                                act.wait_ge(pe_av[s], n * NQ - NQ + q4 - 1)
                            elif n_prev is not None:
                                act.wait_ge(pe_av[1 - s], n_prev * NQ + q4 - 1)
                        nc.scalar.activation(prob[0:rows_, q4 % 2, t, :], ps_prob[k % 2][0:rows_, 0:GT], ACT.Exp,
                                             scale=DH ** -0.5).then_inc(a_prob[s], 1)
                        if k == LAST_AV and n_prev is not None:
                            tail(1 - s, n_prev)

                def tail(s, n):
                    act.wait_ge(pe_av[s], n * NQ)
                    nc.scalar.copy(acc[:], ps_acc[:, 0:GT]).then_inc(a_acc[s], 1)

                run(act, lambda *a: None, step, tail)

            @block.vector
            def _(ve):
                def score_unit(s, n, u):
                    ve.wait_ge(pe_score[s], n * NU - NU + u + 1)
                    scores = ps_score[0:T, (u % 2) * 2:(u % 2) * 2 + 2, 0:HB * NK].rearrange("p b (h n) -> p b h n", h=HB)
                    nc.vector.tensor_reduce(nmax[s][:, u * 2 * HB:(u + 1) * 2 * HB].rearrange("p (b h) -> p b h", b=2),
                                            scores, AX.X, ALU.max, negate=True).then_inc(v_max[s], 1)
                    if (u + 1) % (NU // 2) == 0:
                        split_shift(s, n, (u + 1) * 2 // NU - 1)

                def split_shift(s, n, h):
                    here = nmax[s][:, h * HH:(h + 1) * HH]
                    ve.wait_ge(v_max[s], n * NU - NU + (h + 1) * NU // 2)
                    if masked:
                        nc.vector.tensor_scalar(here, here, -FLOOR, None, ALU.min).then_inc(v_link[h][s], 1)
                        ve.wait_ge(v_link[h][s], n)
                    nc.vector.tensor_copy(split[h][s][:, 0, h * HH:(h + 1) * HH], here).then_inc(v_link[2 + h][s], 1)
                    ve.wait_ge(v_link[2 + h][s], n)
                    nc.vector.tensor_tensor(split[h][s][:, 1, h * HH:(h + 1) * HH], here,
                                            split[h][s][:, 0, h * HH:(h + 1) * HH], ALU.subtract
                                            ).then_inc(v_split[h][s], 1)

                def shift_rows(s, n, h):
                    ve.wait_ge(pe_shift[h][s], n)
                    if shift_by_vector:
                        nc.vector.tensor_tensor(
                            q_sb[s][SHIFT_ROW:P, h],
                            ps_misc[:].bitcast(BF16)[SHIFT_ROW:P, 0:T].unsqueeze(1).broadcast_to([32, HH, T]),
                            prog.c("head_sel")[SHIFT_ROW:P, h * HH:(h + 1) * HH].unsqueeze(2).broadcast_to([32, HH, T]),
                            ALU.mult).then_inc(v_shift[h][s], 1)
                        return
                    nc.vector.tensor_copy(shift[h][SHIFT_ROW:P, :], ps_misc[:].bitcast(BF16)[SHIFT_ROW:P, 0:T]
                                          ).then_inc(v_shift[h][s], 1)

                def values(s, n):
                    for t, (_, rows_) in enumerate(KEYS):
                        ve.wait_ge(pe_val[s], n * NKT - (NKT - 1 - t))
                        ins = nc.vector.tensor_tensor(
                            val[s][0:rows_, t, :, 0:DH], ps_score[0:rows_, t, 0:D].rearrange("p (h d) -> p h d", h=H),
                            prog.w(f"{name}_bv_row")[0:rows_].rearrange("p (h d) -> p h d", h=H), ALU.add)
                    ins.then_inc(v_val[s], 1)

                def to_rows(s, n):
                    ve.wait_ge(pe_rows[s], n)
                    heads = ps_misc[0:T, :].rearrange("p (h d) -> p h d", h=H)
                    nc.vector.reciprocal(rden[:], heads[:, :, DH]).then_inc(v_link[4][s], 1)
                    ve.wait_ge(v_link[4][s], n)
                    nc.vector.tensor_tensor(rows[:], heads[:, :, 0:DH], rden[:].unsqueeze(2).broadcast_to([T, H, DH]),
                                            ALU.mult).then_inc(v_rows[s], 1)

                def turn(s, n):
                    ve.wait_ge(pe_turn[s], n)
                    nc.vector.tensor_copy(turned[:].rearrange("p k t -> p (k t)"), ps_misc[:, 0:KD * T]
                                          ).then_inc(v_turn[s], 1)

                def project(s, n):
                    ve.wait_ge(g_base[s], n)
                    ve.wait_ge(out_free[s], n)
                    ve.wait_ge(pe_out[s], n)
                    nc.vector.tensor_tensor(xo[s][:], ps_misc[0:T, 0:D], base[s][:], ALU.add).then_inc(v_out[s], 1)

                def head(s, n, _):
                    for u in range(NU):
                        score_unit(s, n, u)
                    shift_rows(s, n, 0)
                    values(s, n)

                def step(s, n, n_prev, n_next):
                    for k in range(NPU):
                        if k == SHIFT_B:
                            shift_rows(s, n, 1)
                        if n_prev is not None:
                            if k == ROWS:
                                to_rows(1 - s, n_prev)
                            if k == TURN:
                                turn(1 - s, n_prev)
                            if k == OUT:
                                project(1 - s, n_prev)
                        if n_next is not None:
                            if k in at_unit:
                                score_unit(1 - s, n_next, at_unit[k])
                            if k == SHIFT_A:
                                shift_rows(1 - s, n_next, 0)
                    if n_next is not None:
                        values(1 - s, n_next)

                def tail(s, n):
                    to_rows(s, n)
                    turn(s, n)
                    project(s, n)

                for s in range(2):
                    nc.vector.memset(val[s][:, :, :, DH:DH + 1], 1.0)
                    nc.vector.memset(val[s][:, :, :, DH + 1:], 0.0)
                    for h in range(2):
                        ins = nc.vector.memset(split[h][s][:], 0.0)
                ins.then_inc(consts_set, 1)
                ve.wait_ge(consts_set, 1)
                run(ve, head, step, tail)

            @block.gpsimd
            def _(g):
                def shift_rows(s, n, h, before):
                    if shift_by_vector:
                        return
                    g.wait_ge(*before)
                    g.wait_ge(v_shift[h][s], n)
                    nc.gpsimd.tensor_tensor(
                        q_sb[s][SHIFT_ROW:P, h], shift[h][SHIFT_ROW:P, :].unsqueeze(1).broadcast_to([32, HH, T]),
                        prog.c("head_sel")[SHIFT_ROW:P, h * HH:(h + 1) * HH].unsqueeze(2).broadcast_to([32, HH, T]),
                        ALU.mult).then_inc(g_shift[h][s], 1)

                def set_base(s, n, before):
                    if before is not None:
                        g.wait_ge(*before)
                    if not (isinstance(n, int) and n == 1):
                        g.wait_ge(v_out[s], n - 1)
                    g.wait_ge(x_in[s], n * 16)
                    nc.gpsimd.tensor_tensor(base[s][:], xin[s][:], prog.w(f"{name}_bo_row")[0:T], ALU.add
                                            ).then_inc(g_base[s], 1)

                def set_mask(s, n, n_prev, before):
                    if before is not None:
                        g.wait_ge(*before)
                    if n_prev is not None:
                        g.wait_ge(pe_prob[s], n_prev * NPU)
                    g.wait_ge(mask_in[s], n * 16)
                    g.sem_inc(g_order, 1)
                    nc.gpsimd.tensor_copy(mask[s][:], mask8[s][:]).then_inc(g_mask[s], 1)

                def head(s, n, _):
                    if masked:
                        set_mask(s, n, None, None)
                    set_base(s, n, (g_mask[s], n) if masked else None)
                    shift_rows(s, n, 0, (g_base[s], n))

                def step(s, n, n_prev, n_next):
                    masks = masked and n_next is not None
                    if masks:
                        set_mask(1 - s, n_next, n_prev, (g_shift[0][s], n))
                    shift_rows(s, n, 1, (g_mask[1 - s], n_next) if masks else (g_shift[0][s], n))
                    if n_next is not None:
                        set_base(1 - s, n_next, (g_base[s], n) if shift_by_vector else (g_shift[1][s], n))
                        shift_rows(1 - s, n_next, 0, (g_base[1 - s], n_next))

                for s in range(2):
                    nc.gpsimd.memset(k_sb[s][SHIFT_ROW:P], 1.0).then_inc(ones_set, 1)
                    g.wait_ge(ones_set, s + 1)
                run(g, head, step, lambda *a: None)


def stage_route0(prog):
    nc = prog.nc
    x_dram = prog.x[2]
    NM = HID // P
    NC_ = E0 + NGRP
    with stage(nc, "route0") as (sem, sbuf, psum):
        x_in, v_stat, g_rstd, v_norm = sem("x_in"), sem("v_stat"), sem("g_rstd"), sem("v_norm")
        v_link = [sem(f"v_link{k}") for k in range(30)]
        v_front = [sem(f"v_front{k}") for k in range(2)]
        pe_xt, a_xt, v_xt = sem("pe_xt"), sem("a_xt"), sem("v_xt")
        v_square, g_length = sem("v_square"), sem("g_length")
        pe_logits, v_logits = sem("pe_logits"), sem("v_logits")
        v_gap, a_exp = sem("v_gap"), sem("a_exp")
        v_hot, pe_pos, v_apart, v_rows = sem("v_hot"), sem("pe_pos"), sem("v_apart"), sem("v_rows")
        pe_up = [sem(f"pe_up{m}") for m in range(NM)]
        a_up = [sem(f"a_up{m}") for m in range(NM)]
        v_up = [sem(f"v_up{m}") for m in range(NM)]
        pe_down, v_out = sem("pe_down"), sem("v_out")
        rows_stored, stored, res_in, v_spread = sem("rows_stored"), sem("stored"), sem("res_in"), sem("v_spread")
        zero_set, zeroed, ids_set = sem("zero_set"), sem("zeroed"), sem("ids_set")
        scattered, g_ready = sem("scattered"), sem("g_ready")

        xg = sbuf("xg", [T, G, D])
        xr = sbuf("xr", [T, G, D])
        stats = sbuf("stats", [T, G, 6])
        mv = sbuf("mv", [T, G, 2])
        var = sbuf("var", [T, G])
        rstd = sbuf("rstd", [T, G])
        xf = sbuf("xf", [T, G, D])
        sq = sbuf("sq", [T, G, D])
        xt = sbuf("xt", [P, KD, GT])
        length = sbuf("length", [T, 4, G])
        sc = sbuf("sc", [T, G, NC_])
        gtop = sbuf("gtop", [T, G, 8])
        gidx = sbuf("gidx", [T, G, 8], U32)
        gidf = sbuf("gidf", [T, G, 8])
        geq = sbuf("geq", [T, G, 4, NGRP])
        gsel = sbuf("gsel", [T, G, NGRP])
        gneg = sbuf("gneg", [T, G, NGRP])
        es = sbuf("es", [T, G, E0])
        etop = sbuf("etop", [T, G, 8])
        eidx = sbuf("eidx", [T, G, 8], U32)
        eidf = sbuf("eidf", [T, G, 8])
        gap = sbuf("gap", [T, G, TOPK])
        esum = sbuf("esum", [T, 2, G])
        gates = sbuf("gates", [T, G, TOPK])
        hot = sbuf("hot", [T, G, TOPK, E0])
        any_hot = sbuf("any_hot", [T, G, E0], BF16)
        prior = sbuf("prior", [T, E0], BF16)
        prior_add = sbuf("prior_add", [T, E0])
        prod = sbuf("prod", [T, G, TOPK, E0])
        pos = sbuf("pos", [T, G, TOPK])
        keep = sbuf("keep", [T, G, TOPK])
        rowf = sbuf("rowf", [T, 2, G, TOPK])
        row_put = sbuf("row_put", [T, G * TOPK], I32)
        spare = sbuf("spare", [T, G * TOPK])
        ids = sbuf("ids", [T, B], I32)
        ids_now = sbuf("ids_now", [T, G], I32)
        zeros = sbuf("zeros", [T, SLOTS0 // T], I32)
        act_ = sbuf("act_", [P, NM, GT])
        up = sbuf("up", [P, NM, GT])
        xo = sbuf("xo", [T, G, D])
        bank = [psum(f"bank{k}", [P, 512]) for k in range(8)]
        LEFT = [4, 6]

        def earlier(engine, semaphore, n, per=1):
            if not (isinstance(n, int) and n == 1):
                engine.wait_ge(semaphore, n * per - per)

        def run(engine, front, step):
            front(1)
            step(1, 2)
            with engine.Fori(2, NG) as i:
                step(i, i + 1)
            step(NG, None)

        def group(dram, n):
            return dram[bass.ds((n - 1) * G, G)].rearrange("g t d -> t g d")

        with nc.Block() as block:
            @block.sync
            def _(sp):
                sp.wait_ge(zero_set, 1)
                sp.dma_start(prog.row_token[0:SLOTS0].rearrange("(p n) o -> p (n o)", p=T), zeros[:]).then_inc(zeroed, 16)

                def front(n):
                    earlier(sp, v_norm, n)
                    sp.dma_start(xg[:], group(x_dram, n)).then_inc(x_in, 16)
                    sp.wait_ge(v_norm, n)
                    sp.dma_start(group(prog.ln_rows.rearrange("(b t) d -> b t d", t=T), n), xf[:]
                                 ).then_inc(rows_stored, 16)

                def step(n, n_next):
                    earlier(sp, v_out, n)
                    sp.dma_start(xr[:], group(x_dram, n)).then_inc(res_in, 16)
                    if n_next is not None:
                        front(n_next)
                    sp.wait_ge(v_out, n)
                    sp.dma_start(group(prog.x_shared, n), xo[:]).then_inc(stored, 16)

                run(sp, front, step)
                sp.wait_ge(rows_stored, NG * 16)
                sp.wait_ge(stored, NG * 16)

            @block.gpsimd
            def _(g):
                def front(n):
                    g.wait_ge(v_stat, n)
                    nc.gpsimd.tensor_tensor(rstd[:], var[:], prog.half_neg[0:T, :], ALU.pow).then_inc(g_rstd, 1)
                    g.wait_ge(v_square, n)
                    nc.gpsimd.tensor_tensor(length[:, 1, :], length[:, 0, :], length[:, 3, :], ALU.pow
                                            ).then_inc(g_length, 1)

                def step(n, n_next):
                    if n_next is not None:
                        front(n_next)
                    g.wait_ge(v_rows, n)
                    g.sem_inc(g_ready, 1)
                    for c in range(G * TOPK):
                        g.indirect_dma_start(prog.row_token, bass.IndirectOffsetOnAxis(row_put[:, c:c + 1], 0),
                                             ids_now[:, c // TOPK:c // TOPK + 1], None).then_inc(scattered, 16)

                g.wait_ge(zeroed, 16)
                run(g, front, step)
                g.wait_ge(scattered, NG * (16 * G * TOPK))

            @block.vector
            def _(ve):
                nc.vector.memset(zeros[:], 0).then_inc(zero_set, 1)
                nc.vector.memset(length[:, 3, :], 0.5)
                nc.vector.memset(prior[:], 0.0)
                nc.vector.tensor_copy(ids[:], prog.w("tok_id")[0:T]).then_inc(ids_set, 1)
                ve.wait_ge(ids_set, 1)

                def front(n):
                    ve.wait_ge(x_in, n * 16)
                    ve.sem_inc(v_apart, 1)
                    for j in range(G):
                        ins = nc.vector.bn_stats(stats[:, j, :], xg[:, j, :])
                    ins.then_inc(v_front[0], 1)
                    ve.wait_ge(v_front[0], n)
                    ve.sem_inc(v_apart, 1)
                    for j in range(G):
                        ins = nc.vector.bn_aggr(mv[:, j, :], stats[:, j, :])
                    ins.then_inc(v_front[1], 1)
                    ve.wait_ge(v_front[1], n)
                    nc.vector.tensor_scalar(var[:], mv[:, :, 1], EPS, None, ALU.add).then_inc(v_stat, 1)
                    ve.wait_ge(g_rstd, n)
                    earlier(ve, rows_stored, n, 16)
                    for j in range(G):
                        ins = nc.vector.tensor_scalar(xf[:, j, :], xg[:, j, :], mv[:, j, 0:1], rstd[:, j:j + 1],
                                                      ALU.subtract, ALU.mult)
                    ins.then_inc(v_norm, 1)
                    ve.wait_ge(v_norm, n)
                    for j in range(G):
                        ins = nc.vector.tensor_tensor_reduce(sq[:, j, :], xf[:, j, :], xf[:, j, :], 1.0, 0.0, ALU.mult,
                                                             ALU.add, length[:, 0, j:j + 1])
                    ins.then_inc(v_square, 1)

                def turn(n):
                    ve.wait_ge(pe_xt, n)
                    nc.vector.tensor_copy(xt[:, 1, :], bank[1][:, 0:GT]).then_inc(v_xt, 1)

                def step(n, n_next):
                    used = [0]

                    def link(ins):
                        ins.then_inc(v_link[used[0]], 1)
                        ve.wait_ge(v_link[used[0]], n)
                        used[0] += 1

                    def link_apart(ins):
                        link(ins)
                        ve.sem_inc(v_apart, 1)

                    def gated(m):
                        ve.wait_ge(a_up[m], n)
                        nc.vector.tensor_tensor(up[:, m, :], act_[:, m, :], bank[LEFT[m % 2] + 1][:, 0:GT], ALU.mult
                                                ).then_inc(v_up[m], 1)

                    ve.wait_ge(g_length, n)
                    link(nc.vector.tensor_scalar(length[:, 2, :], length[:, 1, :], 1e-12, None, ALU.max))
                    link(nc.vector.reciprocal(length[:, 2, :], length[:, 2, :]))
                    ve.wait_ge(pe_logits, n)
                    link_apart(nc.vector.tensor_tensor(sc[:], bank[2][0:T, 0:G * NC_].rearrange("p (g c) -> p g c", g=G),
                                                 length[:, 2, :].unsqueeze(2).broadcast_to([T, G, NC_]), ALU.mult))
                    for j in range(G):
                        ins = nc.vector.max(gtop[:, j, :], sc[:, j, E0:NC_])
                    link_apart(ins)
                    for j in range(G):
                        ins = nc.vector.max_index(gidx[:, j, :], gtop[:, j, :], sc[:, j, E0:NC_])
                    link(nc.vector.tensor_tensor(
                        es[:], sc[:, :, 0:E0], prog.w("f0_bias_row")[0:T].unsqueeze(1).broadcast_to([T, G, E0]), ALU.add))
                    link(nc.vector.tensor_copy(gidf[:], gidx[:]))
                    link(nc.vector.tensor_tensor(
                        geq[:], prog.w("iota_e")[0:T, 0:NGRP].unsqueeze(1).unsqueeze(1).broadcast_to([T, G, 4, NGRP]),
                        gidf[:, :, 0:4].unsqueeze(3).broadcast_to([T, G, 4, NGRP]), ALU.is_equal))
                    link(nc.vector.tensor_reduce(gsel[:], geq[:].rearrange("p g k n -> p g n k"), AX.X, ALU.add))
                    per_group = "p g (n e) -> p (g n) e"
                    nc.vector.tensor_scalar(gneg[:], gsel[:], 1e9, -1e9, ALU.mult, ALU.add)
                    link(nc.vector.tensor_tensor(
                        es[:].rearrange(per_group, n=NGRP), es[:].rearrange(per_group, n=NGRP),
                        gsel[:].rearrange("p g n -> p (g n)").unsqueeze(2).broadcast_to([T, G * NGRP, E0 // NGRP]),
                        ALU.mult))
                    link_apart(nc.vector.tensor_tensor(
                        es[:].rearrange(per_group, n=NGRP), es[:].rearrange(per_group, n=NGRP),
                        gneg[:].rearrange("p g n -> p (g n)").unsqueeze(2).broadcast_to([T, G * NGRP, E0 // NGRP]),
                        ALU.add))
                    for j in range(G):
                        ins = nc.vector.max(etop[:, j, :], es[:, j, :])
                    link_apart(ins)
                    for j in range(G):
                        ins = nc.vector.max_index(eidx[:, j, :], etop[:, j, :], es[:, j, :])
                    link(ins)
                    nc.vector.tensor_tensor(gap[:], etop[:, :, 0:TOPK],
                                            etop[:, :, 0:1].broadcast_to([T, G, TOPK]), ALU.subtract).then_inc(v_gap, 1)
                    gated(0)
                    link(nc.vector.tensor_copy(eidf[:], eidx[:]))
                    link(nc.vector.tensor_tensor(
                        hot[:], prog.w("iota_e")[0:T].unsqueeze(1).unsqueeze(1).broadcast_to([T, G, TOPK, E0]),
                        eidf[:, :, 0:TOPK].unsqueeze(3).broadcast_to([T, G, TOPK, E0]), ALU.is_equal))
                    with nc.allow_low_precision("sums of a few ones are exact in bfloat16"):
                        nc.vector.tensor_reduce(any_hot[:], hot[:].rearrange("p g k e -> p g e k"), AX.X, ALU.add
                                                ).then_inc(v_hot, 1)
                    def rows():
                        ve.wait_ge(a_exp, n)
                        link(nc.vector.tensor_reduce(esum[:, 0, :], gates[:], AX.X, ALU.add))
                        link(nc.vector.reciprocal(esum[:, 1, :], esum[:, 0, :]))
                        link(nc.vector.tensor_tensor(gates[:], gates[:],
                                                     esum[:, 1, :].unsqueeze(2).broadcast_to([T, G, TOPK]), ALU.mult))
                        ve.wait_ge(pe_pos, n)
                        nc.vector.tensor_reduce(prior_add[:], any_hot[:].rearrange("p g e -> p e g"), AX.X, ALU.add)
                        link(nc.vector.tensor_tensor(
                            prod[:], hot[:],
                            bank[3][0:T, 0:G * E0].rearrange("p (g e) -> p g e", g=G).unsqueeze(2)
                            .broadcast_to([T, G, TOPK, E0]), ALU.mult))
                        nc.vector.tensor_tensor(prior[:], prior[:], prior_add[:], ALU.add)
                        link(nc.vector.tensor_reduce(pos[:], prod[:], AX.X, ALU.add))
                        nc.vector.tensor_scalar(keep[:], pos[:], float(CAP), None, ALU.is_lt)
                        link(nc.vector.tensor_scalar(pos[:], pos[:], float(CAP - 1), None, ALU.min))
                        link(nc.vector.scalar_tensor_tensor(rowf[:, 0], eidf[:, :, 0:TOPK], float(CAP), pos[:],
                                                            ALU.mult, ALU.add))
                        earlier(ve, scattered, n, 16 * G * TOPK)
                        nc.vector.tensor_tensor(prog.choice_gate[:, bass.ds((n - 1) * G, G), :], gates[:], keep[:], ALU.mult)
                        nc.vector.tensor_copy(prog.choice_row[:, bass.ds((n - 1) * G, G), :], rowf[:, 0])
                        nc.vector.tensor_copy(ids_now[:], ids[:, bass.ds((n - 1) * G, G)])
                        link(nc.vector.tensor_copy(spare[:], prog.w("spare_row")[0:T, bass.ds((n - 1) * (G * TOPK), G * TOPK)]))
                        flat = "p g k -> p (g k)"
                        link(nc.vector.tensor_tensor(rowf[:, 1], rowf[:, 0], spare[:].rearrange("p (g k) -> p g k", g=G),
                                                     ALU.subtract))
                        link(nc.vector.tensor_tensor(rowf[:, 1], rowf[:, 1], keep[:], ALU.mult))
                        nc.vector.tensor_tensor(row_put[:], rowf[:, 1].rearrange(flat), spare[:], ALU.add).then_inc(v_rows, 1)

                    def out():
                        ve.wait_ge(pe_down, n)
                        ve.wait_ge(res_in, n * 16)
                        earlier(ve, stored, n, 16)
                        for h in range(2):
                            ins = nc.vector.tensor_tensor(
                                xo[:, 2 * h:2 * h + 2, :], bank[4 + h][0:T, :].rearrange("p (g d) -> p g d", g=2),
                                xr[:, 2 * h:2 * h + 2, :], ALU.add)
                        ins.then_inc(v_out, 1)

                    gated(1)
                    if n_next is None:
                        rows()
                    gated(2)
                    gated(3)
                    if n_next is not None:
                        front(n_next)
                    out()
                    if n_next is not None:
                        turn(n_next)
                        rows()

                def begin(n):
                    front(n)
                    turn(n)

                run(ve, begin, step)

            @block.scalar
            def _(act):
                def step(n, n_next):
                    act.wait_ge(pe_xt, n)
                    nc.scalar.copy(xt[:, 0, :], bank[0][:, 0:GT]).then_inc(a_xt, 1)
                    for m in range(NM):
                        if m == 2:
                            act.wait_ge(v_gap, n)
                            nc.scalar.activation(gates[:], gap[:], ACT.Exp).then_inc(a_exp, 1)
                        act.wait_ge(pe_up[m], n)
                        nc.scalar.activation(act_[:, m, :], bank[LEFT[m % 2]][:, 0:GT], ACT.Silu).then_inc(a_up[m], 1)

                run(act, lambda n: None, step)

            @block.tensor
            def _(pe):
                def step(n, n_next):
                    pe.wait_ge(v_norm, n)
                    for c in range(KD):
                        for j in range(G):
                            ins = nc.tensor.transpose(bank[c][:, j * T:(j + 1) * T], xf[:, j, c * P:(c + 1) * P],
                                                      prog.w("ident")[0:T, 0:T])
                    ins.then_inc(pe_xt, 1)
                    pe.wait_ge(a_xt, n)
                    pe.wait_ge(v_xt, n)
                    for j in range(G):
                        for k in range(KD):
                            ins = nc.tensor.matmul(bank[2][0:T, j * NC_:(j + 1) * NC_], xt[:, k, j * T:(j + 1) * T],
                                                   prog.cent_t[:, k, :], start=(k == 0), stop=(k == KD - 1))
                    ins.then_inc(pe_logits, 1)
                    earlier(pe, v_out, n)
                    for m in range(NM):
                        if m >= 2:
                            pe.wait_ge(v_up[m - 2], n)
                        for side, name in enumerate(("f0_sg", "f0_su")):
                            for k in range(KD):
                                ins = nc.tensor.matmul(bank[LEFT[m % 2] + side][:, 0:GT],
                                                       prog.w(name, KD)[:, k, m * P:(m + 1) * P], xt[:, k, :],
                                                       start=(k == 0), stop=(k == KD - 1))
                        ins.then_inc(pe_up[m], 1)
                        if m == 1:
                            pe.wait_ge(v_hot, n)
                            for j in range(G):
                                out = bank[3][0:T, j * E0:(j + 1) * E0]
                                nc.tensor.matmul(out, prog.c("before")[0:T, :], any_hot[:, j, :], start=True, stop=False)
                                for before in range(j):
                                    nc.tensor.matmul(out, prog.c("ones_b")[0:T, :], any_hot[:, before, :],
                                                     start=False, stop=False)
                                ins = nc.tensor.matmul(out, prog.c("ones_b")[0:T, :], prior[:], start=False, stop=True)
                            ins.then_inc(pe_pos, 1)
                    pe.wait_ge(v_up[NM - 2], n)
                    for j in range(G):
                        for m in range(NM):
                            if j == 0 and m == NM - 1:
                                pe.wait_ge(v_up[NM - 1], n)
                            ins = nc.tensor.matmul(bank[4 + j // 2][0:T, (j % 2) * D:(j % 2 + 1) * D],
                                                   up[:, m, j * T:(j + 1) * T], prog.w("f0_sd", NM)[:, m, :],
                                                   start=(m == 0), stop=(m == NM - 1))
                    ins.then_inc(pe_down, 1)

                run(pe, lambda n: None, step)


def stage_experts0(prog):
    nc = prog.nc
    NM = HID // P
    HALF = CAP // 2
    ROUNDS = E0 // 2
    with stage(nc, "experts0") as (sem, sbuf, psum):
        def pair(label):
            return [sem(f"{label}{s}") for s in range(2)]

        ids_in, v_idf, pe_id, v_id = sem("ids_in"), sem("v_idf"), sem("pe_id"), sem("v_id")
        g_order = sem("g_order")
        w_in = [pair(f"w_in{k}_") for k in range(3)]
        v_now = pair("v_now")
        rows_in, pe_xt, v_xt = pair("rows_in"), pair("pe_xt"), pair("v_xt")
        pe_up = [pair(f"pe_up{m}_") for m in range(NM)]
        a_up = [pair(f"a_up{m}_") for m in range(NM)]
        v_up = [pair(f"v_up{m}_") for m in range(NM)]
        pe_down, a_out, stored = pair("pe_down"), pair("a_out"), pair("stored")

        ids = sbuf("ids", [2 * E0, HALF], I32)
        idf = sbuf("idf", [2 * E0, HALF])
        token = sbuf("token", [HALF, 2 * E0 + 4], I32)
        now = [sbuf(f"now{s}", [HALF, 2], I32) for s in range(2)]
        wg = [sbuf(f"wg{s}", [P, KD, HID]) for s in range(2)]
        wu = [sbuf(f"wu{s}", [P, KD, HID]) for s in range(2)]
        wd = [sbuf(f"wd{s}", [P, NM, D]) for s in range(2)]
        xe = [sbuf(f"xe{s}", [HALF, 2, D]) for s in range(2)]
        xt = [sbuf(f"xt{s}", [P, KD, CAP]) for s in range(2)]
        act_ = sbuf("act_", [P, 2, CAP])
        up = [sbuf(f"up{s}", [P, NM, CAP]) for s in range(2)]
        ye = [sbuf(f"ye{s}", [HALF, 2, D]) for s in range(2)]
        ps_xt = psum("ps_xt", [P, 512])
        ps_id = psum("ps_id", [P, 512])
        ps_up = [psum(f"ps_up{k}", [P, 2, 256]) for k in range(NM)]
        ps_out = psum("ps_out", [P, 2, D])

        def earlier(engine, semaphore, n, per=1):
            if not (isinstance(n, int) and n == 1):
                engine.wait_ge(semaphore, n * per - per)

        def run(engine, body):
            body(1, False)
            with engine.Fori(2, ROUNDS) as i:
                body(i, False)
            body(ROUNDS, True)

        with nc.Block() as block:
            @block.sync
            def _(sp):
                sp.dma_start(ids[:], prog.row_token[0:SLOTS0].rearrange("(c p) o -> c (p o)", p=HALF)
                             ).then_inc(ids_in, 16)

                def body(n, last):
                    for s in range(2):
                        e = n * 2 + (s - 2)
                        earlier(sp, pe_up[NM - 1][s], n)
                        for k, (dst, name) in enumerate(((wg, "wg"), (wu, "wu"))):
                            sp.dma_start(dst[s][:], prog.ins[name][bass.ds(e, 1)].rearrange("e p k h -> p (e k) h")
                                         ).then_inc(w_in[k][s], 16)
                        if s == 0 and isinstance(n, int) and n == 1:
                            sp.wait_ge(rows_in[0], 32)
                        earlier(sp, pe_down[s], n)
                        sp.dma_start(wd[s][:], prog.ins["wd"][bass.ds(e, 1)].rearrange("e p k h -> p (e k) h")
                                     ).then_inc(w_in[2][s], 16)

                run(sp, body)

            @block.gpsimd
            def _(g):
                with g.Fori(1, ROUNDS + 1) as i:
                    for s in range(2):
                        g.wait_ge(v_now[s], i)
                        g.sem_inc(g_order, 1)
                        for t in range(2):
                            g.indirect_dma_start(xe[s][:, t, :], None, prog.ln_rows,
                                                 bass.IndirectOffsetOnAxis(now[s][:, t:t + 1], 0)).then_inc(rows_in[s], 16)

            @block.tensor
            def _(pe):
                def turn(s, n):
                    pe.wait_ge(rows_in[s], n * 32)
                    if s == 1:
                        pe.wait_ge(v_xt[0], n)
                    else:
                        earlier(pe, v_xt[1], n)
                    for c in range(KD):
                        for t in range(2):
                            ins = nc.tensor.transpose(ps_xt[:, c * CAP + t * HALF:c * CAP + (t + 1) * HALF],
                                                      xe[s][:, t, c * P:(c + 1) * P], prog.w("ident")[0:HALF, 0:HALF])
                    ins.then_inc(pe_xt[s], 1)

                def half(s, n, last):
                    pe.wait_ge(v_xt[s], n)
                    for k in range(2):
                        pe.wait_ge(w_in[k][s], n * 16)
                    for m in range(NM):
                        if s == 1:
                            pe.wait_ge(v_up[m][0], n)
                        else:
                            earlier(pe, v_up[m][1], n)
                        for side, w in enumerate((wg, wu)):
                            for k in range(KD):
                                ins = nc.tensor.matmul(ps_up[m][:, side, 0:CAP], w[s][:, k, m * P:(m + 1) * P],
                                                       xt[s][:, k, :], start=(k == 0), stop=(k == KD - 1))
                        ins.then_inc(pe_up[m][s], 1)
                    if not last:
                        turn(1 - s, n + s)
                    pe.wait_ge(w_in[2][s], n * 16)
                    if s == 1:
                        pe.wait_ge(a_out[0], n)
                    else:
                        earlier(pe, a_out[1], n)
                    for t in range(2):
                        for m in range(NM):
                            if t == 0:
                                pe.wait_ge(v_up[m][s], n)
                            ins = nc.tensor.matmul(ps_out[0:HALF, t, :], up[s][:, m, t * HALF:(t + 1) * HALF],
                                                   wd[s][:, m, :], start=(m == 0), stop=(m == NM - 1))
                    ins.then_inc(pe_down[s], 1)

                pe.wait_ge(v_idf, 1)
                nc.tensor.transpose(ps_id[0:HALF, 0:2 * E0], idf[:], prog.w("ident")[0:2 * E0, 0:2 * E0]
                                    ).then_inc(pe_id, 1)
                turn(0, 1)

                def body(n, last):
                    half(0, n, False)
                    half(1, n, last)

                run(pe, body)

            @block.scalar
            def _(act):
                def body(n, last):
                    for s in range(2):
                        for m in range(NM):
                            if m >= 2:
                                act.wait_ge(v_up[m - 2][s], n)
                            elif s == 1:
                                act.wait_ge(v_up[m + 2][0], n)
                            else:
                                earlier(act, v_up[m + 2][1], n)
                            act.wait_ge(pe_up[m][s], n)
                            nc.scalar.activation(act_[:, m % 2, :], ps_up[m][:, 0, 0:CAP], ACT.Silu
                                                 ).then_inc(a_up[m][s], 1)
                        earlier(act, stored[s], n, 16)
                        act.wait_ge(pe_down[s], n)
                        nc.scalar.copy(ye[s][:], ps_out[0:HALF]).then_inc(a_out[s], 1)
                        act.wait_ge(a_out[s], n)
                        e = n * 2 + (s - 2)
                        act.dma_start(prog.expert_out[0].rearrange("(e t p) d -> e p t d", t=2, p=HALF)[bass.ds(e, 1)]
                                      .rearrange("e p t d -> p (e t) d"), ye[s][:]).then_inc(stored[s], 16)

                run(act, body)
                for s in range(2):
                    act.wait_ge(stored[s], ROUNDS * 16)

            @block.vector
            def _(ve):
                nc.vector.memset(token[:], 0)
                ve.wait_ge(ids_in, 16)
                nc.vector.tensor_copy(idf[:], ids[:]).then_inc(v_idf, 1)
                ve.wait_ge(v_idf, 1)
                ve.wait_ge(pe_id, 1)
                nc.vector.tensor_copy(token[:, 0:2 * E0], ps_id[0:HALF, 0:2 * E0]).then_inc(v_id, 1)
                ve.wait_ge(v_id, 1)
                for s in range(2):
                    nc.vector.tensor_copy(now[s][:], token[:, 2 * s:2 * s + 2]).then_inc(v_now[s], 1)

                def turn(s, n):
                    ve.wait_ge(pe_xt[s], n)
                    nc.vector.tensor_copy(xt[s][:], ps_xt[:, 0:KD * CAP].rearrange("p (k c) -> p k c", k=KD)
                                          ).then_inc(v_xt[s], 1)
                    nc.vector.tensor_copy(now[s][:], token[:, bass.ds(n * 4 + 2 * s, 2)]).then_inc(v_now[s], 1)

                def body(n, last):
                    for s in range(2):
                        for m in range(NM):
                            ve.wait_ge(a_up[m][s], n)
                            if m == 0:
                                earlier(ve, pe_down[s], n)
                            nc.vector.tensor_tensor(up[s][:, m, :], act_[:, m % 2, :], ps_up[m][:, 1, 0:CAP], ALU.mult
                                                    ).then_inc(v_up[m][s], 1)
                        if not (last and s == 1):
                            turn(1 - s, n + s)

                turn(0, 1)
                run(ve, body)



def stage_route1(prog):
    nc = prog.nc
    x_dram = prog.x[5]
    with stage(nc, "route1") as (sem, sbuf, psum):
        x_in, v_stat, g_rstd, v_norm = sem("x_in"), sem("v_stat"), sem("g_rstd"), sem("v_norm")
        v_link = [sem(f"v_link{k}") for k in range(7)]
        v_apart, v_count, v_front = sem("v_apart"), sem("v_count"), [sem(f"v_front{k}") for k in range(2)]
        pe_xt, a_xt, v_xt, pe_logits = sem("pe_xt"), sem("a_xt"), sem("v_xt"), sem("pe_logits")
        landed = sem("landed")
        a_keep, v_hot, v_bf = sem("a_keep"), sem("v_hot"), sem("v_bf")
        pe_count, zero_set, zeroed, scattered = sem("pe_count"), sem("zero_set"), sem("zeroed"), sem("scattered")

        xg = sbuf("xg", [T, B, D])
        stats = sbuf("stats", [T, G, 6])
        mv = sbuf("mv", [T, G, 2])
        var = sbuf("var", [T, G])
        rstd = sbuf("rstd", [T, G])
        xf = sbuf("xf", [T, G, D])
        kept = sbuf("kept", [T, B, D])
        xt = sbuf("xt", [P, KD, GT])
        logits = sbuf("logits", [T, G, E1])
        top = sbuf("top", [T, G, 8])
        arg = sbuf("arg", [T, G, 8], U32)
        argf = sbuf("argf", [T, G, 8])
        hot = sbuf("hot", [T, B, E1])
        hot_b = sbuf("hot_b", [T, B, E1], BF16)
        upto = sbuf("upto", [T, E1, B])
        start = sbuf("start", [T, E1, B])
        full = sbuf("full", [T, E1, MAX_E1_TILES])
        tiles = sbuf("tiles", [T, E1])
        ends = sbuf("ends", [T, E1])
        ones = sbuf("ones", [T, E1])
        first = sbuf("first", [T, E1])
        rank = sbuf("rank", [T, B, E1])
        rowf = sbuf("rowf", [T, B])
        past = sbuf("past", [T, TILES1, E1])
        tile_f = sbuf("tile_f", [T, TILES1])
        zeros = sbuf("zeros", [P, TILES1 * E1_ROWS // P * D])
        bank = [psum(f"bank{k}", [P, 512]) for k in range(4)]

        def earlier(engine, semaphore, n, per=1):
            if not (isinstance(n, int) and n == 1):
                engine.wait_ge(semaphore, n * per - per)

        def run(engine, front, step):
            front(1)
            step(1, 2)
            with engine.Fori(2, NG) as i:
                step(i, i + 1)
            step(NG, None)

        with nc.Block() as block:
            @block.sync
            def _(sp):
                with sp.Fori(1, NG + 1) as i:
                    sp.dma_start(xg[:, bass.ds((i - 1) * G, G), :],
                                 x_dram[bass.ds((i - 1) * G, G)].rearrange("g t d -> t g d")).then_inc(x_in, 16)
                    sp.wait_ge(x_in, i * 16)
                    sp.sem_inc(landed, 1)
                sp.wait_ge(zero_set, 1)
                sp.dma_start(prog.expert_in.rearrange("(p n) d -> p (n d)", p=P), zeros[:]).then_inc(zeroed, 16)

            @block.gpsimd
            def _(g):
                def root(n):
                    g.wait_ge(v_stat, n)
                    nc.gpsimd.tensor_tensor(rstd[:], var[:], prog.half_neg[0:T, :], ALU.pow).then_inc(g_rstd, 1)

                root(1)
                nc.gpsimd.memset(zeros[:], 0.0).then_inc(zero_set, 1)
                g.wait_ge(zero_set, 1)
                with g.Fori(2, NG + 1) as i:
                    root(i)
                g.wait_ge(zeroed, 16)
                g.wait_ge(a_keep, NG)
                g.wait_ge(v_count, prog.route1_rows)
                for b in range(B):
                    g.indirect_dma_start(prog.expert_in, bass.IndirectOffsetOnAxis(prog.row1[:, b:b + 1], 0),
                                         kept[:, b, :], None).then_inc(scattered, 16)
                g.wait_ge(scattered, B * 16)

            @block.scalar
            def _(act):
                def front(n):
                    act.wait_ge(v_norm, n)
                    nc.scalar.copy(kept[:, bass.ds((n - 1) * G, G), :], xf[:]).then_inc(a_keep, 1)

                def step(n, n_next):
                    act.wait_ge(pe_xt, n)
                    nc.scalar.copy(xt[:, 0, :], bank[0][:, 0:GT]).then_inc(a_xt, 1)
                    if n_next is not None:
                        front(n_next)

                run(act, front, step)

            @block.tensor
            def _(pe):
                with pe.Fori(1, NG + 1) as i:
                    pe.wait_ge(v_norm, i)
                    for c in range(KD):
                        for j in range(G):
                            ins = nc.tensor.transpose(bank[c][:, j * T:(j + 1) * T], xf[:, j, c * P:(c + 1) * P],
                                                      prog.w("ident")[0:T, 0:T])
                    ins.then_inc(pe_xt, 1)
                    pe.wait_ge(a_xt, i)
                    pe.wait_ge(v_xt, i)
                    for j in range(G):
                        for k in range(KD):
                            ins = nc.tensor.matmul(bank[2][0:T, j * E1:(j + 1) * E1], xt[:, k, j * T:(j + 1) * T],
                                                   prog.w("f1_gate_w", KD)[:, k, :], start=(k == 0), stop=(k == KD - 1))
                    ins.then_inc(pe_logits, 1)
                pe.wait_ge(v_bf, 1)
                for at, name in enumerate(("ones_b", "before")):
                    ins = nc.tensor.matmul(bank[3][0:T, at * B * E1:(at + 1) * B * E1], prog.c(name)[0:T, :],
                                           hot_b[:].rearrange("t b e -> t (b e)"), start=True, stop=True)
                ins.then_inc(pe_count, 1)

            @block.vector
            def _(ve):
                nc.vector.memset(ones[:], 1.0)

                def x_of(n, j):
                    return xg[:, bass.ds(n * G + (j - G), 1), :].rearrange("t b d -> t (b d)")

                def moments(n):
                    ve.wait_ge(x_in, n * 16)
                    ve.sem_inc(v_apart, 1)
                    for j in range(G):
                        ins = nc.vector.bn_stats(stats[:, j, :], x_of(n, j))
                    ins.then_inc(v_front[0], 1)
                    ve.wait_ge(v_front[0], n)
                    ve.sem_inc(v_apart, 1)
                    for j in range(G):
                        ins = nc.vector.bn_aggr(mv[:, j, :], stats[:, j, :])
                    ins.then_inc(v_front[1], 1)
                    ve.wait_ge(v_front[1], n)
                    nc.vector.tensor_scalar(var[:], mv[:, :, 1], EPS, None, ALU.add).then_inc(v_stat, 1)

                def normalise(n):
                    ve.wait_ge(g_rstd, n)
                    earlier(ve, a_keep, n)
                    for j in range(G):
                        ins = nc.vector.tensor_scalar(xf[:, j, :], x_of(n, j), mv[:, j, 0:1], rstd[:, j:j + 1],
                                                      ALU.subtract, ALU.mult)
                    ins.then_inc(v_norm, 1)

                def front(n):
                    moments(n)
                    normalise(n)

                def step(n, n_next):
                    used = [0]

                    def link(ins, apart=False):
                        ins.then_inc(v_link[used[0]], 1)
                        ve.wait_ge(v_link[used[0]], n)
                        used[0] += 1
                        if apart:
                            ve.sem_inc(v_apart, 1)

                    ve.wait_ge(pe_xt, n)
                    nc.vector.tensor_copy(xt[:, 1, :], bank[1][:, 0:GT]).then_inc(v_xt, 1)
                    if n_next is not None:
                        moments(n_next)
                    ve.wait_ge(pe_logits, n)
                    link(nc.vector.tensor_tensor(
                        logits[:], bank[2][0:T, 0:G * E1].rearrange("p (g e) -> p g e", g=G),
                        prog.w("f1_gate_b_row")[0:T].unsqueeze(1).broadcast_to([T, G, E1]), ALU.add))
                    link(nc.vector.tensor_tensor(
                        logits[:], logits[:], prog.w("f1_ebias_row")[0:T].unsqueeze(1).broadcast_to([T, G, E1]),
                        ALU.add), apart=True)
                    for j in range(G):
                        ins = nc.vector.max(top[:, j, :], logits[:, j, :])
                    if n_next is not None:
                        ins.then_inc(v_link[used[0]], 1)
                        normalise(n_next)
                        ve.wait_ge(v_link[used[0]], n)
                        used[0] += 1
                        ve.sem_inc(v_apart, 1)
                    else:
                        link(ins, apart=True)
                    for j in range(G):
                        ins = nc.vector.max_index(arg[:, j, :], top[:, j, :], logits[:, j, :])
                    link(ins)
                    link(nc.vector.tensor_copy(argf[:], arg[:]))
                    nc.vector.tensor_tensor(
                        hot[:, bass.ds((n - 1) * G, G), :],
                        prog.w("iota_e")[0:T, 0:E1].unsqueeze(1).broadcast_to([T, G, E1]),
                        argf[:, :, 0:1].broadcast_to([T, G, E1]), ALU.is_equal).then_inc(v_hot, 1)

                run(ve, front, step)
                ve.wait_ge(v_hot, NG)
                nc.vector.tensor_copy(hot_b[:], hot[:]).then_inc(v_bf, 1)
                n = [0]

                def step(ins):
                    n[0] += 1
                    ins.then_inc(v_count, 1)
                    ve.wait_ge(v_count, n[0])

                def by_expert(at):
                    return bank[3][0:T, at * B * E1:(at + 1) * B * E1].rearrange("t (b e) -> t e b", b=B)

                ve.wait_ge(pe_count, 1)
                step(nc.vector.tensor_copy(start[:], by_expert(0)))
                step(nc.vector.tensor_tensor_scan(upto[:].rearrange("t e b -> t (e b)"), prog.w("prefix_keep")[0:T],
                                                  start[:].rearrange("t e b -> t (e b)"), 0.0, ALU.mult, ALU.add))
                step(nc.vector.tensor_tensor(
                    full[:], upto[:, :, B - 1:B].broadcast_to([T, E1, MAX_E1_TILES]),
                    prog.w("tile_floor")[0:T].rearrange("t (e m) -> t e m", e=E1), ALU.is_gt))
                step(nc.vector.tensor_reduce(tiles[:], full[:], AX.X, ALU.add))
                step(nc.vector.tensor_tensor_scan(ends[:], ones[:], tiles[:], 0.0, ALU.mult, ALU.add))
                step(nc.vector.tensor_tensor(first[:], ends[:], tiles[:], ALU.subtract))
                step(nc.vector.tensor_scalar(first[:], first[:], float(E1_ROWS), None, ALU.mult))
                step(nc.vector.tensor_tensor(start[:], upto[:], start[:], ALU.subtract))
                step(nc.vector.tensor_tensor(start[:], start[:], first[:].unsqueeze(2).broadcast_to([T, E1, B]), ALU.add))
                step(nc.vector.tensor_tensor(rank[:].rearrange("t b e -> t e b"), by_expert(1), start[:], ALU.add))
                step(nc.vector.tensor_tensor(rank[:], rank[:], hot[:], ALU.mult))
                step(nc.vector.tensor_reduce(rowf[:], rank[:], AX.X, ALU.add))
                step(nc.vector.tensor_copy(prog.row1[:], rowf[:]))
                assert n[0] == prog.route1_rows
                step(nc.vector.tensor_tensor(
                    past[:], ends[:].unsqueeze(1).broadcast_to([T, TILES1, E1]),
                    prog.w("tile_no")[0:T].unsqueeze(2).broadcast_to([T, TILES1, E1]), ALU.is_le))
                step(nc.vector.tensor_reduce(tile_f[:], past[:], AX.X, ALU.add))
                step(nc.vector.tensor_scalar(tile_f[:], tile_f[:], float(E1 - 1), None, ALU.min))
                step(nc.vector.tensor_copy(prog.tile_expert[:], tile_f[0:1]))


def stage_experts1(prog):
    nc = prog.nc
    NM = FF // P
    HM = NM // 2
    ROUNDS = TILES1 // 2
    with stage(nc, "experts1") as (sem, sbuf, psum):
        def pair(label):
            return [sem(f"{label}{s}") for s in range(2)]

        w1_in, b1_in, w2_in, b2_in = pair("w1_in"), pair("b1_in"), pair("w2_in"), pair("b2_in")
        rows_in, pe_xt, v_xt = pair("rows_in"), pair("pe_xt"), pair("v_xt")
        pe_h = [pair(f"pe_h{q}_") for q in range(2)]
        a_h = [pair(f"a_h{q}_") for q in range(2)]
        pe_down, v_out, stored = pair("pe_down"), pair("v_out"), pair("stored")

        w1 = [sbuf(f"w1_{s}", [P, KD, FF]) for s in range(2)]
        b1 = [sbuf(f"b1_{s}", [P, NM]) for s in range(2)]
        w2 = [sbuf(f"w2_{s}", [P, NM, D]) for s in range(2)]
        b2 = [sbuf(f"b2_{s}", [P, D]) for s in range(2)]
        xe = [sbuf(f"xe{s}", [P, D]) for s in range(2)]
        xt = [sbuf(f"xt{s}", [P, KD, P]) for s in range(2)]
        h = [sbuf(f"h{s}", [P, NM, P]) for s in range(2)]
        ye = [sbuf(f"ye{s}", [P, D]) for s in range(2)]
        ps_xt = psum("ps_xt", [P, 512])
        ps_h = [[psum(f"ps_h{q}_{s}", [P, HM, P]) for s in range(2)] for q in range(2)]
        ps_out = [psum(f"ps_out{s}", [P, 512]) for s in range(2)]

        def earlier(engine, semaphore, n, per=1):
            if not (isinstance(n, int) and n == 1):
                engine.wait_ge(semaphore, n * per - per)

        def run(engine, body):
            body(1, False)
            with engine.Fori(2, ROUNDS) as i:
                body(i, False)
            body(ROUNDS, True)

        with nc.Block() as block:
            @block.sync
            def _(sp):
                def body(n, last):
                    for s in range(2):
                        tile = n * 2 + (s - 2)
                        e = sp.value_load(prog.tile_expert[0:1, bass.ds(tile, 1)], min_val=0, max_val=E1 - 1)
                        earlier(sp, pe_h[1][s], n)
                        sp.dma_start(w1[s][:], prog.ins["w1"][bass.ds(e, 1)].rearrange("e p k f -> p (e k) f")
                                     ).then_inc(w1_in[s], 16)
                        earlier(sp, a_h[1][s], n)
                        sp.dma_start(b1[s][:], prog.ins["b1"][bass.ds(e, 1)].rearrange("e p m -> p (e m)")
                                     ).then_inc(b1_in[s], 16)
                        earlier(sp, pe_down[s], n)
                        sp.dma_start(w2[s][:], prog.ins["w2"][bass.ds(e, 1)].rearrange("e p k d -> p (e k) d")
                                     ).then_inc(w2_in[s], 16)
                        earlier(sp, v_out[s], n)
                        sp.dma_start(b2[s][:], prog.ins["b2"][bass.ds(e, 1)].broadcast_to([P, D])
                                     ).then_inc(b2_in[s], 16)

                run(sp, body)

            @block.gpsimd
            def _(g):
                def body(n, last):
                    for s in range(2):
                        earlier(g, pe_xt[s], n)
                        g.dma_start(xe[s][:], prog.expert_in.rearrange("(c p) d -> c p d", p=P)
                                    [bass.ds(n * 2 + (s - 2), 1)].rearrange("c p d -> p (c d)")).then_inc(rows_in[s], 16)

                run(g, body)

            @block.tensor
            def _(pe):
                def turn(s, n):
                    pe.wait_ge(rows_in[s], n * 16)
                    if s == 1:
                        pe.wait_ge(v_xt[0], n)
                    else:
                        earlier(pe, v_xt[1], n)
                    for c in range(KD):
                        ins = nc.tensor.transpose(ps_xt[:, c * P:(c + 1) * P], xe[s][:, c * P:(c + 1) * P],
                                                  prog.w("ident"))
                    ins.then_inc(pe_xt[s], 1)

                def tile(s, n, last):
                    pe.wait_ge(v_xt[s], n)
                    pe.wait_ge(w1_in[s], n * 16)
                    for q in range(2):
                        earlier(pe, a_h[q][s], n)
                        for m in range(q * HM, (q + 1) * HM):
                            for k in range(KD):
                                ins = nc.tensor.matmul(ps_h[q][s][:, m % HM, :], w1[s][:, k, m * P:(m + 1) * P],
                                                       xt[s][:, k, :], start=(k == 0), stop=(k == KD - 1))
                        ins.then_inc(pe_h[q][s], 1)
                    if not last:
                        turn(1 - s, n + s)
                    pe.wait_ge(w2_in[s], n * 16)
                    earlier(pe, v_out[s], n)
                    for m in range(NM):
                        if m % HM == 0:
                            pe.wait_ge(a_h[m // HM][s], n)
                        ins = nc.tensor.matmul(ps_out[s][:, 0:D], h[s][:, m, :], w2[s][:, m, :],
                                               start=(m == 0), stop=(m == NM - 1))
                    ins.then_inc(pe_down[s], 1)

                turn(0, 1)

                def body(n, last):
                    tile(0, n, False)
                    tile(1, n, last)

                run(pe, body)

            @block.scalar
            def _(act):
                def body(n, last):
                    for s in range(2):
                        act.wait_ge(b1_in[s], n * 16)
                        earlier(act, pe_down[s], n)
                        for q in range(2):
                            act.wait_ge(pe_h[q][s], n)
                            for m in range(q * HM, (q + 1) * HM):
                                ins = nc.scalar.activation(h[s][:, m, :], ps_h[q][s][:, m % HM, :], ACT.Relu,
                                                           bias=b1[s][:, m:m + 1])
                            ins.then_inc(a_h[q][s], 1)
                        if s == 1:
                            store(0, n)
                        elif not (isinstance(n, int) and n == 1):
                            store(1, n - 1)

                def store(s, n):
                    act.wait_ge(v_out[s], n)
                    act.dma_start(prog.expert_out[1].rearrange("(c p) d -> c p d", p=P)[bass.ds(n * 2 + (s - 2), 1)]
                                  .rearrange("c p d -> p (c d)"), ye[s][:]).then_inc(stored[s], 16)

                run(act, body)
                store(1, ROUNDS)
                for s in range(2):
                    act.wait_ge(stored[s], ROUNDS * 16)

            @block.vector
            def _(ve):
                def turn(s, n):
                    ve.wait_ge(pe_xt[s], n)
                    nc.vector.tensor_copy(xt[s][:], ps_xt[:, 0:KD * P].rearrange("p (k c) -> p k c", k=KD)
                                          ).then_inc(v_xt[s], 1)

                def body(n, last):
                    for s in range(2):
                        if not (last and s == 1):
                            turn(1 - s, n + s)
                        ve.wait_ge(pe_down[s], n)
                        ve.wait_ge(b2_in[s], n * 16)
                        earlier(ve, stored[s], n, 16)
                        nc.vector.tensor_tensor(ye[s][:], ps_out[s][:, 0:D], b2[s][:], ALU.add).then_inc(v_out[s], 1)

                turn(0, 1)
                run(ve, body)


def stage_combine1(prog):
    nc = prog.nc
    with stage(nc, "combine1") as (sem, sbuf, psum):
        x_in, got_in = ([sem(f"{n}{k}") for k in range(NG)] for n in ("x_in", "got_in"))
        v_out, stored = sem("v_out"), sem("stored")
        got = sbuf("got", [T, B, D])
        acc = sbuf("acc", [T, B, D])

        with nc.Block() as block:
            @block.sync
            def _(sp):
                for k in range(NG):
                    here = slice(k * G, (k + 1) * G)
                    sp.dma_start(acc[:, here], prog.x[5][here].rearrange("g t d -> t g d")).then_inc(x_in[k], 16)
                for k in range(NG):
                    here = slice(k * G, (k + 1) * G)
                    sp.wait_ge(v_out, k + 1)
                    sp.dma_start(prog.out[here].rearrange("g t d -> t g d"), acc[:, here]).then_inc(stored, 16)
                sp.wait_ge(stored, NG * 16)

            @block.gpsimd
            def _(g):
                for b in range(B):
                    g.indirect_dma_start(got[:, b, :], None, prog.expert_out[1],
                                         bass.IndirectOffsetOnAxis(prog.row1[:, b:b + 1], 0)).then_inc(got_in[b // G], 16)

            @block.vector
            def _(ve):
                for k in range(NG):
                    here = slice(k * G, (k + 1) * G)
                    ve.wait_ge(x_in[k], 16)
                    ve.wait_ge(got_in[k], 16 * G)
                    nc.vector.tensor_tensor(acc[:, here], got[:, here], acc[:, here], ALU.add).then_inc(v_out, 1)


def build(nc, ins, out):
    prog = Program(nc, ins, out)
    stage_setup(prog)
    stage_mixer(prog)
    stage_queries(prog, 0, combine=False)
    stage_attention(prog, 0)
    stage_route0(prog)
    stage_experts0(prog)
    stage_queries(prog, 1, combine=True)
    stage_attention(prog, 1)
    stage_queries(prog, 2, combine=False)
    stage_attention(prog, 2)
    stage_route1(prog)
    stage_experts1(prog)
    stage_combine1(prog)


def kernel(**inputs):
    import concourse.bacc as bacc
    from concourse.bass_utils import run_bass_kernel_spmd

    arrays = {f"in_{name}": np.ascontiguousarray(a)
              for name, a in host_layout({k: np.asarray(v) for k, v in inputs.items()}).items()}
    nc = bacc.Bacc("TRN2", target_bir_lowering=False, num_devices=1)
    ins = {name[3:]: nc.dram_tensor(name, a.shape, mybir.dt.from_np(a.dtype), kind="ExternalInput").ap()
           for name, a in arrays.items()}
    out = nc.dram_tensor("out", [B, T, D], F32, kind="ExternalOutput").ap()
    build(nc, ins, out)
    r = run_bass_kernel_spmd(nc, [arrays], core_ids=[0])
    return r.results[0]["out"]
```
